# Optimizing a Trainium2 kernel written in Bass

```python
import numpy as np
import jax
import jax.numpy as jnp

def _softmax(x, axis=-1):
    return jax.nn.softmax(x, axis=axis)

def _gelu(x):
    return jax.nn.gelu(x, approximate=True)

def _silu(x):
    return jax.nn.silu(x)

def _sigmoid(x):
    return jax.nn.sigmoid(x)

def _layernorm(x, axis=-1, eps=1e-05):
    m = jnp.mean(x, axis=axis, keepdims=True)
    v = jnp.var(x, axis=axis, keepdims=True)
    return (x - m) / jnp.sqrt(v + eps)

def _scatter_add(tgt, idx, src, axis=0):
    return tgt.at[idx].add(src)

def _segment_sum(src, seg, n):
    return jax.ops.segment_sum(src, seg, n)
kernel_name = 'mk_recurrent_d2_jaxref_r4_2d5036'

def setup_inputs(seed: int=0):
    np.random.seed(seed)
    _w = jnp.asarray

    def _L0_attn_setup():
        import jax, jax.numpy as jnp
        import numpy as np
        EPS = 1e-06
        key = jax.random.key(seed)
        kx, kw = jax.random.split(key)
        B, L, D = (4, 2048, 256)
        x = jax.random.normal(kx, (B, L, D), dtype=jnp.float32)
        W = jax.random.normal(kw, (D, 3 * D), dtype=jnp.float32) * 0.02
        return {'x': x, 'W': W}
    _L0_attn_in = _L0_attn_setup()

    def _L0_ffn_setup():
        import jax, jax.numpy as jnp
        import numpy as np
        B, S, H, E, D = (4, 1024, 256, 8, 64)
        key = jax.random.key(seed)
        k0, k1, k2, k3, k4 = jax.random.split(key, 5)
        scale_h = 1.0 / np.sqrt(H)
        scale_d = 1.0 / np.sqrt(D)
        return {'x': jax.random.normal(k0, (B, S, H), dtype=jnp.float32), 'gate_w': jax.random.normal(k1, (E, H), dtype=jnp.float32) * scale_h, 'wg': jax.random.normal(k2, (E, H, D), dtype=jnp.float32) * scale_h, 'wu': jax.random.normal(k3, (E, H, D), dtype=jnp.float32) * scale_h, 'wd': jax.random.normal(k4, (E, D, H), dtype=jnp.float32) * scale_d}
    _L0_ffn_in = _L0_ffn_setup()

    def _L1_attn_setup():
        import jax, jax.numpy as jnp
        import numpy as np
        B, S, E, H, BS = (4, 1024, 256, 256, 128)
        key = jax.random.key(seed)
        k1, k2, k3, k4 = jax.random.split(key, 4)
        x = jax.random.normal(k1, (B, S, E), dtype=jnp.float32)
        W_qkv = jax.random.normal(k2, (E, 3 * H), dtype=jnp.float32) * E ** (-0.5)
        W_out = jax.random.normal(k3, (H, H), dtype=jnp.float32) * H ** (-0.5)
        b_out = jax.random.normal(k4, (H,), dtype=jnp.float32) * 0.01
        return {'x': x, 'W_qkv': W_qkv, 'W_out': W_out, 'b_out': b_out}
    _L1_attn_in = _L1_attn_setup()

    def _L1_ffn_setup():
        import jax, jax.numpy as jnp
        import numpy as np
        S, B, D, H, DH = (1024, 8, 256, 16, 64)

        def _forward(x, Wg, Wq, bq, Wkv, bkv, Wo, bo, ln_g, ln_b):
            s_len, bsz, d_model = x.shape
            n_head, _, d_head = Wq.shape
            cap = s_len // n_head
            scale = 1.0 / d_head ** 0.5
            h = jnp.transpose(x, (1, 0, 2))
            t = h
            probs = jax.nn.softmax(h @ Wg, axis=-1)
            scores = jnp.transpose(probs, (0, 2, 1))
            _, idx = jax.lax.top_k(scores, cap)
            idx = jnp.sort(idx, axis=-1)
            hg = jnp.take_along_axis(h[:, None, :, :], idx[..., None], axis=2)
            hg = jnp.transpose(hg, (1, 0, 2, 3))
            q = jnp.einsum('hbcd,hde->hbce', hg, Wq) + bq[:, None, None, :]
            kv = jnp.einsum('hbcd,hde->hbce', hg, Wkv) + bkv[:, None, None, :]
            k, v = jnp.split(kv, 2, axis=-1)
            att = jnp.einsum('hbid,hbjd->hbij', q, k) * scale
            p = jax.nn.softmax(att, axis=1)
            av = jnp.einsum('hbij,hbjd->hbid', p, v)
            ao = jnp.einsum('hbid,hde->hbie', av, Wo) + bo
            tok = jnp.transpose(idx, (1, 0, 2))
            b_ids = jnp.arange(bsz)[None, :, None]
            outs = jnp.zeros_like(t).at[b_ids, tok].add(ao)
            y = t + outs
            mu = jnp.mean(y, axis=-1, keepdims=True)
            var = jnp.var(y, axis=-1, keepdims=True)
            yn = (y - mu) * jax.lax.rsqrt(var + 1e-05) * ln_g + ln_b
            return jnp.transpose(yn, (1, 0, 2))
        key = jax.random.key(seed)
        ks = jax.random.split(key, 6)
        s = 0.02
        return {'x': jax.random.normal(ks[0], (S, B, D), jnp.float32), 'attn_mask': jnp.zeros((S, S), jnp.bool_), 'Wg': jax.random.normal(ks[1], (D, H), jnp.float32) * s, 'Wq': jax.random.normal(ks[2], (H, D, DH), jnp.float32) * s, 'bq': jnp.zeros((H, DH), jnp.float32), 'Wkv': jax.random.normal(ks[3], (H, D, 2 * DH), jnp.float32) * s, 'bkv': jnp.zeros((H, 2 * DH), jnp.float32), 'Wo': jax.random.normal(ks[4], (H, DH, D), jnp.float32) * s, 'bo': jnp.zeros((D,), jnp.float32), 'ln_g': jnp.ones((D,), jnp.float32), 'ln_b': jnp.zeros((D,), jnp.float32)}
    _L1_ffn_in = _L1_ffn_setup()
    _d = {'L0_attn_x': _L0_attn_in['x'], 'L0_attn_W': _L0_attn_in['W'], 'L0_ffn_gate_w': _L0_ffn_in['gate_w'], 'L0_ffn_wg': _L0_ffn_in['wg'], 'L0_ffn_wu': _L0_ffn_in['wu'], 'L0_ffn_wd': _L0_ffn_in['wd'], 'L1_attn_W_qkv': _L1_attn_in['W_qkv'], 'L1_attn_W_out': _L1_attn_in['W_out'], 'L1_attn_b_out': _L1_attn_in['b_out'], 'L1_ffn_attn_mask': _L1_ffn_in['attn_mask'], 'L1_ffn_Wg': _L1_ffn_in['Wg'], 'L1_ffn_Wq': _L1_ffn_in['Wq'], 'L1_ffn_bq': _L1_ffn_in['bq'], 'L1_ffn_Wkv': _L1_ffn_in['Wkv'], 'L1_ffn_bkv': _L1_ffn_in['bkv'], 'L1_ffn_Wo': _L1_ffn_in['Wo'], 'L1_ffn_bo': _L1_ffn_in['bo'], 'L1_ffn_ln_g': _L1_ffn_in['ln_g'], 'L1_ffn_ln_b': _L1_ffn_in['ln_b']}
    _x0 = _d['L0_attn_x']
    _d['L0_attn_x'] = jax.random.normal(jax.random.fold_in(jax.random.key(seed), 1), (8, 1024, 256), dtype=_x0.dtype)
    del _x0
    return _d

def reference(L0_attn_x, L0_attn_W, L0_ffn_gate_w, L0_ffn_wg, L0_ffn_wu, L0_ffn_wd, L1_attn_W_qkv, L1_attn_W_out, L1_attn_b_out, L1_ffn_attn_mask, L1_ffn_Wg, L1_ffn_Wq, L1_ffn_bq, L1_ffn_Wkv, L1_ffn_bkv, L1_ffn_Wo, L1_ffn_bo, L1_ffn_ln_g, L1_ffn_ln_b):

    def _L0_attn_ref(x, W):
        import jax, jax.numpy as jnp
        import numpy as np
        EPS = 1e-06
        D = x.shape[-1]
        qkv = x @ W
        q, k, v = jnp.split(qkv, 3, axis=-1)
        q = jax.nn.elu(q) + 1.0
        k = jax.nn.elu(k) + 1.0
        KV = jnp.einsum('bld,blh->bhd', k, v)
        k_sum = k.sum(axis=1)
        Z = 1.0 / (jnp.einsum('bld,bd->bl', q, k_sum) + EPS)
        V = jnp.einsum('bld,bhd,bl->blh', q, KV, Z)
        return V

    def _L0_ffn_ref(x, gate_w, wg, wu, wd):
        import jax, jax.numpy as jnp
        import numpy as np
        B, S, H, E, D = (4, 1024, 256, 8, 64)
        b, s, h = x.shape
        xf = x.reshape(-1, h)
        logits = jnp.einsum('th,eh->te', xf, gate_w)
        expert_idx = jnp.argmax(logits, axis=-1)
        onehot = jax.nn.one_hot(expert_idx, gate_w.shape[0], dtype=x.dtype)
        g = jnp.einsum('th,ehd->etd', xf, wg)
        u = jnp.einsum('th,ehd->etd', xf, wu)
        inter = jnp.square(jax.nn.relu(g)) * u
        inter = inter * onehot.T[:, :, None]
        out = jnp.einsum('etd,edh->th', inter, wd)
        return out.reshape(b, s, h)

    def _L1_attn_ref(x, W_qkv, W_out, b_out):
        import jax, jax.numpy as jnp
        import numpy as np
        B, S, E, H, BS = (4, 1024, 256, 256, 128)
        b, s, e = x.shape
        h = W_out.shape[1]
        nb = s // BS
        qkv = x @ W_qkv
        q, k, v = jnp.split(qkv, 3, axis=-1)

        def blk(t):
            return t.reshape(b, nb, BS, h)
        scale = h ** (-0.5)
        scores = jnp.einsum('bnqd,bnkd->bnqk', blk(q), blk(k)) * scale
        causal = jnp.tril(jnp.ones((BS, BS), dtype=bool))
        scores = jnp.where(causal, scores, -jnp.inf)
        scores = scores - jnp.max(scores, axis=-1, keepdims=True)
        p = jnp.exp(scores)
        p = p / (jnp.sum(p, axis=-1, keepdims=True) + 1e-06)
        out = jnp.einsum('bnqk,bnkd->bnqd', p, blk(v)).reshape(b, s, h)
        return out @ W_out.T + b_out

    def _L1_ffn_ref(x, attn_mask, Wg, Wq, bq, Wkv, bkv, Wo, bo, ln_g, ln_b):
        import jax, jax.numpy as jnp
        import numpy as np
        S, B, D, H, DH = (1024, 8, 256, 16, 64)

        def _forward(x, Wg, Wq, bq, Wkv, bkv, Wo, bo, ln_g, ln_b):
            s_len, bsz, d_model = x.shape
            n_head, _, d_head = Wq.shape
            cap = s_len // n_head
            scale = 1.0 / d_head ** 0.5
            h = jnp.transpose(x, (1, 0, 2))
            t = h
            probs = jax.nn.softmax(h @ Wg, axis=-1)
            scores = jnp.transpose(probs, (0, 2, 1))
            _, idx = jax.lax.top_k(scores, cap)
            idx = jnp.sort(idx, axis=-1)
            hg = jnp.take_along_axis(h[:, None, :, :], idx[..., None], axis=2)
            hg = jnp.transpose(hg, (1, 0, 2, 3))
            q = jnp.einsum('hbcd,hde->hbce', hg, Wq) + bq[:, None, None, :]
            kv = jnp.einsum('hbcd,hde->hbce', hg, Wkv) + bkv[:, None, None, :]
            k, v = jnp.split(kv, 2, axis=-1)
            att = jnp.einsum('hbid,hbjd->hbij', q, k) * scale
            p = jax.nn.softmax(att, axis=1)
            av = jnp.einsum('hbij,hbjd->hbid', p, v)
            ao = jnp.einsum('hbid,hde->hbie', av, Wo) + bo
            tok = jnp.transpose(idx, (1, 0, 2))
            b_ids = jnp.arange(bsz)[None, :, None]
            outs = jnp.zeros_like(t).at[b_ids, tok].add(ao)
            y = t + outs
            mu = jnp.mean(y, axis=-1, keepdims=True)
            var = jnp.var(y, axis=-1, keepdims=True)
            yn = (y - mu) * jax.lax.rsqrt(var + 1e-05) * ln_g + ln_b
            return jnp.transpose(yn, (1, 0, 2))
        return _forward(x, Wg, Wq, bq, Wkv, bkv, Wo, bo, ln_g, ln_b)
    x = L0_attn_x
    xn = _layernorm(x, axis=-1)
    s = _L0_attn_ref(xn, L0_attn_W)
    g = _silu(_L0_ffn_ref(xn, L0_ffn_gate_w, L0_ffn_wg, L0_ffn_wu, L0_ffn_wd))
    x = x + s * g
    xn = _layernorm(x, axis=-1)
    s = _L1_attn_ref(xn, L1_attn_W_qkv, L1_attn_W_out, L1_attn_b_out)
    g = _silu(_L1_ffn_ref(xn, L1_ffn_attn_mask, L1_ffn_Wg, L1_ffn_Wq, L1_ffn_bq, L1_ffn_Wkv, L1_ffn_bkv, L1_ffn_Wo, L1_ffn_bo, L1_ffn_ln_g, L1_ffn_ln_b))
    x = x + s * g
    return x

_drawn_inputs = setup_inputs


def setup_inputs(seed=0):
    import zlib

    import numpy as np

    out = dict(_drawn_inputs(seed))
    spreads = {'L1_ffn_bq': (0.0, 0.1),
     'L1_ffn_bkv': (0.0, 0.1),
     'L1_ffn_bo': (0.0, 0.1),
     'L1_ffn_ln_g': (1.0, 0.6),
     'L1_ffn_ln_b': (0.0, 2.0)}
    factors = {'L0_attn_W': 7.146,
     'L0_ffn_gate_w': 8.0,
     'L0_ffn_wg': 8.0,
     'L0_ffn_wu': 8.0,
     'L0_ffn_wd': 8.0,
     'L1_attn_b_out': 64.0,
     'L1_attn_W_qkv': 8.0,
     'L1_attn_W_out': 8.0}
    for name, (base, spread) in spreads.items():
        noise = np.random.default_rng([zlib.crc32(name.encode()), seed]).standard_normal(out[name].shape)
        drawn = base * np.exp(spread * noise) if base else spread * noise
        out[name] = jnp.asarray(drawn.astype(out[name].dtype))
    for name, factor in factors.items():
        out[name] = (out[name] * factor).astype(out[name].dtype)
    return out
```

```python
from contextlib import ExitStack

import concourse.bass as bass
from concourse import mybir

F32 = mybir.dt.float32
F32R = mybir.dt.float32r
BF16 = mybir.dt.bfloat16
I32 = mybir.dt.int32
U32 = mybir.dt.uint32
ALU = mybir.AluOpType
ACT = mybir.ActivationFunctionType
AX_X = mybir.AxisListType.X

P = 128
CT = 4
CHUNK = CT * P
CPB = 2
LN_EPS = 1e-5
Z_EPS = 1e-6
MASKED = -3.0e38


class Names:
    pass


def program(nc, x, W, gate_w, wg, wu, wd, W_qkv, W_out, b_out, ln_g, ln_b, out):
    z = Names()
    z.B, z.L, z.D = x.shape
    z.E, _, z.DE = wg.shape
    z.KD = z.D // P
    z.NK = z.D + z.E
    z.NV = z.D + 2
    z.TILES = z.B * z.L // P
    z.REGION = z.B * z.L + P
    z.SLOTS = z.TILES + z.E
    assert z.L == CPB * CHUNK and z.D == z.KD * P and z.SLOTS % 2 == 0 and z.KD == 2
    z.x_rows = x.rearrange("b (h t p) d -> (b h) p t d", p=P, t=CT)
    z.x, z.out = x, out
    z.sorted_dram = nc.dram_tensor("sorted_rows", (z.E * z.REGION, z.D), F32)
    z.expert_dram = nc.dram_tensor("expert_rows", (z.SLOTS * P, z.D), F32)

    with ExitStack() as whole:
        def sb(name, shape, dt=F32):
            return whole.enter_context(nc.sbuf_tensor(name, shape, dt))

        z.wq = sb("wq", [P, 2, z.KD, z.D], F32R)
        z.wkg = sb("wkg", [P, 2, z.KD, z.NK], F32R)
        z.wv = sb("wv", [P, 2, z.KD, z.NV], F32R)
        z.wqk = sb("wqk", [P, z.KD, z.D])
        z.wvo = sb("wvo", [P, z.KD, z.D])
        z.ident = sb("ident", [P, P])
        z.ones_r = sb("ones_r", [P, P], F32R)
        z.sum_col = sb("sum_col", [P, z.NV], F32R)
        z.ones_b = sb("ones_b", [P, P], BF16)
        z.before = sb("before", [P, P], BF16)
        z.ident_b = sb("ident_b", [P, P], BF16)
        z.causal = sb("causal", [P, P], BF16)
        z.first_rank = sb("first_rank", [P, CT, z.E])
        z.region0 = sb("region0", [P, z.E])
        z.row_id = sb("row_id", [P, 1])
        z.slot_id = sb("slot_id", [P, z.SLOTS])
        z.neg_half = sb("neg_half", [P, CPB * CT])
        z.eps = sb("eps", [P, CPB * CT])
        z.bout = sb("bout", [P, z.D])
        z.lng_half = sb("lng_half", [P, z.D])
        z.lnb_half = sb("lnb_half", [P, z.D])
        z.res = sb("res", [P, z.TILES, z.D])
        z.chosen = sb("chosen", [P, z.TILES, z.E], BF16)
        z.place = sb("place", [P, z.TILES + CPB * CT])
        z.next_row = sb("next_row", [P, z.E])
        prologue(nc, z, W, gate_w, W_qkv, W_out, b_out, ln_g, ln_b)
        first_layer(nc, z)
        experts(nc, z, wg, wu, wd)
        second_layer(nc, z)


def scope(nc, ctx):
    def sb(name, shape, dt=F32):
        return ctx.enter_context(nc.sbuf_tensor(name, shape, dt))

    def ps(name, shape):
        return ctx.enter_context(nc.psum_tensor(name, shape, F32))

    def sems(names):
        return {n: ctx.enter_context(nc.semaphore(n)) for n in names.split()}

    return sb, ps, sems


def prologue(nc, z, W, gate_w, W_qkv, W_out, b_out, ln_g, ln_b):
    KD, D, E, DE, NK, NV = z.KD, z.D, z.E, z.DE, z.NK, z.NV
    with ExitStack() as ctx:
        sb, ps, sems = scope(nc, ctx)
        w_s = sb("w_s", [P, KD, 3 * D])
        gate_s = sb("gate_s", [E, D])
        kg_s = sb("kg_s", [P, KD, NK])
        v_s = sb("v_s", [P, KD, NV])
        w2_s = sb("w2_s", [P, KD, 3 * D])
        wo_s = sb("wo_s", [P, KD, D])
        turned = sb("turned", [P, 4, KD, D])
        ones_s = sb("ones_s", [P, P])
        col_s = sb("col_s", [P, NV])
        tri_s = sb("tri_s", [P, P])
        causal_s = sb("causal_s", [P, P])
        ids = sb("ids", [P, z.SLOTS], I32)
        pid = sb("pid", [P, 1], I32)
        lng_s = sb("lng_s", [P, D])
        lnb_s = sb("lnb_s", [P, D])
        turn_ps = ps("turn_ps", [P, 4, KD, D])
        fold_ps = ps("fold_ps", [P, 2, KD, D])
        gate_ps = ps("gate_ps", [P, KD, 64])
        g = sems("w_loaded gate_loaded w2_loaded wo_loaded rows_loaded blank consts gate_turned staged "
                 "rounded split turned_ready turned_copied folded_ready folded_copied placed")
        block = ctx.enter_context(nc.Block())

        @block.sync
        def _(sp):
            sp.dma_start(w_s[:], W.rearrange("(k p) n -> p k n", p=P)).then_inc(g["w_loaded"], 16)
            sp.dma_start(gate_s[:], gate_w).then_inc(g["gate_loaded"], 16)
            sp.dma_start(w2_s[:], W_qkv.rearrange("(k p) n -> p k n", p=P)).then_inc(g["w2_loaded"], 16)
            sp.dma_start(wo_s[:], W_out.rearrange("(k p) n -> p k n", p=P)).then_inc(g["wo_loaded"], 16)
            for dst, src in ((z.bout, b_out), (lng_s, ln_g), (lnb_s, ln_b)):
                sp.dma_start(dst[:], src.partition_broadcast(P)).then_inc(g["rows_loaded"], 16)
            sp.wait_ge(g["rows_loaded"], 48)

        @block.gpsimd
        def _(pool):
            nc.gpsimd.memset(z.ident[:], 0.0).then_inc(g["blank"], 1)
            nc.gpsimd.memset(tri_s[:], 1.0).then_inc(g["blank"], 1)
            nc.gpsimd.memset(causal_s[:], 0.0).then_inc(g["blank"], 1)
            nc.gpsimd.memset(col_s[:], 0.0).then_inc(g["blank"], 1)
            pool.wait_ge(g["blank"], 4)
            nc.gpsimd.affine_select(out=z.ident[:], in_=z.ident[:], compare_op=ALU.not_equal, fill=1.0, base=0,
                                    pattern=[[-1, P]], channel_multiplier=1).then_inc(g["consts"], 1)
            nc.gpsimd.affine_select(out=tri_s[:], in_=tri_s[:], compare_op=ALU.is_gt, fill=0.0, base=0,
                                    pattern=[[1, P]], channel_multiplier=-1).then_inc(g["consts"], 1)
            nc.gpsimd.affine_select(out=causal_s[:], in_=causal_s[:], compare_op=ALU.is_ge, fill=MASKED, base=0,
                                    pattern=[[-1, P]], channel_multiplier=1).then_inc(g["consts"], 1)
            nc.gpsimd.memset(col_s[0:1, D:D + 1], 1.0).then_inc(g["consts"], 1)
            nc.gpsimd.memset(ones_s[:], 1.0).then_inc(g["consts"], 1)
            nc.gpsimd.iota(ids[:], pattern=[[1, z.SLOTS]], base=0, channel_multiplier=0).then_inc(g["consts"], 1)
            nc.gpsimd.iota(pid[:], pattern=[[0, 1]], base=0, channel_multiplier=1).then_inc(g["consts"], 1)
            nc.gpsimd.memset(z.neg_half[:], -0.5).then_inc(g["placed"], 1)
            nc.gpsimd.memset(z.eps[:], LN_EPS).then_inc(g["placed"], 1)
            for e in range(E):
                nc.gpsimd.memset(z.first_rank[:, :, e:e + 1], float(E - e)).then_inc(g["placed"], 1)
                nc.gpsimd.memset(z.region0[:, e:e + 1], float(e * z.REGION)).then_inc(g["placed"], 1)
                nc.gpsimd.memset(z.next_row[:, e:e + 1], float(e * z.REGION)).then_inc(g["placed"], 1)
            nc.gpsimd.memset(z.place[:, z.TILES:], 0.0).then_inc(g["placed"], 1)
            pool.wait_ge(g["placed"], 3 + 3 * E)

        @block.tensor
        def _(pe):
            pe.wait_ge(g["consts"], 7)
            pe.wait_ge(g["gate_loaded"], 16)
            for k in range(KD):
                t = nc.tensor.transpose(gate_ps[:, k, 0:E], gate_s[:, k * P:(k + 1) * P], z.ident[0:E, 0:E])
            t.then_inc(g["gate_turned"], 1)
            pe.wait_ge(g["w2_loaded"], 16)
            pe.wait_ge(g["wo_loaded"], 16)
            for m, src in enumerate((w2_s[:, :, 0:D], w2_s[:, :, D:2 * D], w2_s[:, :, 2 * D:3 * D], wo_s[:, :, :])):
                for k in range(KD):
                    for j in range(KD):
                        t = nc.tensor.transpose(turn_ps[:, m, k, j * P:(j + 1) * P], src[:, j, k * P:(k + 1) * P], z.ident[:])
                t.then_inc(g["turned_ready"], 1)
            pe.wait_ge(g["turned_copied"], 4)
            for m, (a, b) in enumerate(((0, 1), (2, 3))):
                for j in range(KD):
                    for k in range(KD):
                        t = nc.tensor.matmul(fold_ps[:, m, j, :], turned[:, a, k, j * P:(j + 1) * P], turned[:, b, k, :],
                                             start=(k == 0), stop=(k == KD - 1))
                t.then_inc(g["folded_ready"], 1)

        @block.scalar
        def _(act):
            for m in range(4):
                act.wait_ge(g["turned_ready"], m + 1)
                nc.scalar.activation(turned[:, m], turn_ps[:, m], ACT.Copy).then_inc(g["turned_copied"], 1)
            for m, dst in enumerate((z.wqk, z.wvo)):
                act.wait_ge(g["folded_ready"], m + 1)
                nc.scalar.activation(dst[:], fold_ps[:, m], ACT.Copy).then_inc(g["folded_copied"], 1)
            act.wait_ge(g["folded_copied"], 2)

        @block.vector
        def _(dve):
            dve.wait_ge(g["w_loaded"], 16)
            nc.vector.tensor_copy(kg_s[:, :, 0:D], w_s[:, :, D:2 * D]).then_inc(g["staged"], 1)
            nc.vector.tensor_copy(v_s[:, :, 0:D], w_s[:, :, 2 * D:3 * D]).then_inc(g["staged"], 1)
            nc.vector.memset(v_s[:, :, D:NV], 0.0).then_inc(g["staged"], 1)
            dve.wait_ge(g["gate_turned"], 1)
            nc.vector.tensor_copy(kg_s[:, :, D:NK], gate_ps[:, :, 0:E]).then_inc(g["staged"], 1)
            dve.wait_ge(g["staged"], 4)
            pairs = ((z.wq, w_s[:, :, 0:D]), (z.wkg, kg_s[:]), (z.wv, v_s[:]))
            for dst, src in pairs:
                nc.vector.tensor_copy(dst[:, 0], src).then_inc(g["rounded"], 1)
            for i, (dst, src) in enumerate(pairs):
                dve.wait_ge(g["rounded"], i + 1)
                nc.vector.tensor_tensor(dst[:, 1], src, dst[:, 0].bitcast(F32), ALU.subtract).then_inc(g["split"], 1)
            dve.wait_ge(g["consts"], 7)
            for dst, src in ((z.ones_r, ones_s), (z.ones_b, ones_s), (z.sum_col, col_s), (z.before, tri_s), (z.causal, causal_s), (z.ident_b, z.ident),
                             (z.slot_id, ids), (z.row_id, pid)):
                nc.vector.tensor_copy(dst[:], src[:]).then_inc(g["split"], 1)
            dve.wait_ge(g["rows_loaded"], 48)
            nc.vector.tensor_scalar(z.lng_half[:], lng_s[:], 0.5, None, ALU.mult).then_inc(g["split"], 1)
            nc.vector.tensor_scalar(z.lnb_half[:], lnb_s[:], 0.5, None, ALU.mult).then_inc(g["split"], 1)
            dve.wait_ge(g["split"], 13)


def spread(nc, dve, g, buf, b, rows, D):
    dve.wait_ge(g["stats_done"], rows * b + rows)
    st = buf.stats
    nc.vector.tensor_tensor(buf.pair[:], st[:, :, 1:3], st[:, :, 4:6], ALU.add).then_inc(g["halves_met"], 1)
    nc.vector.tensor_tensor(buf.diff[:], st[:, :, 1], st[:, :, 4], ALU.subtract).then_inc(g["halves_met"], 1)
    dve.wait_ge(g["halves_met"], 2 * b + 2)
    nc.vector.tensor_scalar(buf.mean[:], buf.pair[:, :, 0], 0.5, None, ALU.mult).then_inc(g["mean_ready"], 1)
    nc.vector.scalar_tensor_tensor(buf.diff2[:], buf.diff[:], 0.25, buf.diff[:], ALU.mult, ALU.mult).then_inc(g["diff_squared"], 1)
    dve.wait_ge(g["diff_squared"], b + 1)
    nc.vector.scalar_tensor_tensor(buf.var[:], buf.pair[:, :, 1], 1.0 / D, buf.diff2[:], ALU.mult, ALU.add).then_inc(g["var_ready"], 1)


def mm3(nc, out, lhs, rhs, first, last, **kw):
    nc.tensor.matmul(out, lhs[0], rhs[0], start=first, stop=False, **kw)
    nc.tensor.matmul(out, lhs[0], rhs[1], start=False, stop=False, **kw)
    return nc.tensor.matmul(out, lhs[1], rhs[0], start=False, stop=last, **kw)


def first_layer(nc, z):
    B, KD, D, E, NK, NV = z.B, z.KD, z.D, z.E, z.NK, z.NV
    with ExitStack() as ctx:
        sb, ps, sems = scope(nc, ctx)
        xa = sb("xa", [P, CPB, CT, D])
        xn = sb("xn", [P, CPB, CT, D])
        xn2 = sb("xn2", [P, CPB, 2, CT, D], F32R)
        xt2 = sb("xt2", [P, CPB, 2, KD, CHUNK], F32R)
        qf = sb("qf", [P, CPB, KD, CHUNK])
        qt2 = sb("qt2", [P, CPB, 2, KD, CHUNK], F32R)
        kf = sb("kf", [P, CPB, CT, D])
        k2 = sb("k2", [P, CPB, 2, CT, D], F32R)
        norm = Names()
        norm.stats = sb("stats", [P, CPB * CT, 6])
        norm.pair = sb("pair", [P, CPB * CT, 2])
        norm.diff = sb("diff", [P, CPB * CT])
        norm.diff2 = sb("diff_sq", [P, CPB * CT])
        norm.mean = sb("mean", [P, CPB * CT])
        norm.var = sb("var", [P, CPB * CT])
        var_eps = sb("var_eps", [P, CPB * CT])
        rstd = sb("rstd", [P, CPB * CT])
        logit = sb("logit", [P, CPB, CT, E])
        best = sb("best", [P, CPB, CT])
        tied = sb("tied", [P, CPB, CT, E])
        lead = sb("lead", [P, CPB, CT])
        pick = sb("pick", [P, CPB, CT, E], BF16)
        row = sb("row", [P, CPB, CT, E])
        row_f = sb("row_f", [P, CPB, CT])
        row_u = sb("row_u", [P, CPB, CT], U32)
        m2 = sb("m2", [P, 2, KD, D], F32R)
        ks2 = sb("ks2", [P, 2, D], F32R)
        kv2 = sb("kv2", [P, 2, KD, NV], F32R)
        zsum = sb("zsum", [P, CPB, CT])
        zinv = sb("zinv", [P, CPB, CT])
        pad_u = sb("pad_u", [P, E], U32)
        pad_f = sb("pad_f", [P, E])
        zeros = sb("zeros", [P, D])
        wide = ps("wide", [P, 2, KD, CHUNK])
        narrow = ps("narrow", [P, 2, 512])
        m_ps = ps("m_ps", [P, KD, D])
        ks_ps = ps("ks_ps", [P, 512])

        g = sems("stats_done halves_met mean_ready diff_squared var_ready eps_added rstd_ready xn_ready xn_rounded xn_split t_ready t_rounded t_split "
                 "k_ready k_exp k_capped k_full k_read k_rounded k_split q_ready q_exp q_capped q_full q_rounded q_split "
                 "best_found ties_found ties_ranked lead_found picked pick_kept counted row_based row_masked row_found "
                 "row_ready base_moved m_done m_rounded m_split kv_ready kv_rounded kv_split v_ready zsum_ready zinv_ready "
                 "rows_ready zeroed pads_based pads_ready pads_stored row_kept")
        xa_loaded = [ctx.enter_context(nc.semaphore(f"xa_loaded{h}")) for h in range(CPB)]
        scattered = [ctx.enter_context(nc.semaphore(f"scattered{h}")) for h in range(CPB)]
        block = ctx.enter_context(nc.Block())
        LAST = B - 1
        K0, KV, K1, V0, R0, V1, R1, USES = 0, CT, CT + KD, 2 * CT + KD, 3 * CT + KD, 3 * CT + KD + 1, 4 * CT + KD + 1, 4 * CT + KD + 2
        k_slot = lambda h, t: narrow[:, ((K0, K1)[h] + t) % 2, :]
        kv_slot = lambda j: narrow[:, (KV + j) % 2, :]
        v_slot = lambda h, t: narrow[:, ((V0, V1)[h] + t) % 2, :]
        r_slot = lambda h: narrow[:, (R0, R1)[h] % 2, :]
        assert USES % 2 == 0

        @block.sync
        def _(sp):
            for h in range(CPB):
                sp.dma_start(xa[:, h], z.x_rows[h]).then_inc(xa_loaded[h], 16)
            with sp.Fori(1, B) as b:
                for h in range(CPB):
                    sp.wait_ge(g["xn_ready"], CPB * b - CPB + h + 1)
                    sp.dma_start(xa[:, h], z.x_rows[CPB * b + h]).then_inc(xa_loaded[h], 16)
            sp.wait_ge(xa_loaded[CPB - 1], 16 * B)

        @block.tensor
        def _(pe):
            def turn(b, h, reused):
                pe.wait_ge(g["xn_ready"], CPB * b + h + 1)
                if reused:
                    pe.wait_ge(g["q_full"], KD * (CPB * b - CPB + h + 1))
                for k in range(KD):
                    for t in range(CT):
                        i = nc.tensor.transpose(wide[:, h, k, t * P:(t + 1) * P], xn[:, h, t, k * P:(k + 1) * P], z.ident[:])
                i.then_inc(g["t_ready"], 1)

            def sums(b, h):
                pe.wait_ge(g["xn_split"], CPB * b + h + 1)
                pe.wait_ge(g["k_split"], CPB * b + h + 1)
                if h == 0:
                    pe.wait_ge(g["m_split"], 2 * b)
                for t in range(CT):
                    st, en = (h == 0 and t == 0), (h == CPB - 1 and t == CT - 1)
                    kk = [k2[:, h, a, t, :] for a in range(2)]
                    for j in range(KD):
                        mm3(nc, m_ps[:, j, :], [xn2[:, h, a, t, j * P:(j + 1) * P] for a in range(2)], kk,
                            st and j == 0, en, skip_group_check=True)
                    nc.tensor.matmul(ks_ps[:, 0:D], z.ones_r[:], kk[0], start=st, stop=False)
                    i = nc.tensor.matmul(ks_ps[:, 0:D], z.ones_r[:], kk[1], start=False, stop=en)
                i.then_inc(g["m_done"], 1)

            def keys(b, h, before):
                pe.wait_ge(g["t_split"], CPB * b + h + 1)
                for t in range(CT):
                    if before[t] is not None:
                        pe.wait_ge(*before[t])
                    for k in range(KD):
                        i = mm3(nc, k_slot(h, t)[:, 0:NK], [xt2[:, h, a, k, t * P:(t + 1) * P] for a in range(2)],
                                [z.wkg[:, a, k, :] for a in range(2)], k == 0, k == KD - 1)
                    i.then_inc(g["k_ready"], 1)

            def kv(b, before):
                pe.wait_ge(g["m_split"], 2 * b + 2)
                for j in range(KD):
                    pe.wait_ge(*before[j])
                    o = kv_slot(j)[:, 0:NV]
                    for k in range(KD):
                        mm3(nc, o, [m2[:, a, k, j * P:(j + 1) * P] for a in range(2)], [z.wv[:, a, k, :] for a in range(2)],
                            k == 0, False)
                    nc.tensor.matmul(o, ks2[:, 0, j * P:(j + 1) * P], z.sum_col[:], start=False, stop=False)
                    nc.tensor.matmul(o, ks2[:, 1, j * P:(j + 1) * P], z.sum_col[:], start=False, stop=True).then_inc(g["kv_ready"], 1)

            def values(b, h, before):
                pe.wait_ge(g["kv_split"], KD * b + KD)
                pe.wait_ge(g["q_split"], CPB * b + h + 1)
                for t in range(CT):
                    pe.wait_ge(*before[t])
                    for j in range(KD):
                        i = mm3(nc, v_slot(h, t)[:, 0:NV], [qt2[:, h, a, j, t * P:(t + 1) * P] for a in range(2)],
                                [kv2[:, a, j, :] for a in range(2)], j == 0, j == KD - 1)
                    i.then_inc(g["v_ready"], 1)

            def count(b, h, before):
                pe.wait_ge(g["picked"], CPB * b + h + 1)
                pe.wait_ge(*before)
                o = r_slot(h)
                flat = pick[:, h].rearrange("p t e -> p (t e)")
                nc.tensor.matmul(o[:, 0:CT * E], z.before[:], flat, start=True, stop=False, skip_group_check=True)
                for d in range(1, CT):
                    nc.tensor.matmul(o[:, d * E:CT * E], z.ones_b[:], flat[:, 0:(CT - d) * E], start=False, stop=False,
                                     skip_group_check=True)
                for t in range(CT):
                    i = nc.tensor.matmul(o[:, CT * E:CT * E + E], z.ones_b[:], pick[:, h, t, :], start=False,
                                         stop=(t == CT - 1), skip_group_check=True)
                i.then_inc(g["counted"], 1)

            def q(b, h):
                for j in range(KD):
                    for k in range(KD):
                        i = mm3(nc, wide[:, h, j, :], [z.wq[:, a, k, j * P:(j + 1) * P] for a in range(2)],
                                [xt2[:, h, a, k, :] for a in range(2)], k == 0, k == KD - 1)
                    i.then_inc(g["q_ready"], 1)

            key_read = lambda b, h, t: (g["k_read"], CT * (CPB * b + h) + t + 1)
            kv_read = lambda b, j: (g["kv_split"], KD * b + j + 1)
            row_read = lambda b, h, t: (g["rows_ready"], CT * (CPB * b + h) + t + 1)
            place_read = lambda b, h: (g["base_moved"], CPB * b + h + 1)

            turn(0, 0, False)
            turn(0, 1, False)
            keys(0, 0, [None, None, key_read(0, 0, 0), key_read(0, 0, 1)])
            keys(0, 1, [key_read(0, 0, 2), key_read(0, 0, 3), key_read(0, 1, 0), key_read(0, 1, 1)])
            count(0, 0, key_read(0, 1, 2))
            q(0, 0)
            count(0, 1, key_read(0, 1, 3))
            q(0, 1)
            sums(0, 0)
            with pe.Fori(1, B) as b:
                turn(b, 0, True)
                sums(b - 1, 1)
                turn(b, 1, True)
                pe.wait_ge(*place_read(b - 1, 0))
                keys(b, 0, [None, place_read(b - 1, 1), key_read(b, 0, 0), key_read(b, 0, 1)])
                kv(b - 1, [key_read(b, 0, 2), key_read(b, 0, 3)])
                keys(b, 1, [kv_read(b - 1, 0), kv_read(b - 1, 1), key_read(b, 1, 0), key_read(b, 1, 1)])
                values(b - 1, 0, [key_read(b, 1, 2), key_read(b, 1, 3), row_read(b - 1, 0, 0), row_read(b - 1, 0, 1)])
                count(b, 0, row_read(b - 1, 0, 2))
                q(b, 0)
                values(b - 1, 1, [row_read(b - 1, 0, 3), place_read(b, 0), row_read(b - 1, 1, 0), row_read(b - 1, 1, 1)])
                count(b, 1, row_read(b - 1, 1, 2))
                q(b, 1)
                sums(b, 0)
            sums(LAST, 1)
            kv(LAST, [row_read(LAST - 1, 1, CT - 1), place_read(LAST, 1)])
            values(LAST, 0, [kv_read(LAST, 0), kv_read(LAST, 1), row_read(LAST, 0, 0), row_read(LAST, 0, 1)])
            values(LAST, 1, [row_read(LAST, 0, 3), row_read(LAST, 0, 2), row_read(LAST, 1, 0), row_read(LAST, 1, 1)])

        @block.scalar
        def _(act):
            def round_turned(b, h):
                act.wait_ge(g["t_ready"], CPB * b + h + 1)
                nc.scalar.activation(xt2[:, h, 0], wide[:, h], ACT.Copy).then_inc(g["t_rounded"], 1)

            def round_sums(b):
                act.wait_ge(g["m_done"], CPB * b + CPB)
                nc.scalar.activation(m2[:, 0], m_ps[:], ACT.Copy).then_inc(g["m_rounded"], 1)
                nc.scalar.activation(ks2[:, 0], ks_ps[:, 0:D], ACT.Copy).then_inc(g["m_rounded"], 1)

            def exp_keys(b, h):
                for t in range(CT):
                    act.wait_ge(g["k_ready"], CT * (CPB * b + h) + t + 1)
                    nc.scalar.activation(kf[:, h, t, :], k_slot(h, t)[:, 0:D], ACT.Exp).then_inc(g["k_exp"], 1)

            def exp_q(b, h):
                for j in range(KD):
                    act.wait_ge(g["q_ready"], KD * (CPB * b + h) + j + 1)
                    nc.scalar.activation(qf[:, h, j, :], wide[:, h, j, :], ACT.Exp).then_inc(g["q_exp"], 1)

            def round_kv(b):
                for j in range(KD):
                    act.wait_ge(g["kv_ready"], KD * b + j + 1)
                    nc.scalar.activation(kv2[:, 0, j, :], kv_slot(j)[:, 0:NV], ACT.Copy).then_inc(g["kv_rounded"], 1)

            def round_xn(b, h):
                act.wait_ge(g["xn_ready"], CPB * b + h + 1)
                act.wait_ge(g["m_done"], CPB * b)
                nc.scalar.activation(xn2[:, h, 0], xn[:, h], ACT.Copy).then_inc(g["xn_rounded"], 1)

            def round_keys(b, h):
                act.wait_ge(g["k_full"], CT * (CPB * b + h + 1))
                nc.scalar.activation(k2[:, h, 0], kf[:, h], ACT.Copy).then_inc(g["k_rounded"], 1)

            def round_q(b, h):
                act.wait_ge(g["q_full"], KD * (CPB * b + h + 1))
                nc.scalar.activation(qt2[:, h, 0], qf[:, h], ACT.Copy).then_inc(g["q_rounded"], 1)

            def scale_rows(b, h):
                for t in range(CT):
                    act.wait_ge(g["zinv_ready"], CT * (CPB * b + h) + t + 1)
                    nc.scalar.activation(z.res[:, bass.ds(CT * CPB * b + CT * h + t, 1), :], v_slot(h, t)[:, 0:D].unsqueeze(1),
                                         ACT.Copy, scale=zinv[:, h, t:t + 1]).then_inc(g["rows_ready"], 1)

            round_turned(0, 0)
            round_turned(0, 1)
            exp_keys(0, 0)
            exp_keys(0, 1)
            round_xn(0, 0)
            round_keys(0, 0)
            round_xn(0, 1)
            exp_q(0, 0)
            round_keys(0, 1)
            exp_q(0, 1)
            round_q(0, 0)
            round_q(0, 1)
            with act.Fori(1, B) as b:
                round_turned(b, 0)
                round_sums(b - 1)
                round_turned(b, 1)
                exp_keys(b, 0)
                round_kv(b - 1)
                exp_keys(b, 1)
                round_xn(b, 0)
                scale_rows(b - 1, 0)
                round_keys(b, 0)
                round_xn(b, 1)
                exp_q(b, 0)
                scale_rows(b - 1, 1)
                round_keys(b, 1)
                exp_q(b, 1)
                round_q(b, 0)
                round_q(b, 1)
            round_sums(LAST)
            round_kv(LAST)
            scale_rows(LAST, 0)
            scale_rows(LAST, 1)

        @block.vector
        def _(dve):
            def norm_stats(b):
                for h in range(CPB):
                    dve.wait_ge(xa_loaded[h], 16 * b + 16)
                    for t in range(CT):
                        nc.vector.bn_stats(norm.stats[:, h * CT + t, :], xa[:, h, t, :]).then_inc(g["stats_done"], 1)
                spread(nc, dve, g, norm, b, CPB * CT, D)

            def norm_apply(b, h, reused):
                dve.wait_ge(g["rstd_ready"], b + 1)
                if reused:
                    dve.wait_ge(scattered[h], 16 * CT * b)
                    dve.wait_ge(g["xn_split"], CPB * b - CPB + h + 1)
                for t in range(CT):
                    n = h * CT + t
                    i = nc.vector.tensor_scalar(xn[:, h, t, :], xa[:, h, t, :], norm.mean[:, n:n + 1], rstd[:, n:n + 1],
                                                ALU.subtract, ALU.mult)
                i.then_inc(g["xn_ready"], 1)

            def split_turned(b, h):
                dve.wait_ge(g["t_rounded"], CPB * b + h + 1)
                nc.vector.tensor_tensor(xt2[:, h, 1], wide[:, h], xt2[:, h, 0].bitcast(F32), ALU.subtract).then_inc(g["t_split"], 1)

            def split_sums(b):
                dve.wait_ge(g["m_rounded"], 2 * b + 2)
                nc.vector.tensor_tensor(m2[:, 1], m_ps[:], m2[:, 0].bitcast(F32), ALU.subtract).then_inc(g["m_split"], 1)
                nc.vector.tensor_tensor(ks2[:, 1], ks_ps[:, 0:D], ks2[:, 0].bitcast(F32), ALU.subtract).then_inc(g["m_split"], 1)

            def keys(b, h):
                for t in range(CT):
                    n = CT * (CPB * b + h) + t + 1
                    dve.wait_ge(g["k_exp"], n)
                    nc.vector.tensor_scalar(kf[:, h, t, :], kf[:, h, t, :], 1.0, None, ALU.min).then_inc(g["k_capped"], 1)
                    dve.wait_ge(g["k_capped"], n)
                    nc.vector.scalar_tensor_tensor(kf[:, h, t, :], k_slot(h, t)[:, 0:D], 0.0, kf[:, h, t, :], ALU.max, ALU.add).then_inc(g["k_full"], 1)
                    nc.vector.tensor_copy(logit[:, h, t, :], k_slot(h, t)[:, D:NK]).then_inc(g["k_read"], 1)

            def q(b, h):
                for j in range(KD):
                    n = KD * (CPB * b + h) + j + 1
                    dve.wait_ge(g["q_exp"], n)
                    nc.vector.tensor_scalar(qf[:, h, j, :], qf[:, h, j, :], 1.0, None, ALU.min).then_inc(g["q_capped"], 1)
                    dve.wait_ge(g["q_capped"], n)
                    nc.vector.scalar_tensor_tensor(qf[:, h, j, :], wide[:, h, j, :], 0.0, qf[:, h, j, :], ALU.max, ALU.add).then_inc(g["q_full"], 1)

            def split_kv(b):
                for j in range(KD):
                    dve.wait_ge(g["kv_rounded"], KD * b + j + 1)
                    nc.vector.tensor_tensor(kv2[:, 1, j, :], kv_slot(j)[:, 0:NV], kv2[:, 0, j, :].bitcast(F32), ALU.subtract).then_inc(g["kv_split"], 1)

            def route(b, h):
                c = CPB * b + h + 1
                dve.wait_ge(g["k_read"], CT * c)
                nc.vector.tensor_reduce(best[:, h], logit[:, h], AX_X, ALU.max).then_inc(g["best_found"], 1)
                dve.wait_ge(g["best_found"], c)
                nc.vector.tensor_tensor(tied[:, h], logit[:, h], best[:, h].unsqueeze(2).to_broadcast([P, CT, E]), ALU.is_equal).then_inc(g["ties_found"], 1)
                dve.wait_ge(g["ties_found"], c)
                nc.vector.tensor_tensor(tied[:, h], tied[:, h], z.first_rank[:], ALU.mult).then_inc(g["ties_ranked"], 1)
                dve.wait_ge(g["ties_ranked"], c)
                nc.vector.tensor_reduce(lead[:, h], tied[:, h], AX_X, ALU.max).then_inc(g["lead_found"], 1)
                dve.wait_ge(g["lead_found"], c)
                nc.vector.tensor_tensor(pick[:, h], tied[:, h], lead[:, h].unsqueeze(2).to_broadcast([P, CT, E]), ALU.is_equal).then_inc(g["picked"], 1)
                dve.wait_ge(g["picked"], c)
                nc.vector.tensor_copy(z.chosen[:, bass.ds(CT * CPB * b + CT * h, CT), :], pick[:, h]).then_inc(g["pick_kept"], 1)

            def place(b, h):
                c = CPB * b + h + 1
                o = r_slot(h)
                dve.wait_ge(g["counted"], c)
                if not (isinstance(b, int) and b == 0 and h == 0):
                    dve.wait_ge(g["base_moved"], c - 1)
                nc.vector.tensor_tensor(row[:, h], o[:, 0:CT * E].rearrange("p (t e) -> p t e", e=E),
                                        z.next_row[:].unsqueeze(1).to_broadcast([P, CT, E]), ALU.add).then_inc(g["row_based"], 1)
                dve.wait_ge(g["row_based"], c)
                nc.vector.tensor_tensor(z.next_row[:], o[:, CT * E:CT * E + E], z.next_row[:], ALU.add).then_inc(g["base_moved"], 1)
                nc.vector.tensor_tensor(row[:, h], row[:, h], pick[:, h], ALU.mult).then_inc(g["row_masked"], 1)
                dve.wait_ge(g["row_masked"], c)
                nc.vector.tensor_reduce(row_f[:, h], row[:, h], AX_X, ALU.add).then_inc(g["row_found"], 1)
                dve.wait_ge(g["row_found"], c)
                nc.vector.tensor_copy(row_u[:, h], row_f[:, h]).then_inc(g["row_ready"], 1)
                nc.vector.tensor_copy(z.place[:, bass.ds(CT * CPB * b + CT * h, CT)], row_f[:, h]).then_inc(g["row_kept"], 1)

            def divisors(b, h):
                for t in range(CT):
                    n = CT * (CPB * b + h) + t + 1
                    dve.wait_ge(g["v_ready"], n)
                    nc.vector.tensor_scalar(zsum[:, h, t:t + 1], v_slot(h, t)[:, D:D + 1], Z_EPS, 2.0, ALU.add, ALU.mult).then_inc(g["zsum_ready"], 1)
                    dve.wait_ge(g["zsum_ready"], n)
                    nc.vector.reciprocal(zinv[:, h, t:t + 1], zsum[:, h, t:t + 1]).then_inc(g["zinv_ready"], 1)

            norm_stats(0)
            norm_apply(0, 0, False)
            norm_apply(0, 1, False)
            split_turned(0, 0)
            split_turned(0, 1)
            keys(0, 0)
            route(0, 0)
            keys(0, 1)
            route(0, 1)
            place(0, 0)
            norm_stats(1)
            q(0, 0)
            place(0, 1)
            q(0, 1)
            norm_apply(1, 0, True)
            norm_apply(1, 1, True)

            def body(b, more):
                split_turned(b, 0)
                split_sums(b - 1)
                split_turned(b, 1)
                keys(b, 0)
                split_kv(b - 1)
                route(b, 0)
                keys(b, 1)
                route(b, 1)
                divisors(b - 1, 0)
                place(b, 0)
                if more:
                    norm_stats(b + 1)
                q(b, 0)
                divisors(b - 1, 1)
                place(b, 1)
                q(b, 1)
                if more:
                    norm_apply(b + 1, 0, True)
                    norm_apply(b + 1, 1, True)

            with dve.Fori(1, LAST) as b:
                body(b, True)
            body(LAST, False)
            split_sums(LAST)
            split_kv(LAST)
            divisors(LAST, 0)
            divisors(LAST, 1)
            dve.wait_ge(g["base_moved"], CPB * B)
            nc.vector.tensor_scalar(pad_f[:], z.next_row[:], z.row_id[:, 0:1], None, ALU.add).then_inc(g["pads_based"], 1)
            dve.wait_ge(g["pads_based"], 1)
            nc.vector.tensor_copy(pad_u[:], pad_f[:]).then_inc(g["pads_ready"], 1)
            dve.wait_ge(g["row_kept"], CPB * B)

        @block.gpsimd
        def _(pool):
            def norm_scale(b):
                pool.wait_ge(g["var_ready"], b + 1)
                nc.gpsimd.tensor_tensor(var_eps[:], norm.var[:], z.eps[:], ALU.add).then_inc(g["eps_added"], 1)
                pool.wait_ge(g["eps_added"], b + 1)
                nc.gpsimd.tensor_tensor(rstd[:], var_eps[:], z.neg_half[:], ALU.pow).then_inc(g["rstd_ready"], 1)

            def split_xn(b, h):
                pool.wait_ge(g["xn_rounded"], CPB * b + h + 1)
                nc.gpsimd.tensor_tensor(xn2[:, h, 1], xn[:, h], xn2[:, h, 0].bitcast(F32), ALU.subtract).then_inc(g["xn_split"], 1)

            def split_keys(b, h):
                pool.wait_ge(g["k_rounded"], CPB * b + h + 1)
                nc.gpsimd.tensor_tensor(k2[:, h, 1], kf[:, h], k2[:, h, 0].bitcast(F32), ALU.subtract).then_inc(g["k_split"], 1)

            def split_q(b, h):
                pool.wait_ge(g["q_rounded"], CPB * b + h + 1)
                nc.gpsimd.tensor_tensor(qt2[:, h, 1], qf[:, h], qt2[:, h, 0].bitcast(F32), ALU.subtract).then_inc(g["q_split"], 1)

            def rows_placed(b, h):
                pool.wait_ge(g["row_ready"], CPB * b + h + 1)

            def scatter(b, h):
                for t in range(CT):
                    nc.gpsimd.indirect_dma_start(
                        out=z.sorted_dram.ap(), out_offset=bass.IndirectOffsetOnAxis(ap=row_u[:, h, t:t + 1], axis=0),
                        in_=xn[:, h, t, :], in_offset=None).then_inc(scattered[h], 16)

            def body(b, more):
                split_xn(b, 0)
                split_keys(b, 0)
                split_xn(b, 1)
                if more:
                    norm_scale(b + 1)
                rows_placed(b, 0)
                split_keys(b, 1)
                scatter(b, 0)
                rows_placed(b, 1)
                split_q(b, 0)
                scatter(b, 1)
                split_q(b, 1)

            norm_scale(0)
            with pool.Fori(0, LAST) as b:
                body(b, True)
            nc.gpsimd.memset(zeros[:], 0.0).then_inc(g["zeroed"], 1)
            body(LAST, False)
            pool.wait_ge(g["pads_ready"], 1)
            pool.wait_ge(g["zeroed"], 1)
            for e in range(E):
                nc.gpsimd.indirect_dma_start(
                    out=z.sorted_dram.ap(), out_offset=bass.IndirectOffsetOnAxis(ap=pad_u[:, e:e + 1], axis=0),
                    in_=zeros[:], in_offset=None).then_inc(g["pads_stored"], 16)
            for h in range(CPB):
                pool.wait_ge(scattered[h], 16 * CT * B)
            pool.wait_ge(g["pads_stored"], 16 * E)


def experts(nc, z, wg, wu, wd):
    KD, D, E, DE, SLOTS = z.KD, z.D, z.E, z.DE, z.SLOTS
    QUAD = 4
    PAIRS = SLOTS // 2
    ROUNDS = PAIRS // QUAD
    BITS = (E - 1).bit_length()
    assert PAIRS == ROUNDS * QUAD and E == 1 << BITS and 2 * QUAD * BITS <= 24
    with ExitStack() as ctx:
        sb, ps, sems = scope(nc, ctx)
        wgu = sb("wgu", [P, KD, E, 2 * DE])
        wdn = sb("wdn", [DE, E, D])
        held = sb("held", [P, E])
        held_i = sb("held_i", [P, E], I32)
        tiles_i = sb("tiles_i", [P, E], I32)
        tiles = sb("tiles", [P, E])
        ends = sb("ends", [P, E])
        starts = sb("starts", [P, E])
        moved = sb("moved", [P, E])
        one_col = sb("one_col", [P, E])
        past = sb("past", [P, SLOTS, E])
        past_end = sb("past_end", [P, SLOTS, E])
        owner = sb("owner", [P, SLOTS])
        start = sb("start", [P, SLOTS])
        within = sb("within", [P, SLOTS])
        real = sb("real", [P, SLOTS])
        row_a = sb("row_a", [P, SLOTS])
        row_b = sb("row_b", [P, SLOTS])
        owner_c = sb("owner_c", [P, SLOTS])
        row_i = sb("row_i", [P, SLOTS], I32)
        shifted = sb("shifted", [P, ROUNDS, 2 * QUAD])
        owners = sb("owners", [P, ROUNDS])
        owners_i = sb("owners_i", [P, ROUNDS], I32)
        shift_all = sb("shift_all", [P, z.TILES, E])
        shift = sb("shift", [P, z.TILES])
        xg = sb("xg", [P, QUAD, 2, D])
        xgt = sb("xgt", [P, QUAD, KD, 2, P])
        gate = sb("gate", [P, 2, 2, DE])
        hid = sb("hid", [P, 2, 2, DE])
        hidt = sb("hidt", [DE, 2, 2, P])
        th = sb("th", [P, 2, 2, D])
        y = sb("y", [P, QUAD, 2, D])
        t_ps = ps("t_ps", [P, 2, KD, 2, P])
        gu_ps = ps("gu_ps", [P, 2, 512])
        ht_ps = ps("ht_ps", [P, 2, 512])
        y_ps = ps("y_ps", [P, 2, 2, D])
        g = sems("weights_loaded step tables_ready t_ready t_copied gu_ready gate_relu squared hid_ready ht_ready ht_copied y_ready y_tanh "
                 "silu_ready")
        loaded = [[ctx.enter_context(nc.semaphore(f"loaded{u}_{i}")) for i in range(QUAD)] for u in range(2)]
        stored = [ctx.enter_context(nc.semaphore(f"stored{i}")) for i in range(QUAD)]
        block = ctx.enter_context(nc.Block())
        y_rows = z.expert_dram.ap().rearrange("(n u p) d -> n p u d", u=2, p=P)

        def load(eng, n, i, u):
            first = eng.value_load(row_i[0:1, bass.ds(n * 2 + u, 1)], min_val=0, max_val=E * z.REGION - P)
            eng.dma_start(xg[:, i, u, :], z.sorted_dram.ap()[bass.ds(first, P), :]).then_inc(loaded[u][i], 16)

        def load_again(eng, n, i, u):
            eng.wait_ge(g["t_ready"], n + i - QUAD + 1)
            load(eng, n + i, i, u)

        def load_first(eng, u):
            for i in range(QUAD):
                load(eng, i, i, u)
            for i in range(QUAD):
                load_again(eng, QUAD, i, u)

        @block.sync
        def _(sp):
            for k in range(KD):
                for half, src in ((0, wg), (1, wu)):
                    sp.dma_start(wgu[:, k, :, half * DE:(half + 1) * DE],
                                 src[:, k * P:(k + 1) * P, :].rearrange("e p d -> p e d")).then_inc(g["weights_loaded"], 16)
            sp.dma_start(wdn[:], wd.rearrange("e d h -> d e h")).then_inc(g["weights_loaded"], 16)
            sp.wait_ge(g["tables_ready"], 1)

            def store(n, i):
                sp.wait_ge(g["silu_ready"], n + i + 1)
                sp.dma_start(y_rows[n + i], y[:, i]).then_inc(stored[i], 16)

            load_first(sp, 0)
            with sp.Fori(0, ROUNDS - 2) as r:
                for i in range(QUAD + 1):
                    if i < QUAD:
                        load_again(sp, r * QUAD + 2 * QUAD, i, 0)
                    if i == QUAD:
                        store(r * QUAD, i - 2)
                        store(r * QUAD, i - 1)
                    elif i >= 2:
                        store(r * QUAD, i - 2)
            for n in range(PAIRS - 2 * QUAD, PAIRS, QUAD):
                for i in range(QUAD):
                    store(n, i)
            for i in range(QUAD):
                sp.wait_ge(stored[i], 16 * ROUNDS)

        @block.gpsimd
        def _(pool):
            pool.wait_ge(g["tables_ready"], 1)
            load_first(pool, 1)
            with pool.Fori(0, ROUNDS - 2) as r:
                for i in range(QUAD):
                    load_again(pool, r * QUAD + 2 * QUAD, i, 1)

        @block.tensor
        def _(pe):
            pe.wait_ge(g["tables_ready"], 1)
            pe.wait_ge(g["weights_loaded"], 16 * (2 * KD + 1))

            def turn(n, i, reused):
                for u in range(2):
                    pe.wait_ge(loaded[u][i], (n - i) * (16 // QUAD) + 16)
                if reused:
                    pe.wait_ge(g["t_copied"], n - 1)
                for k in range(KD):
                    for u in range(2):
                        t = nc.tensor.transpose(t_ps[:, i % 2, k, u, :], xg[:, i, u, k * P:(k + 1) * P], z.ident[:])
                t.then_inc(g["t_ready"], 1)

            def gate_up(n, i, e, reused):
                pe.wait_ge(g["t_copied"], n + 1)
                if reused:
                    pe.wait_ge(g["hid_ready"], n - 1)
                for u in range(2):
                    for k in range(KD):
                        m = nc.tensor.matmul(gu_ps[:, i % 2, u * 2 * DE:(u + 1) * 2 * DE], xgt[:, i, k, u, :],
                                             wgu[:, k, bass.ds(e[i][u], 1), :].rearrange("p a f -> p (a f)"),
                                             start=(u == 0 and k == 0), stop=(k == KD - 1), skip_group_check=True)
                m.then_inc(g["gu_ready"], 1)

            def hidden_ready(n, reused):
                pe.wait_ge(g["hid_ready"], n + 1)
                if reused:
                    pe.wait_ge(g["ht_copied"], n - 1)

            def turn_hidden(n, i):
                for u in range(2):
                    t = nc.tensor.transpose(ht_ps[0:DE, i % 2, u * P:(u + 1) * P], hid[:, i % 2, u, :], z.ident[:])
                t.then_inc(g["ht_ready"], 1)

            def down(n, i, e, reused):
                pe.wait_ge(g["ht_copied"], n + 1)
                if reused:
                    pe.wait_ge(g["silu_ready"], n - 1)
                for u in range(2):
                    m = nc.tensor.matmul(y_ps[:, i % 2, u, :], hidt[:, i % 2, u, :],
                                         wdn[:, bass.ds(e[i][u], 1), :].rearrange("p a h -> p (a h)"),
                                         start=(u == 0), stop=True, skip_group_check=True)
                m.then_inc(g["y_ready"], 1)

            def four_pairs(r, first, last):
                n = r * QUAD
                owners = pe.value_load(owners_i[0:1, bass.ds(r, 1)], min_val=0, max_val=E ** (2 * QUAD) - 1)
                e = [[(owners >> (BITS * (2 * i + u))) & (E - 1) for u in range(2)] for i in range(QUAD)]
                up = lambda i: gate_up(n + i, i, e, not first or i >= 2)
                dn = lambda i: down(n + i, i, e, not first or i >= 2)

                def turns(i):
                    hidden_ready(n + i, not first or i >= 2)
                    if not last:
                        turn(n + QUAD + i, i, True)
                    turn_hidden(n + i, i)

                up(0)
                up(1)
                turns(0)
                up(2)
                turns(1)
                dn(0)
                up(3)
                turns(2)
                dn(1)
                turns(3)
                dn(2)
                dn(3)

            for i in range(QUAD):
                turn(i, i, i >= 2)
            four_pairs(0, True, False)
            with pe.Fori(1, ROUNDS - 1) as r:
                four_pairs(r, False, False)
            four_pairs(ROUNDS - 1, False, True)

        @block.scalar
        def _(act):
            def copy_turned(n, i, reused):
                act.wait_ge(g["t_ready"], n + 1)
                if reused:
                    act.wait_ge(g["gu_ready"], n - QUAD + 1)
                nc.scalar.activation(xgt[:, i], t_ps[:, i % 2], ACT.Copy).then_inc(g["t_copied"], 1)

            def relu(n, i):
                act.wait_ge(g["gu_ready"], n + 1)
                o = gu_ps[:, i % 2, 0:4 * DE].rearrange("p (u f) -> p u f", u=2)
                nc.scalar.activation(gate[:, i % 2], o[:, :, 0:DE], ACT.Relu).then_inc(g["gate_relu"], 1)

            def copy_hidden(n, i):
                act.wait_ge(g["ht_ready"], n + 1)
                nc.scalar.activation(hidt[:, i % 2], ht_ps[0:DE, i % 2, 0:2 * P].rearrange("p (u t) -> p u t", u=2), ACT.Copy).then_inc(g["ht_copied"], 1)

            def tanh(n, i):
                act.wait_ge(g["y_ready"], n + 1)
                nc.scalar.activation(th[:, i % 2], y_ps[:, i % 2], ACT.Tanh, scale=0.5).then_inc(g["y_tanh"], 1)

            def four_pairs(n, last):
                def turns(i):
                    if not last:
                        copy_turned(n + QUAD + i, i, True)
                    copy_hidden(n + i, i)

                relu(n, 0)
                relu(n + 1, 1)
                turns(0)
                relu(n + 2, 2)
                turns(1)
                tanh(n, 0)
                relu(n + 3, 3)
                turns(2)
                tanh(n + 1, 1)
                turns(3)
                tanh(n + 2, 2)
                tanh(n + 3, 3)

            for i in range(QUAD):
                copy_turned(i, i, False)
            with act.Fori(0, ROUNDS - 1) as r:
                four_pairs(r * QUAD, False)
            four_pairs(PAIRS - QUAD, True)

        @block.vector
        def _(dve):
            count = 0

            def link(ins):
                nonlocal count
                count += 1
                ins.then_inc(g["step"], 1)
                dve.wait_ge(g["step"], count)

            link(nc.vector.tensor_tensor(held[:], z.next_row[:], z.region0[:], ALU.subtract))
            link(nc.vector.tensor_scalar(held[:], held[:], float(P - 1), None, ALU.add))
            link(nc.vector.tensor_copy(held_i[:], held[:]))
            link(nc.vector.tensor_scalar(tiles_i[:], held_i[:], P.bit_length() - 1, None, ALU.arith_shift_right))
            link(nc.vector.tensor_copy(tiles[:], tiles_i[:]))
            link(nc.vector.memset(one_col[:], 1.0))
            link(nc.vector.tensor_tensor_scan(ends[:], one_col[:], tiles[:], 0.0, ALU.mult, ALU.add))
            link(nc.vector.tensor_tensor(starts[:], ends[:], tiles[:], ALU.subtract))
            shape = [P, SLOTS, E]
            link(nc.vector.tensor_tensor(past[:], ends[:].unsqueeze(1).to_broadcast(shape), z.slot_id[:].unsqueeze(2).to_broadcast(shape), ALU.is_le))
            link(nc.vector.tensor_reduce(owner[:], past[:], AX_X, ALU.add))
            link(nc.vector.tensor_tensor(past_end[:], past[:], ends[:].unsqueeze(1).to_broadcast(shape), ALU.mult))
            link(nc.vector.tensor_reduce(start[:], past_end[:], AX_X, ALU.max))
            link(nc.vector.tensor_tensor(within[:], z.slot_id[:], start[:], ALU.subtract))
            link(nc.vector.tensor_scalar(real[:], owner[:], float(E), None, ALU.is_lt))
            link(nc.vector.tensor_scalar(row_a[:], owner[:], float(z.REGION), float(-(E - 1) * z.REGION), ALU.mult, ALU.add))
            link(nc.vector.scalar_tensor_tensor(row_b[:], within[:], float(P), row_a[:], ALU.mult, ALU.add))
            link(nc.vector.tensor_tensor(row_b[:], row_b[:], real[:], ALU.mult))
            link(nc.vector.tensor_scalar(row_b[:], row_b[:], float((E - 1) * z.REGION), None, ALU.add))
            link(nc.vector.tensor_scalar(owner_c[:], owner[:], float(E - 1), None, ALU.min))
            link(nc.vector.tensor_copy(row_i[:], row_b[:]))
            for i in range(2 * QUAD):
                link(nc.vector.tensor_scalar(shifted[:, :, i], owner_c[:].rearrange("p (r i) -> p r i", i=2 * QUAD)[:, :, i], float(E ** i), None, ALU.mult))
            link(nc.vector.tensor_reduce(owners[:], shifted[:], AX_X, ALU.add))
            nc.vector.tensor_copy(owners_i[:], owners[:]).then_inc(g["tables_ready"], 1)
            link(nc.vector.scalar_tensor_tensor(moved[:], starts[:], float(P), z.region0[:], ALU.mult, ALU.subtract))
            link(nc.vector.tensor_tensor(shift_all[:], z.chosen[:], moved[:].unsqueeze(1).to_broadcast([P, z.TILES, E]), ALU.mult))
            link(nc.vector.tensor_reduce(shift[:], shift_all[:], AX_X, ALU.add))
            link(nc.vector.tensor_tensor(z.place[:, 0:z.TILES], z.place[:, 0:z.TILES], shift[:], ALU.add))

            def hidden(n, i):
                dve.wait_ge(g["gate_relu"], n + 1)
                o = gu_ps[:, i % 2, 0:4 * DE].rearrange("p (u f) -> p u f", u=2)
                nc.vector.scalar_tensor_tensor(hid[:, i % 2], o[:, :, 0:DE], 0.0, gate[:, i % 2], ALU.max, ALU.mult).then_inc(g["squared"], 1)
                dve.wait_ge(g["squared"], n + 1)
                nc.vector.tensor_tensor(hid[:, i % 2], o[:, :, DE:2 * DE], hid[:, i % 2], ALU.mult).then_inc(g["hid_ready"], 1)

            def silu(n, i, reused):
                dve.wait_ge(g["y_tanh"], n + 1)
                if reused:
                    dve.wait_ge(stored[i], (n - i) * (16 // QUAD))
                nc.vector.scalar_tensor_tensor(y[:, i], th[:, i % 2], 1.0, y_ps[:, i % 2], ALU.add, ALU.mult).then_inc(g["silu_ready"], 1)

            def four_pairs(n, reused):
                hidden(n, 0)
                hidden(n + 1, 1)
                hidden(n + 2, 2)
                silu(n, 0, reused)
                hidden(n + 3, 3)
                for i in range(1, QUAD):
                    silu(n + i, i, reused)

            four_pairs(0, False)
            with dve.Fori(1, ROUNDS) as r:
                four_pairs(r * QUAD, True)


def second_layer(nc, z):
    B, KD, D = z.B, z.KD, z.D
    SCALE = float(D) ** -0.5
    UT = 2
    UNITS = z.TILES // UT
    SLOTS = 4
    ROUNDS = UNITS // SLOTS
    assert UNITS == SLOTS * ROUNDS and UT * D <= 512
    with ExitStack() as ctx:
        sb, ps, sems = scope(nc, ctx)
        xin = sb("xin", [P, SLOTS, UT, D])
        moe = sb("moe", [P, SLOTS, UT, D])
        gather_u = sb("gather_u", [P, SLOTS, UT], U32)
        stats = sb("stats2", [P, SLOTS, UT, 6])
        pair = sb("pair2", [P, SLOTS, UT, 2])
        diff = sb("diff2", [P, SLOTS, UT])
        diff_sq = sb("diff_sq2", [P, SLOTS, UT])
        neg_mean = sb("neg_mean", [P, SLOTS, UT])
        var = sb("var2", [P, SLOTS, UT])
        var_eps = sb("var_eps2", [P, SLOTS, UT])
        rstd = sb("rstd2", [P, SLOTS, UT])
        shift = sb("shift2", [P, SLOTS, UT])
        var_n = sb("var_n", [P, SLOTS, UT])
        var_n2 = sb("var_n2", [P, SLOTS, UT])
        var_n_eps = sb("var_n_eps", [P, SLOTS, UT])
        rstd_n = sb("rstd_n", [P, SLOTS, UT])
        xn = sb("xn2nd", [P, SLOTS, UT, D])
        xt = sb("xt", [P, 2, KD, UT * P])
        qt = sb("qt", [P, 2, KD, UT * P])
        vo = sb("vo", [P, 2, UT, D])
        top = sb("top", [P, SLOTS, UT])
        ntop = sb("ntop", [P, SLOTS, UT])
        pr = sb("pr", [P, 2, UT, P])
        total = sb("total", [P, SLOTS, UT])
        total_eps = sb("total_eps", [P, SLOTS, UT])
        inv = sb("inv", [P, SLOTS, UT])
        prt = sb("prt", [P, 2, UT, P])
        zg = sb("zg", [P, SLOTS, UT, D])
        th = sb("th2", [P, SLOTS, UT, D])
        att = sb("att", [P, SLOTS, UT, D])
        t_ps = ps("t2_ps", [P, KD, UT * P])
        q_ps = ps("q_ps", [P, KD, UT * P])
        v_ps = ps("v_ps", [P, UT, D])
        s_ps = ps("s_ps", [P, 4, P])
        pt_ps = ps("pt_ps", [P, 4, P])
        a_ps = ps("a_ps", [P, UT, D])
        g = sems("index_ready moe_scaled x1_ready stats_done halves_met mean_ready diff_squared var_ready eps_added rstd_ready "
                 "shift_ready var_scaled var_scaled2 neps_added nrstd_ready xn_ready t_ready t_copied q_ready q_copied "
                 "v_ready v_copied s_ready top_found top_ready p_ready pt_ready pt_copied att_ready z_scaled z_ready "
                 "z_tanh gate_ready total_based inv_ready att_scaled gated out_ready")
        per_slot = lambda name: [ctx.enter_context(nc.semaphore(f"{name}{i}")) for i in range(SLOTS)]
        x_loaded, moe_loaded, out_stored = per_slot("x_loaded"), per_slot("moe_loaded"), per_slot("out_stored")
        block = ctx.enter_context(nc.Block())
        x_units = z.x.rearrange("b (n u p) d -> (b n) p u d", u=UT, p=P)
        out_units = z.out.rearrange("b (n u p) d -> (b n) p u d", u=UT, p=P)
        tiles = lambda n: z.res[:, bass.ds(UT * n, UT), :]

        def there(n, least=0):
            return not isinstance(n, int) or least <= n < UNITS

        def steps(eng, first, step, last):
            for n in range(first, SLOTS):
                step(n, n % SLOTS)
            with eng.Fori(1, ROUNDS - 1) as r:
                for i in range(SLOTS):
                    step(r * SLOTS + i, i)
            for n in range(UNITS - SLOTS, last + 1):
                step(n, n % SLOTS)

        at = lambda i, ahead: (i + ahead) % SLOTS
        turns = lambda n, i, k: (n - i) * (k // SLOTS)

        @block.sync
        def _(sp):
            def load(n, i):
                if there(n):
                    if there(n, SLOTS):
                        sp.wait_ge(g["x1_ready"], n - SLOTS + 1)
                    sp.dma_start(xin[:, i], x_units[n]).then_inc(x_loaded[i], 16)

            def store(n, i):
                if there(n):
                    sp.wait_ge(g["out_ready"], n + 1)
                    sp.dma_start(out_units[n], att[:, i]).then_inc(out_stored[i], 16)

            def step(n, i):
                load(n + 4, i)
                store(n - 2, at(i, -2))

            steps(sp, -4, step, UNITS + 1)
            for i in range(SLOTS):
                sp.wait_ge(out_stored[i], 16 * ROUNDS)

        @block.tensor
        def _(pe):
            def q(n, i):
                if there(n):
                    pe.wait_ge(g["t_copied"], n + 1)
                    if there(n, 1):
                        pe.wait_ge(g["q_copied"], n)
                    for j in range(KD):
                        for k in range(KD):
                            m = nc.tensor.matmul(q_ps[:, j, :], z.wqk[:, k, j * P:(j + 1) * P], xt[:, i % 2, k, :],
                                                 start=(j == 0 and k == 0), stop=(k == KD - 1), skip_group_check=True)
                    m.then_inc(g["q_ready"], 1)

            def turn(n, i):
                if there(n):
                    pe.wait_ge(g["xn_ready"], n + 1)
                    if there(n, 1):
                        pe.wait_ge(g["t_copied"], n)
                    for k in range(KD):
                        for t in range(UT):
                            m = nc.tensor.transpose(t_ps[:, k, t * P:(t + 1) * P], xn[:, i, t, k * P:(k + 1) * P], z.ident[:])
                    m.then_inc(g["t_ready"], 1)

            def v(n, i):
                if there(n):
                    if there(n, 1):
                        pe.wait_ge(g["v_copied"], n)
                    for t in range(UT):
                        for k in range(KD):
                            m = nc.tensor.matmul(v_ps[:, t, :], xt[:, i % 2, k, t * P:(t + 1) * P], z.wvo[:, k, :],
                                                 start=(t == 0 and k == 0), stop=(k == KD - 1), skip_group_check=True)
                    m.then_inc(g["v_ready"], 1)

            def turn_probs(n, i):
                if there(n):
                    pe.wait_ge(g["p_ready"], UT * n + UT)
                    if there(n, 1):
                        pe.wait_ge(g["pt_copied"], n)
                    for t in range(UT):
                        m = nc.tensor.transpose(pt_ps[:, t, :], pr[:, i % 2, t, :], z.ident[:])
                    m.then_inc(g["pt_ready"], 1)

            def scores(n, i):
                if there(n):
                    pe.wait_ge(g["q_copied"], n + 1)
                    for t in range(UT):
                        for j in range(KD):
                            nc.tensor.matmul(s_ps[:, t, :], qt[:, i % 2, j, t * P:(t + 1) * P], xt[:, i % 2, j, t * P:(t + 1) * P],
                                             start=(t == 0 and j == 0), stop=False, skip_group_check=True)
                        m = nc.tensor.matmul(s_ps[:, t, :], z.ident_b[:], z.causal[:], start=False, stop=True, skip_group_check=True)
                    m.then_inc(g["s_ready"], 1)

            def attend(n, i):
                if there(n):
                    pe.wait_ge(g["pt_copied"], n + 1)
                    pe.wait_ge(g["v_copied"], n + 1)
                    if there(n, 1):
                        pe.wait_ge(g["att_scaled"], UT * n)
                    for t in range(UT):
                        m = nc.tensor.matmul(a_ps[:, t, :], prt[:, i % 2, t, :], vo[:, i % 2, t, :], start=(t == 0), stop=True,
                                             skip_group_check=True)
                    m.then_inc(g["att_ready"], 1)

            def step(n, i):
                q(n, i)
                turn(n + 1, at(i, 1))
                v(n, i)
                turn_probs(n - 1, at(i, -1))
                scores(n, i)
                attend(n - 1, at(i, -1))

            steps(pe, -1, step, UNITS)

        @block.scalar
        def _(act):
            def copy_q(n, i):
                if there(n):
                    act.wait_ge(g["q_ready"], n + 1)
                    nc.scalar.activation(qt[:, i % 2], q_ps[:], ACT.Copy).then_inc(g["q_copied"], 1)

            def copy_turned(n, i):
                if there(n):
                    act.wait_ge(g["t_ready"], n + 1)
                    if there(n, 2):
                        act.wait_ge(g["s_ready"], n - 1)
                    nc.scalar.activation(xt[:, i % 2], t_ps[:], ACT.Copy).then_inc(g["t_copied"], 1)

            def copy_probs(n, i):
                if there(n):
                    act.wait_ge(g["pt_ready"], n + 1)
                    if there(n, 2):
                        act.wait_ge(g["att_ready"], n - 1)
                    nc.scalar.activation(prt[:, i % 2], pt_ps[:, 0:UT], ACT.Copy).then_inc(g["pt_copied"], 1)

            def copy_v(n, i):
                if there(n):
                    act.wait_ge(g["v_ready"], n + 1)
                    if there(n, 2):
                        act.wait_ge(g["att_ready"], n - 1)
                    nc.scalar.activation(vo[:, i % 2], v_ps[:], ACT.Copy).then_inc(g["v_copied"], 1)

            def norm_apply(n, i):
                if there(n):
                    act.wait_ge(g["shift_ready"], n + 1)
                    if there(n, SLOTS):
                        act.wait_ge(g["z_scaled"], n - SLOTS + 1)
                    for t in range(UT):
                        m = nc.scalar.activation(xn[:, i, t, :].unsqueeze(1), z.res[:, bass.ds(UT * n + t, 1), :], ACT.Identity,
                                                 bias=shift[:, i, t:t + 1], scale=rstd[:, i, t:t + 1])
                    m.then_inc(g["xn_ready"], 1)

            def tanh(n, i):
                if there(n):
                    act.wait_ge(g["z_ready"], n + 1)
                    nc.scalar.activation(th[:, i], zg[:, i], ACT.Tanh).then_inc(g["z_tanh"], 1)

            def exp(n, i):
                if there(n):
                    act.wait_ge(g["top_ready"], n + 1)
                    for t in range(UT):
                        nc.scalar.activation(pr[:, i % 2, t, :], s_ps[:, t, :], ACT.Exp, bias=ntop[:, i, t:t + 1], scale=SCALE,
                                             accum_out=total[:, i, t:t + 1]).then_inc(g["p_ready"], 1)

            def step(n, i):
                copy_q(n, i)
                copy_turned(n + 1, at(i, 1))
                copy_probs(n - 1, at(i, -1))
                copy_v(n, i)
                norm_apply(n + 2, at(i, 2))
                tanh(n, i)
                exp(n, i)

            steps(act, -2, step, UNITS)

        @block.vector
        def _(dve):
            def index(n, i):
                nc.vector.tensor_copy(gather_u[:, i], z.place[:, bass.ds(UT * n, UT)]).then_inc(g["index_ready"], 1)

            def gate(n, i):
                if there(n):
                    dve.wait_ge(g["z_tanh"], n + 1)
                    nc.vector.scalar_tensor_tensor(zg[:, i], th[:, i], 1.0, zg[:, i], ALU.add, ALU.mult).then_inc(g["gate_ready"], 1)

            def first_result(n, i):
                if there(n):
                    dve.wait_ge(moe_loaded[i], turns(n, i, 16 * UT) + 16 * UT)
                    nc.vector.tensor_tensor(moe[:, i], moe[:, i], tiles(n), ALU.mult).then_inc(g["moe_scaled"], 1)
                    dve.wait_ge(x_loaded[i], turns(n, i, 16) + 16)
                    dve.wait_ge(g["moe_scaled"], n + 1)
                    nc.vector.tensor_tensor(tiles(n), moe[:, i], xin[:, i], ALU.add).then_inc(g["x1_ready"], 1)
                    dve.wait_ge(g["x1_ready"], n + 1)
                    if there(n + 2, SLOTS):
                        index(n + 2, at(i, 2))
                    for t in range(UT):
                        nc.vector.bn_stats(stats[:, i, t], z.res[:, bass.ds(UT * n + t, 1), :]).then_inc(g["stats_done"], 1)

            def spread(n, i):
                if there(n):
                    dve.wait_ge(g["stats_done"], UT * n + UT)
                    nc.vector.tensor_tensor(pair[:, i], stats[:, i, :, 1:3], stats[:, i, :, 4:6], ALU.add).then_inc(g["halves_met"], 1)
                    nc.vector.tensor_tensor(diff[:, i], stats[:, i, :, 1], stats[:, i, :, 4], ALU.subtract).then_inc(g["halves_met"], 1)
                    dve.wait_ge(g["halves_met"], 2 * n + 2)
                    nc.vector.tensor_scalar(neg_mean[:, i], pair[:, i, :, 0], -0.5, None, ALU.mult).then_inc(g["mean_ready"], 1)
                    nc.vector.scalar_tensor_tensor(diff_sq[:, i], diff[:, i], 0.25, diff[:, i], ALU.mult, ALU.mult).then_inc(g["diff_squared"], 1)
                    dve.wait_ge(g["diff_squared"], n + 1)
                    nc.vector.scalar_tensor_tensor(var[:, i], pair[:, i, :, 1], 1.0 / D, diff_sq[:, i], ALU.mult, ALU.add).then_inc(g["var_ready"], 1)

            def scale_gate(n, i):
                if there(n):
                    dve.wait_ge(g["nrstd_ready"], n + 1)
                    dve.wait_ge(g["xn_ready"], n + 1)
                    if there(n, SLOTS):
                        dve.wait_ge(g["gated"], n - SLOTS + 1)
                    for t in range(UT):
                        m = nc.vector.scalar_tensor_tensor(zg[:, i, t, :], xn[:, i, t, :], rstd_n[:, i, t:t + 1], z.lng_half[:], ALU.mult, ALU.mult)
                    m.then_inc(g["z_scaled"], 1)

            def maximum(n, i):
                if there(n):
                    dve.wait_ge(g["s_ready"], n + 1)
                    nc.vector.tensor_reduce(top[:, i], s_ps[:, 0:UT], AX_X, ALU.max).then_inc(g["top_found"], 1)
                    dve.wait_ge(g["top_found"], n + 1)
                    nc.vector.tensor_scalar(ntop[:, i], top[:, i], -SCALE, None, ALU.mult).then_inc(g["top_ready"], 1)

            def divisor(n, i):
                if there(n):
                    dve.wait_ge(g["p_ready"], UT * n + UT)
                    nc.vector.tensor_scalar(total_eps[:, i], total[:, i], Z_EPS, None, ALU.add).then_inc(g["total_based"], 1)
                    dve.wait_ge(g["total_based"], n + 1)
                    nc.vector.reciprocal(inv[:, i], total_eps[:, i]).then_inc(g["inv_ready"], 1)

            def attend(n, i):
                if there(n):
                    dve.wait_ge(g["inv_ready"], n + 1)
                    dve.wait_ge(g["att_ready"], n + 1)
                    if there(n, SLOTS):
                        dve.wait_ge(out_stored[i], turns(n, i, 16))
                    for t in range(UT):
                        nc.vector.scalar_tensor_tensor(att[:, i, t, :], a_ps[:, t, :], inv[:, i, t:t + 1], z.bout[:], ALU.mult, ALU.add).then_inc(g["att_scaled"], 1)
                    dve.wait_ge(g["att_scaled"], UT * n + UT)
                    dve.wait_ge(g["gate_ready"], n + 1)
                    nc.vector.tensor_tensor(att[:, i], att[:, i], zg[:, i], ALU.mult).then_inc(g["gated"], 1)

            def step(n, i):
                gate(n - 1, at(i, -1))
                first_result(n + 3, at(i, 3))
                divisor(n - 1, at(i, -1))
                spread(n + 3, at(i, 3))
                scale_gate(n + 1, at(i, 1))
                maximum(n, i)
                attend(n - 1, at(i, -1))

            for n in range(SLOTS):
                index(n, n)
            steps(dve, -3, step, UNITS)

        @block.gpsimd
        def _(pool):
            def indexed(n, i):
                if there(n):
                    pool.wait_ge(g["index_ready"], n + 1)

            def gather(n, i):
                if there(n):
                    for t in range(UT):
                        nc.gpsimd.indirect_dma_start(
                            out=moe[:, i, t, :], out_offset=None, in_=z.expert_dram.ap(),
                            in_offset=bass.IndirectOffsetOnAxis(ap=gather_u[:, i, t:t + 1], axis=0)).then_inc(moe_loaded[i], 16)

            def norm_scale(n, i):
                if there(n):
                    eps, power = z.eps[:, 0:UT], z.neg_half[:, 0:UT]
                    pool.wait_ge(g["var_ready"], n + 1)
                    nc.gpsimd.tensor_tensor(var_eps[:, i], var[:, i], eps, ALU.add).then_inc(g["eps_added"], 1)
                    pool.wait_ge(g["eps_added"], n + 1)
                    nc.gpsimd.tensor_tensor(rstd[:, i], var_eps[:, i], power, ALU.pow).then_inc(g["rstd_ready"], 1)
                    pool.wait_ge(g["rstd_ready"], n + 1)
                    nc.gpsimd.tensor_tensor(shift[:, i], neg_mean[:, i], rstd[:, i], ALU.mult).then_inc(g["shift_ready"], 1)
                    nc.gpsimd.tensor_tensor(var_n[:, i], var[:, i], rstd[:, i], ALU.mult).then_inc(g["var_scaled"], 1)
                    pool.wait_ge(g["var_scaled"], n + 1)
                    nc.gpsimd.tensor_tensor(var_n2[:, i], var_n[:, i], rstd[:, i], ALU.mult).then_inc(g["var_scaled2"], 1)
                    pool.wait_ge(g["var_scaled2"], n + 1)
                    nc.gpsimd.tensor_tensor(var_n_eps[:, i], var_n2[:, i], eps, ALU.add).then_inc(g["neps_added"], 1)
                    pool.wait_ge(g["neps_added"], n + 1)
                    nc.gpsimd.tensor_tensor(rstd_n[:, i], var_n_eps[:, i], power, ALU.pow).then_inc(g["nrstd_ready"], 1)

            def shift_gate(n, i):
                if there(n):
                    pool.wait_ge(g["z_scaled"], n + 1)
                    nc.gpsimd.tensor_tensor(zg[:, i], zg[:, i], z.lnb_half[:].unsqueeze(1).to_broadcast([P, UT, D]), ALU.add).then_inc(g["z_ready"], 1)

            def result(n, i):
                if there(n):
                    pool.wait_ge(g["gated"], n + 1)
                    nc.gpsimd.tensor_tensor(att[:, i], att[:, i], tiles(n), ALU.add).then_inc(g["out_ready"], 1)

            def step(n, i):
                indexed(n + 4, i)
                norm_scale(n + 2, at(i, 2))
                shift_gate(n, i)
                gather(n + 4, i)
                result(n - 2, at(i, -2))

            steps(pool, -4, step, UNITS + 1)


_INS = ["L0_attn_x", "L0_attn_W", "L0_ffn_gate_w", "L0_ffn_wg", "L0_ffn_wu", "L0_ffn_wd", "L1_attn_W_qkv", "L1_attn_W_out",
        "L1_attn_b_out", "L1_ffn_ln_g", "L1_ffn_ln_b"]


def kernel(**inputs):
    import numpy as np
    import concourse.bacc as bacc
    from concourse.bass_utils import run_bass_kernel_spmd

    nc = bacc.Bacc("TRN2", target_bir_lowering=False, num_devices=1)
    arrays, args = {}, []
    for name in _INS:
        a = np.ascontiguousarray(inputs[name])
        arrays[f"in_{name}"] = a
        args.append(nc.dram_tensor(f"in_{name}", a.shape, mybir.dt.from_np(a.dtype), kind="ExternalInput").ap())
    x = arrays["in_L0_attn_x"]
    out = nc.dram_tensor("out_rows", x.shape, mybir.dt.from_np(x.dtype), kind="ExternalOutput").ap()
    program(nc, *args, out)
    result = run_bass_kernel_spmd(nc, [arrays], core_ids=[0])
    return result.results[0]["out_rows"]
```

```python
from contextlib import ExitStack

import concourse.bass as bass
from concourse import mybir

F32 = mybir.dt.float32
F32R = mybir.dt.float32r
BF16 = mybir.dt.bfloat16
I32 = mybir.dt.int32
U32 = mybir.dt.uint32
ALU = mybir.AluOpType
ACT = mybir.ActivationFunctionType
AX_X = mybir.AxisListType.X

P = 128
CT = 4
CHUNK = CT * P
CPB = 2
LN_EPS = 1e-5
Z_EPS = 1e-6
MASKED = -3.0e38


class Names:
    pass


def program(nc, x, W, gate_w, wg, wu, wd, W_qkv, W_out, b_out, ln_g, ln_b, out):
    z = Names()
    z.B, z.L, z.D = x.shape
    z.E, _, z.DE = wg.shape
    z.KD = z.D // P
    z.NK = z.D + z.E
    z.NV = z.D + 2
    z.TILES = z.B * z.L // P
    z.REGION = z.B * z.L + P
    z.SLOTS = z.TILES + z.E
    assert z.L == CPB * CHUNK and z.D == z.KD * P and z.SLOTS % 2 == 0 and z.KD == 2
    z.x, z.out = x, out
    z.sorted_dram = nc.dram_tensor("sorted_rows", (z.E * z.REGION, z.D), F32)
    z.expert_dram = nc.dram_tensor("expert_rows", (z.SLOTS * P, z.D), F32)

    with ExitStack() as whole:
        def sb(name, shape, dt=F32):
            return whole.enter_context(nc.sbuf_tensor(name, shape, dt))

        z.wq = sb("wq", [P, 2, z.KD, z.D], F32R)
        z.wkg = sb("wkg", [P, 2, z.KD, z.NK], F32R)
        z.wv = sb("wv", [P, 2, z.KD, z.D], F32R)
        z.wqk = sb("wqk", [P, z.KD, z.D])
        z.wvo = sb("wvo", [P, z.KD, z.D])
        z.ident = sb("ident", [P, P])
        z.ones_r = sb("ones_r", [P, 2], F32R)
        z.ones_b = sb("ones_b", [P, P], BF16)
        z.before = sb("before", [P, P], BF16)
        z.ident_b = sb("ident_b", [P, P], BF16)
        z.causal = sb("causal", [P, P], BF16)
        z.first_rank = sb("first_rank", [P, CT, z.E])
        z.region0 = sb("region0", [P, z.E])
        z.row_id = sb("row_id", [P, 1])
        z.slot_id = sb("slot_id", [P, z.SLOTS])
        z.neg_half = sb("neg_half", [P, CPB * CT])
        z.eps = sb("eps", [P, CPB * CT])
        z.bout = sb("bout", [P, z.D])
        z.lng_half = sb("lng_half", [P, z.D])
        z.lnb_half = sb("lnb_half", [P, z.D])
        z.res = sb("res", [P, z.TILES, z.D])
        z.chosen = sb("chosen", [P, z.TILES, z.E], BF16)
        z.place = sb("place", [P, z.TILES + CPB * CT])
        z.next_row = sb("next_row", [P, z.E])
        prologue(nc, z, W, gate_w, W_qkv, W_out, b_out, ln_g, ln_b)
        first_layer(nc, z)
        experts(nc, z, wg, wu, wd)
        second_layer(nc, z)


def scope(nc, ctx):
    def sb(name, shape, dt=F32):
        return ctx.enter_context(nc.sbuf_tensor(name, shape, dt))

    def ps(name, shape):
        return ctx.enter_context(nc.psum_tensor(name, shape, F32))

    def sems(names):
        return {n: ctx.enter_context(nc.semaphore(n)) for n in names.split()}

    return sb, ps, sems


def prologue(nc, z, W, gate_w, W_qkv, W_out, b_out, ln_g, ln_b):
    KD, D, E, NK = z.KD, z.D, z.E, z.NK
    with ExitStack() as ctx:
        sb, ps, sems = scope(nc, ctx)
        w_s = sb("w_s", [P, KD, 3 * D])
        gate_s = sb("gate_s", [E, D])
        kg_s = sb("kg_s", [P, KD, NK])
        w2_s = sb("w2_s", [P, KD, 3 * D])
        wo_s = sb("wo_s", [P, KD, D])
        turned = sb("turned", [P, 4, KD, D])
        ones_s = sb("ones_s", [P, P])
        tri_s = sb("tri_s", [P, P])
        causal_s = sb("causal_s", [P, P])
        ids = sb("ids", [P, z.SLOTS], I32)
        pid = sb("pid", [P, 1], I32)
        lng_s = sb("lng_s", [P, D])
        lnb_s = sb("lnb_s", [P, D])
        turn_ps = ps("turn_ps", [P, 4, KD, D])
        fold_ps = ps("fold_ps", [P, 2, KD, D])
        gate_ps = ps("gate_ps", [P, KD, 64])
        g = sems("w_loaded gate_loaded w2_loaded wo_loaded rows_loaded blank consts gate_turned staged "
                 "rounded split turned_ready turned_copied folded_ready folded_copied placed")
        block = ctx.enter_context(nc.Block())

        @block.sync
        def _(sp):
            sp.dma_start(w_s[:], W.rearrange("(k p) n -> p k n", p=P)).then_inc(g["w_loaded"], 16)
            sp.dma_start(gate_s[:], gate_w).then_inc(g["gate_loaded"], 16)
            sp.dma_start(w2_s[:], W_qkv.rearrange("(k p) n -> p k n", p=P)).then_inc(g["w2_loaded"], 16)
            sp.dma_start(wo_s[:], W_out.rearrange("(k p) n -> p k n", p=P)).then_inc(g["wo_loaded"], 16)
            for dst, src in ((z.bout, b_out), (lng_s, ln_g), (lnb_s, ln_b)):
                sp.dma_start(dst[:], src.partition_broadcast(P)).then_inc(g["rows_loaded"], 16)
            sp.wait_ge(g["rows_loaded"], 48)

        @block.gpsimd
        def _(pool):
            nc.gpsimd.memset(z.ident[:], 0.0).then_inc(g["blank"], 1)
            nc.gpsimd.memset(tri_s[:], 1.0).then_inc(g["blank"], 1)
            nc.gpsimd.memset(causal_s[:], 0.0).then_inc(g["blank"], 1)
            pool.wait_ge(g["blank"], 3)
            nc.gpsimd.affine_select(out=z.ident[:], in_=z.ident[:], compare_op=ALU.not_equal, fill=1.0, base=0,
                                    pattern=[[-1, P]], channel_multiplier=1).then_inc(g["consts"], 1)
            nc.gpsimd.affine_select(out=tri_s[:], in_=tri_s[:], compare_op=ALU.is_gt, fill=0.0, base=0,
                                    pattern=[[1, P]], channel_multiplier=-1).then_inc(g["consts"], 1)
            nc.gpsimd.affine_select(out=causal_s[:], in_=causal_s[:], compare_op=ALU.is_ge, fill=MASKED, base=0,
                                    pattern=[[-1, P]], channel_multiplier=1).then_inc(g["consts"], 1)
            nc.gpsimd.memset(ones_s[:], 1.0).then_inc(g["consts"], 1)
            nc.gpsimd.iota(ids[:], pattern=[[1, z.SLOTS]], base=0, channel_multiplier=0).then_inc(g["consts"], 1)
            nc.gpsimd.iota(pid[:], pattern=[[0, 1]], base=0, channel_multiplier=1).then_inc(g["consts"], 1)
            nc.gpsimd.memset(z.neg_half[:], -0.5).then_inc(g["placed"], 1)
            nc.gpsimd.memset(z.eps[:], LN_EPS).then_inc(g["placed"], 1)
            for e in range(E):
                nc.gpsimd.memset(z.first_rank[:, :, e:e + 1], float(E - e)).then_inc(g["placed"], 1)
                nc.gpsimd.memset(z.region0[:, e:e + 1], float(e * z.REGION)).then_inc(g["placed"], 1)
                nc.gpsimd.memset(z.next_row[:, e:e + 1], float(e * z.REGION)).then_inc(g["placed"], 1)
            nc.gpsimd.memset(z.place[:, z.TILES:], 0.0).then_inc(g["placed"], 1)
            pool.wait_ge(g["placed"], 3 + 3 * E)

        @block.tensor
        def _(pe):
            pe.wait_ge(g["consts"], 6)
            pe.wait_ge(g["gate_loaded"], 16)
            for k in range(KD):
                t = nc.tensor.transpose(gate_ps[:, k, 0:E], gate_s[:, k * P:(k + 1) * P], z.ident[0:E, 0:E])
            t.then_inc(g["gate_turned"], 1)
            pe.wait_ge(g["w2_loaded"], 16)
            pe.wait_ge(g["wo_loaded"], 16)
            for m, src in enumerate((w2_s[:, :, 0:D], w2_s[:, :, D:2 * D], w2_s[:, :, 2 * D:3 * D], wo_s[:, :, :])):
                for k in range(KD):
                    for j in range(KD):
                        t = nc.tensor.transpose(turn_ps[:, m, k, j * P:(j + 1) * P], src[:, j, k * P:(k + 1) * P], z.ident[:])
                t.then_inc(g["turned_ready"], 1)
            pe.wait_ge(g["turned_copied"], 4)
            for m, (a, b) in enumerate(((0, 1), (2, 3))):
                for j in range(KD):
                    for k in range(KD):
                        t = nc.tensor.matmul(fold_ps[:, m, j, :], turned[:, a, k, j * P:(j + 1) * P], turned[:, b, k, :],
                                             start=(k == 0), stop=(k == KD - 1))
                t.then_inc(g["folded_ready"], 1)

        @block.scalar
        def _(act):
            for m in range(4):
                act.wait_ge(g["turned_ready"], m + 1)
                nc.scalar.activation(turned[:, m], turn_ps[:, m], ACT.Copy).then_inc(g["turned_copied"], 1)
            for m, dst in enumerate((z.wqk, z.wvo)):
                act.wait_ge(g["folded_ready"], m + 1)
                nc.scalar.activation(dst[:], fold_ps[:, m], ACT.Copy).then_inc(g["folded_copied"], 1)
            act.wait_ge(g["folded_copied"], 2)

        @block.vector
        def _(dve):
            dve.wait_ge(g["w_loaded"], 16)
            nc.vector.tensor_copy(kg_s[:, :, 0:D], w_s[:, :, D:2 * D]).then_inc(g["staged"], 1)
            dve.wait_ge(g["gate_turned"], 1)
            nc.vector.tensor_copy(kg_s[:, :, D:NK], gate_ps[:, :, 0:E]).then_inc(g["staged"], 1)
            dve.wait_ge(g["staged"], 2)
            pairs = ((z.wq, w_s[:, :, 0:D]), (z.wkg, kg_s[:]), (z.wv, w_s[:, :, 2 * D:3 * D]))
            for dst, src in pairs:
                nc.vector.tensor_copy(dst[:, 0], src).then_inc(g["rounded"], 1)
            for i, (dst, src) in enumerate(pairs):
                dve.wait_ge(g["rounded"], i + 1)
                nc.vector.tensor_tensor(dst[:, 1], src, dst[:, 0].bitcast(F32), ALU.subtract).then_inc(g["split"], 1)
            dve.wait_ge(g["consts"], 6)
            for dst, src in ((z.ones_r, ones_s[:, 0:2]), (z.ones_b, ones_s), (z.before, tri_s), (z.causal, causal_s), (z.ident_b, z.ident),
                             (z.slot_id, ids), (z.row_id, pid)):
                nc.vector.tensor_copy(dst[:], src[:]).then_inc(g["split"], 1)
            dve.wait_ge(g["rows_loaded"], 48)
            nc.vector.tensor_scalar(z.lng_half[:], lng_s[:], 0.5, None, ALU.mult).then_inc(g["split"], 1)
            nc.vector.tensor_scalar(z.lnb_half[:], lnb_s[:], 0.5, None, ALU.mult).then_inc(g["split"], 1)
            dve.wait_ge(g["split"], 12)


def pipeline(eng, first, step, last, units, slots):
    for n in range(first, slots):
        step(n, n % slots, n // slots)
    with eng.Fori(1, units // slots - 1) as r:
        for i in range(slots):
            step(r * slots + i, i, r)
    for n in range(units - slots, last + 1):
        step(n, n % slots, n // slots)


def mm3(nc, out, lhs, rhs, first, last, **kw):
    nc.tensor.matmul(out, lhs[0], rhs[0], start=first, stop=False, **kw)
    nc.tensor.matmul(out, lhs[0], rhs[1], start=False, stop=False, **kw)
    return nc.tensor.matmul(out, lhs[1], rhs[0], start=False, stop=last, **kw)


def first_layer(nc, z):
    KD, D, E, NK, NV = z.KD, z.D, z.E, z.NK, z.NV
    UT = 2
    UNITS = z.TILES // UT
    ROW = z.L // (UT * P)
    SLOTS = 2 * ROW
    CU = CT // UT
    X_SLOTS, TWO = 4, 2
    V_LAG = ROW + 2
    COUNT_LAG = CU + 1
    SCATTER_LAG = COUNT_LAG + 1
    assert UNITS % SLOTS == 0 and CU == 2 and UT * D <= 512 and NK + (CT + 1) * E <= 512
    with ExitStack() as ctx:
        sb, ps, sems = scope(nc, ctx)
        xa = sb("xa", [P, X_SLOTS, UT, D])
        stats = sb("stats", [P, X_SLOTS, UT, 6])
        pair = sb("pair", [P, X_SLOTS, UT, 2])
        diff = sb("diff", [P, X_SLOTS, UT])
        diff_sq = sb("diff_sq", [P, X_SLOTS, UT])
        neg_mean = sb("neg_mean1", [P, X_SLOTS, UT])
        var = sb("var", [P, X_SLOTS, UT])
        var_eps = sb("var_eps", [P, X_SLOTS, UT])
        rstd = sb("rstd", [P, X_SLOTS, UT])
        shift = sb("shift1", [P, X_SLOTS, UT])
        xn = sb("xn", [P, SLOTS, UT, D])
        xn2 = sb("xn2", [P, X_SLOTS, 2, UT, D], F32R)
        xt2 = sb("xt2", [P, TWO, 2, KD, UT * P], F32R)
        qf = sb("qf", [P, TWO, KD, UT * P])
        qt2 = sb("qt2", [P, SLOTS, 2, KD, UT * P], F32R)
        kf = sb("kf", [P, TWO, UT, D])
        k2 = sb("k2", [P, TWO, 2, UT, D], F32R)
        logit = sb("logit", [P, TWO, CT, E])
        best = sb("best", [P, TWO, CT])
        tied = sb("tied", [P, TWO, CT, E])
        lead = sb("lead", [P, TWO, CT])
        pick = sb("pick", [P, TWO, CT, E], BF16)
        row = sb("row", [P, TWO, CT, E])
        row_f = sb("row_f", [P, TWO, CT])
        row_u = sb("row_u", [P, SLOTS // CU, CT], U32)
        m2 = sb("m2", [P, 2, KD, D], F32R)
        kv2 = sb("kv2", [P, TWO, 2, KD, NV], F32R)
        zsum = sb("zsum", [P, SLOTS, UT])
        zinv = sb("zinv", [P, SLOTS, UT])
        pad_u = sb("pad_u", [P, E], U32)
        pad_f = sb("pad_f", [P, E])
        zeros = sb("zeros", [P, D])
        t_ps = ps("t1_ps", [P, KD, UT * P])
        q_ps = ps("q1_ps", [P, KD, UT * P])
        k_ps = ps("k1_ps", [P, UT, 512])
        m_ps = ps("m1_ps", [P, KD, D])
        ks_ps = ps("ks1_ps", [P, 512])
        v_ps = ps("v1_ps", [P, UT, 512])
        count_ps = k_ps[:, 0, NK:NK + (CT + 1) * E]
        g = sems("stats_done halves_met diff_squared var_found var_ready rstd_ready shift_ready xn_ready xn_rounded "
                 "xn_split t_ready t_rounded t_split k_ready k_exp k_capped k_full k_read k_rounded k_split q_ready q_exp "
                 "q_capped q_full q_rounded q_split best_found ties_found ties_ranked lead_found picked counted "
                 "row_based row_masked row_found row_ready row_kept base_moved sums_done m_rounded m_split kv_ready "
                 "kv_rounded kv_split v_ready zsum_ready zinv_ready rows_ready zeroed pads_based pads_ready pads_stored")
        x_loaded = [ctx.enter_context(nc.semaphore(f"xa_loaded{i}")) for i in range(X_SLOTS)]
        scattered = [ctx.enter_context(nc.semaphore(f"scattered{i}")) for i in range(SLOTS)]
        block = ctx.enter_context(nc.Block())
        x_units = z.x.rearrange("b (n u p) d -> (b n) p u d", u=UT, p=P)

        def there(n, least=0):
            return not isinstance(n, int) or least <= n < UNITS

        at = lambda i, ahead: (i + ahead) % SLOTS

        def chunk_counted(n, i, r):
            if (i - COUNT_LAG) % CU == 0 and there(n - COUNT_LAG):
                c = r * (SLOTS // CU) + (i - COUNT_LAG) // CU
                return c, (i - COUNT_LAG) // CU % TWO
            return None

        def row_closed(n, i, r):
            if (i - 1) % ROW == 0 and there(n - ROW - 1):
                return r * TWO + (i - 1) // ROW - 1, ((i - 1) // ROW - 1) % TWO
            return None

        run = lambda eng, first, step, last: pipeline(eng, first, step, last, UNITS, SLOTS)

        @block.sync
        def _(sp):
            def step(n, i, r):
                m = n + 5
                if there(m):
                    if there(m, X_SLOTS):
                        sp.wait_ge(g["xn_ready"], m - X_SLOTS + 1)
                    sp.dma_start(xa[:, at(i, 5) % X_SLOTS], x_units[m]).then_inc(x_loaded[at(i, 5) % X_SLOTS], 16)

            run(sp, -5, step, UNITS - 1)

        @block.tensor
        def _(pe):
            def turn(n, i):
                if there(n):
                    pe.wait_ge(g["xn_ready"], n + 1)
                    if there(n, 1):
                        pe.wait_ge(g["t_split"], n)
                    for k in range(KD):
                        for t in range(UT):
                            m = nc.tensor.transpose(t_ps[:, k, t * P:(t + 1) * P], xn[:, i, t, k * P:(k + 1) * P], z.ident[:])
                    m.then_inc(g["t_ready"], 1)

            def q(n, i, r):
                if there(n):
                    pe.wait_ge(g["t_split"], n + 1)
                    if there(n, 1):
                        pe.wait_ge(g["q_full"], n)
                    closed = row_closed(n - 1, (i - 1) % SLOTS, r if i else r - 1)
                    if closed:
                        pe.wait_ge(g["kv_split"], closed[0] + 1)
                    for j in range(KD):
                        for k in range(KD):
                            m = mm3(nc, q_ps[:, j, :], [z.wq[:, a, k, j * P:(j + 1) * P] for a in range(2)],
                                    [xt2[:, i % TWO, a, k, :] for a in range(2)], j == 0 and k == 0, k == KD - 1, skip_group_check=True)
                    m.then_inc(g["q_ready"], 1)

            def keys(n, i, r):
                if there(n):
                    if there(n, 1):
                        pe.wait_ge(g["k_read"], n)
                    before = chunk_counted(n - 1, (i - 1) % SLOTS, r if i else r - 1)
                    if before:
                        pe.wait_ge(g["base_moved"], before[0] + 1)
                    for t in range(UT):
                        for k in range(KD):
                            m = mm3(nc, k_ps[:, t, 0:NK], [xt2[:, i % TWO, a, k, t * P:(t + 1) * P] for a in range(2)],
                                    [z.wkg[:, a, k, :] for a in range(2)], k == 0, k == KD - 1, skip_group_check=True)
                        if t == 0:
                            count(n, i, r)
                    m.then_inc(g["k_ready"], 1)

            def count(n, i, r):
                counted = chunk_counted(n, i, r)
                if counted:
                    c, s = counted
                    pe.wait_ge(g["picked"], c + 1)
                    flat = pick[:, s].rearrange("p t e -> p (t e)")
                    m = nc.tensor.matmul(count_ps[:, 0:CT * E], z.before[:], flat, start=not there(n), stop=False, skip_group_check=True)
                    for d in range(1, CT):
                        nc.tensor.matmul(count_ps[:, d * E:CT * E], z.ones_b[:], flat[:, 0:(CT - d) * E], start=False, stop=False,
                                         skip_group_check=True)
                    for t in range(CT):
                        m = nc.tensor.matmul(count_ps[:, CT * E:], z.ones_b[:], pick[:, s, t, :], start=False,
                                             stop=(t == CT - 1), skip_group_check=True)
                    m.then_inc(g["counted"], 1)

            def sums(n, i, r):
                if there(n):
                    pe.wait_ge(g["xn_split"], n + 1)
                    pe.wait_ge(g["k_split"], n + 1)
                    first, last = i % ROW == 0, i % ROW == ROW - 1
                    if first and there(n, 1):
                        pe.wait_ge(g["m_split"], (r * TWO + i // ROW) * 2)
                    for t in range(UT):
                        st, en = first and t == 0, last and t == UT - 1
                        kk = [k2[:, i % TWO, a, t, :] for a in range(2)]
                        for j in range(KD):
                            mm3(nc, m_ps[:, j, :], [xn2[:, i % X_SLOTS, a, t, j * P:(j + 1) * P] for a in range(2)], kk,
                                st and j == 0, en, skip_group_check=True)
                        for j in range(KD):
                            for a in range(2):
                                m = nc.tensor.matmul(ks_ps[:, 2 * j:2 * j + 2], kk[a][:, j * P:(j + 1) * P], z.ones_r[:],
                                                     start=st and j == 0 and a == 0, stop=en and a == 1, skip_group_check=True)
                    m.then_inc(g["sums_done"], 1)

            def kv(n, i, r):
                closed = row_closed(n, i, r)
                if closed:
                    b, _ = closed
                    pe.wait_ge(g["m_split"], 2 * b + 2)
                    if there(n):
                        pe.wait_ge(g["q_full"], n + 1)
                    for j in range(KD):
                        for k in range(KD):
                            m = mm3(nc, q_ps[:, j, :], [m2[:, a, k, j * P:(j + 1) * P] for a in range(2)],
                                    [z.wv[:, a, k, :] for a in range(2)], j == 0 and k == 0, k == KD - 1, skip_group_check=True)
                    m.then_inc(g["kv_ready"], 1)

            def values(n, i, r):
                if there(n):
                    if i % ROW == 0:
                        pe.wait_ge(g["kv_split"], r * TWO + i // ROW + 1)
                    pe.wait_ge(g["q_split"], n + 1)
                    if there(n, 1):
                        pe.wait_ge(g["rows_ready"], UT * n)
                    for t in range(UT):
                        for j in range(KD):
                            m = mm3(nc, v_ps[:, t, 0:NV], [qt2[:, i, a, j, t * P:(t + 1) * P] for a in range(2)],
                                    [kv2[:, i // ROW, a, j, :] for a in range(2)], j == 0, j == KD - 1)
                    m.then_inc(g["v_ready"], 1)

            def step(n, i, r):
                turn(n + 1, at(i, 1))
                q(n, i, r)
                keys(n, i, r)
                if not there(n):
                    count(n, i, r)
                sums(n - 1, at(i, -1), r if i else r - 1)
                kv(n, i, r)
                values(n - V_LAG, at(i, -V_LAG), r if i >= V_LAG else r - 1)

            run(pe, -1, step, UNITS - 1 + V_LAG)

        @block.scalar
        def _(act):
            def norm_apply(n, i):
                if there(n):
                    act.wait_ge(g["shift_ready"], n + 1)
                    if there(n, SLOTS):
                        act.wait_ge(scattered[i], (n - i) * (16 * UT // SLOTS))
                    for t in range(UT):
                        m = nc.scalar.activation(xn[:, i, t, :], xa[:, i % X_SLOTS, t, :], ACT.Identity,
                                                 bias=shift[:, i % X_SLOTS, t:t + 1], scale=rstd[:, i % X_SLOTS, t:t + 1])
                    m.then_inc(g["xn_ready"], 1)

            def round_xn(n, i):
                if there(n):
                    act.wait_ge(g["xn_ready"], n + 1)
                    if there(n, X_SLOTS):
                        act.wait_ge(g["sums_done"], n - X_SLOTS + 1)
                    nc.scalar.activation(xn2[:, i % X_SLOTS, 0], xn[:, i], ACT.Copy).then_inc(g["xn_rounded"], 1)

            def round_turned(n, i):
                if there(n):
                    act.wait_ge(g["t_ready"], n + 1)
                    nc.scalar.activation(xt2[:, i % TWO, 0], t_ps[:], ACT.Copy).then_inc(g["t_rounded"], 1)

            def exp_q(n, i):
                if there(n):
                    act.wait_ge(g["q_ready"], n + 1)
                    if there(n, TWO):
                        act.wait_ge(g["q_split"], n - TWO + 1)
                    nc.scalar.activation(qf[:, i % TWO], q_ps[:], ACT.Exp).then_inc(g["q_exp"], 1)

            def exp_keys(n, i):
                if there(n):
                    act.wait_ge(g["k_ready"], n + 1)
                    if there(n, TWO):
                        act.wait_ge(g["k_split"], n - TWO + 1)
                    nc.scalar.activation(kf[:, i % TWO], k_ps[:, :, 0:D], ACT.Exp).then_inc(g["k_exp"], 1)

            def round_q(n, i):
                if there(n):
                    act.wait_ge(g["q_full"], n + 1)
                    nc.scalar.activation(qt2[:, i, 0], qf[:, i % TWO], ACT.Copy).then_inc(g["q_rounded"], 1)

            def round_keys(n, i):
                if there(n):
                    act.wait_ge(g["k_full"], n + 1)
                    if there(n, TWO):
                        act.wait_ge(g["sums_done"], n - TWO + 1)
                    nc.scalar.activation(k2[:, i % TWO, 0], kf[:, i % TWO], ACT.Copy).then_inc(g["k_rounded"], 1)

            def round_sums(n, i, r):
                closed = row_closed(n, i, r)
                if closed:
                    act.wait_ge(g["sums_done"], n - 1)
                    nc.scalar.activation(m2[:, 0], m_ps[:], ACT.Copy).then_inc(g["m_rounded"], 1)
                    nc.scalar.activation(kv2[:, closed[1], 0, :, D:NV], ks_ps[:, 0:2 * KD].rearrange("p (j c) -> p j c", c=2),
                                         ACT.Copy).then_inc(g["m_rounded"], 1)

            def round_kv(n, i, r):
                closed = row_closed(n, i, r)
                if closed:
                    act.wait_ge(g["kv_ready"], closed[0] + 1)
                    nc.scalar.activation(kv2[:, closed[1], 0, :, 0:D], q_ps[:], ACT.Copy).then_inc(g["kv_rounded"], 1)

            def scale_rows(n, i):
                if there(n):
                    act.wait_ge(g["zinv_ready"], n + 1)
                    for t in range(UT):
                        nc.scalar.activation(z.res[:, bass.ds(UT * n + t, 1), :], v_ps[:, t, 0:D].unsqueeze(1), ACT.Copy,
                                             scale=zinv[:, i, t:t + 1]).then_inc(g["rows_ready"], 1)

            def step(n, i, r):
                round_sums(n, i, r)
                round_turned(n + 1, at(i, 1))
                scale_rows(n - V_LAG - 1, at(i, -V_LAG - 1))
                exp_q(n, i)
                norm_apply(n + 2, at(i, 2))
                exp_keys(n, i)
                round_q(n, i)
                round_xn(n + 1, at(i, 1))
                round_keys(n, i)
                round_kv(n, i, r)

            run(act, -2, step, UNITS + V_LAG)

        @block.vector
        def _(dve):
            def norm_stats(n, i):
                if there(n):
                    s = i % X_SLOTS
                    dve.wait_ge(x_loaded[s], (n - s) * (16 // X_SLOTS) + 16)
                    for t in range(UT):
                        nc.vector.bn_stats(stats[:, s, t], xa[:, s, t, :]).then_inc(g["stats_done"], 1)

            def spread(n, i):
                if there(n):
                    s = i % X_SLOTS
                    dve.wait_ge(g["stats_done"], UT * n + UT)
                    nc.vector.tensor_tensor(pair[:, s], stats[:, s, :, 1:3], stats[:, s, :, 4:6], ALU.add).then_inc(g["halves_met"], 1)
                    nc.vector.tensor_tensor(diff[:, s], stats[:, s, :, 1], stats[:, s, :, 4], ALU.subtract).then_inc(g["halves_met"], 1)
                    dve.wait_ge(g["halves_met"], 2 * n + 2)
                    nc.vector.tensor_scalar(neg_mean[:, s], pair[:, s, :, 0], -0.5, None, ALU.mult)
                    nc.vector.scalar_tensor_tensor(diff_sq[:, s], diff[:, s], 0.25, diff[:, s], ALU.mult, ALU.mult).then_inc(g["diff_squared"], 1)
                    dve.wait_ge(g["diff_squared"], n + 1)
                    nc.vector.scalar_tensor_tensor(var[:, s], pair[:, s, :, 1], 1.0 / D, diff_sq[:, s], ALU.mult, ALU.add).then_inc(g["var_found"], 1)
                    dve.wait_ge(g["var_found"], n + 1)
                    nc.vector.tensor_scalar(var_eps[:, s], var[:, s], LN_EPS, None, ALU.add).then_inc(g["var_ready"], 1)

            def split_turned(n, i):
                if there(n):
                    dve.wait_ge(g["t_rounded"], n + 1)
                    nc.vector.tensor_tensor(xt2[:, i % TWO, 1], t_ps[:], xt2[:, i % TWO, 0].bitcast(F32), ALU.subtract).then_inc(g["t_split"], 1)

            def q(n, i):
                if there(n):
                    dve.wait_ge(g["q_exp"], n + 1)
                    f = qf[:, i % TWO]
                    nc.vector.tensor_scalar(f, f, 1.0, None, ALU.min).then_inc(g["q_capped"], 1)
                    dve.wait_ge(g["q_capped"], n + 1)
                    nc.vector.scalar_tensor_tensor(f, q_ps[:], 0.0, f, ALU.max, ALU.add).then_inc(g["q_full"], 1)

            def keys(n, i):
                if there(n):
                    dve.wait_ge(g["k_exp"], n + 1)
                    f = kf[:, i % TWO]
                    nc.vector.tensor_scalar(f, f, 1.0, None, ALU.min).then_inc(g["k_capped"], 1)
                    dve.wait_ge(g["k_capped"], n + 1)
                    nc.vector.scalar_tensor_tensor(f, k_ps[:, :, 0:D], 0.0, f, ALU.max, ALU.add).then_inc(g["k_full"], 1)
                    nc.vector.tensor_copy(logit[:, i // CU % TWO, i % CU * UT:i % CU * UT + UT, :], k_ps[:, :, D:NK]).then_inc(g["k_read"], 1)

            def route(n, i, r):
                if there(n) and i % CU == CU - 1:
                    s, c = i // CU % TWO, r * (SLOTS // CU) + i // CU + 1
                    dve.wait_ge(g["k_read"], n + 1)
                    nc.vector.tensor_reduce(best[:, s], logit[:, s], AX_X, ALU.max).then_inc(g["best_found"], 1)
                    dve.wait_ge(g["best_found"], c)
                    nc.vector.tensor_tensor(tied[:, s], logit[:, s], best[:, s].unsqueeze(2).to_broadcast([P, CT, E]), ALU.is_equal).then_inc(g["ties_found"], 1)
                    dve.wait_ge(g["ties_found"], c)
                    nc.vector.tensor_tensor(tied[:, s], tied[:, s], z.first_rank[:], ALU.mult).then_inc(g["ties_ranked"], 1)
                    dve.wait_ge(g["ties_ranked"], c)
                    nc.vector.tensor_reduce(lead[:, s], tied[:, s], AX_X, ALU.max).then_inc(g["lead_found"], 1)
                    dve.wait_ge(g["lead_found"], c)
                    nc.vector.tensor_tensor(pick[:, s], tied[:, s], lead[:, s].unsqueeze(2).to_broadcast([P, CT, E]), ALU.is_equal).then_inc(g["picked"], 1)
                    dve.wait_ge(g["picked"], c)
                    nc.vector.tensor_copy(z.chosen[:, bass.ds(CT * c - CT, CT), :], pick[:, s])

            def place(n, i, r):
                counted = chunk_counted(n, i, r)
                if counted:
                    c, s = counted
                    dve.wait_ge(g["counted"], c + 1)
                    if not (isinstance(c, int) and c == 0):
                        dve.wait_ge(g["base_moved"], c)
                    nc.vector.tensor_tensor(row[:, s], count_ps[:, 0:CT * E].rearrange("p (t e) -> p t e", e=E),
                                            z.next_row[:].unsqueeze(1).to_broadcast([P, CT, E]), ALU.add).then_inc(g["row_based"], 1)
                    dve.wait_ge(g["row_based"], c + 1)
                    nc.vector.tensor_tensor(z.next_row[:], count_ps[:, CT * E:], z.next_row[:], ALU.add).then_inc(g["base_moved"], 1)
                    nc.vector.tensor_tensor(row[:, s], row[:, s], pick[:, s], ALU.mult).then_inc(g["row_masked"], 1)
                    dve.wait_ge(g["row_masked"], c + 1)
                    nc.vector.tensor_reduce(row_f[:, s], row[:, s], AX_X, ALU.add).then_inc(g["row_found"], 1)
                    dve.wait_ge(g["row_found"], c + 1)
                    nc.vector.tensor_copy(row_u[:, (i - COUNT_LAG) // CU % (SLOTS // CU)], row_f[:, s]).then_inc(g["row_ready"], 1)
                    nc.vector.tensor_copy(z.place[:, bass.ds(CT * c, CT)], row_f[:, s]).then_inc(g["row_kept"], 1)

            def split_sums(n, i, r):
                closed = row_closed(n, i, r)
                if closed:
                    b, s = closed
                    dve.wait_ge(g["m_rounded"], 2 * b + 2)
                    nc.vector.tensor_tensor(m2[:, 1], m_ps[:], m2[:, 0].bitcast(F32), ALU.subtract).then_inc(g["m_split"], 1)
                    nc.vector.tensor_tensor(kv2[:, s, 1, :, D:NV], ks_ps[:, 0:2 * KD].rearrange("p (j c) -> p j c", c=2),
                                            kv2[:, s, 0, :, D:NV].bitcast(F32), ALU.subtract).then_inc(g["m_split"], 1)

            def split_kv(n, i, r):
                closed = row_closed(n, i, r)
                if closed:
                    b, s = closed
                    dve.wait_ge(g["kv_rounded"], b + 1)
                    nc.vector.tensor_tensor(kv2[:, s, 1, :, 0:D], q_ps[:], kv2[:, s, 0, :, 0:D].bitcast(F32), ALU.subtract).then_inc(g["kv_split"], 1)

            def divisors(n, i):
                if there(n):
                    dve.wait_ge(g["v_ready"], n + 1)
                    nc.vector.tensor_scalar(zsum[:, i], v_ps[:, :, D], Z_EPS, 2.0, ALU.add, ALU.mult).then_inc(g["zsum_ready"], 1)
                    dve.wait_ge(g["zsum_ready"], n + 1)
                    nc.vector.reciprocal(zinv[:, i], zsum[:, i]).then_inc(g["zinv_ready"], 1)

            def step(n, i, r):
                divisors(n - V_LAG - 1, at(i, -V_LAG - 1))
                split_sums(n, i, r)
                split_turned(n + 1, at(i, 1))
                norm_stats(n + 3, at(i, 3))
                q(n, i)
                spread(n + 3, at(i, 3))
                keys(n, i)
                place(n, i, r)
                route(n, i, r)
                split_kv(n, i, r)

            run(dve, -3, step, UNITS + V_LAG)
            dve.wait_ge(g["base_moved"], UNITS // CU)
            nc.vector.tensor_scalar(pad_f[:], z.next_row[:], z.row_id[:, 0:1], None, ALU.add).then_inc(g["pads_based"], 1)
            dve.wait_ge(g["pads_based"], 1)
            nc.vector.tensor_copy(pad_u[:], pad_f[:]).then_inc(g["pads_ready"], 1)
            dve.wait_ge(g["row_kept"], UNITS // CU)

        @block.gpsimd
        def _(pool):
            def norm_scale(n, i):
                if there(n):
                    s = i % X_SLOTS
                    pool.wait_ge(g["var_ready"], n + 1)
                    nc.gpsimd.tensor_tensor(rstd[:, s], var_eps[:, s], z.neg_half[:, 0:UT], ALU.pow).then_inc(g["rstd_ready"], 1)
                    pool.wait_ge(g["rstd_ready"], n + 1)
                    nc.gpsimd.tensor_tensor(shift[:, s], neg_mean[:, s], rstd[:, s], ALU.mult).then_inc(g["shift_ready"], 1)

            def split_xn(n, i):
                if there(n):
                    pool.wait_ge(g["xn_rounded"], n + 1)
                    s = i % X_SLOTS
                    nc.gpsimd.tensor_tensor(xn2[:, s, 1], xn[:, i], xn2[:, s, 0].bitcast(F32), ALU.subtract).then_inc(g["xn_split"], 1)

            def split_keys(n, i):
                if there(n):
                    pool.wait_ge(g["k_rounded"], n + 1)
                    nc.gpsimd.tensor_tensor(k2[:, i % TWO, 1], kf[:, i % TWO], k2[:, i % TWO, 0].bitcast(F32), ALU.subtract).then_inc(g["k_split"], 1)

            def split_q(n, i):
                if there(n):
                    pool.wait_ge(g["q_rounded"], n + 1)
                    nc.gpsimd.tensor_tensor(qt2[:, i, 1], qf[:, i % TWO], qt2[:, i, 0].bitcast(F32), ALU.subtract).then_inc(g["q_split"], 1)

            def placed(n, i, r):
                if there(n):
                    pool.wait_ge(g["row_ready"], r * (SLOTS // CU) + i // CU + 1)

            def scatter(n, i):
                if there(n):
                    for t in range(UT):
                        k = i % CU * UT + t
                        nc.gpsimd.indirect_dma_start(
                            out=z.sorted_dram.ap(), out_offset=bass.IndirectOffsetOnAxis(ap=row_u[:, i // CU, k:k + 1], axis=0),
                            in_=xn[:, i, t, :], in_offset=None).then_inc(scattered[i], 16)

            def step(n, i, r):
                norm_scale(n + 2, at(i, 2))
                placed(n - SCATTER_LAG, at(i, -SCATTER_LAG), r if i >= SCATTER_LAG else r - 1)
                split_xn(n, i)
                scatter(n - SCATTER_LAG, at(i, -SCATTER_LAG))
                split_q(n, i)
                split_keys(n, i)

            nc.gpsimd.memset(zeros[:], 0.0).then_inc(g["zeroed"], 1)
            run(pool, -2, step, UNITS - 1 + SCATTER_LAG)
            pool.wait_ge(g["pads_ready"], 1)
            pool.wait_ge(g["zeroed"], 1)
            for e in range(E):
                nc.gpsimd.indirect_dma_start(
                    out=z.sorted_dram.ap(), out_offset=bass.IndirectOffsetOnAxis(ap=pad_u[:, e:e + 1], axis=0),
                    in_=zeros[:], in_offset=None).then_inc(g["pads_stored"], 16)
            for i in range(SLOTS):
                pool.wait_ge(scattered[i], 16 * UT * UNITS // SLOTS)
            pool.wait_ge(g["pads_stored"], 16 * E)


def experts(nc, z, wg, wu, wd):
    KD, D, E, DE, SLOTS = z.KD, z.D, z.E, z.DE, z.SLOTS
    QUAD = 4
    PAIRS = SLOTS // 2
    ROUNDS = PAIRS // QUAD
    BITS = (E - 1).bit_length()
    assert PAIRS == ROUNDS * QUAD and E == 1 << BITS and 2 * QUAD * BITS <= 24
    with ExitStack() as ctx:
        sb, ps, sems = scope(nc, ctx)
        wgu = sb("wgu", [P, KD, E, 2 * DE])
        wdn = sb("wdn", [DE, E, D])
        held = sb("held", [P, E])
        held_i = sb("held_i", [P, E], I32)
        tiles_i = sb("tiles_i", [P, E], I32)
        tiles = sb("tiles", [P, E])
        ends = sb("ends", [P, E])
        starts = sb("starts", [P, E])
        moved = sb("moved", [P, E])
        one_col = sb("one_col", [P, E])
        past = sb("past", [P, SLOTS, E])
        past_end = sb("past_end", [P, SLOTS, E])
        owner = sb("owner", [P, SLOTS])
        start = sb("start", [P, SLOTS])
        within = sb("within", [P, SLOTS])
        real = sb("real", [P, SLOTS])
        row_a = sb("row_a", [P, SLOTS])
        row_b = sb("row_b", [P, SLOTS])
        owner_c = sb("owner_c", [P, SLOTS])
        row_i = sb("row_i", [P, SLOTS], I32)
        shifted = sb("shifted", [P, ROUNDS, 2 * QUAD])
        owners = sb("owners", [P, ROUNDS])
        owners_i = sb("owners_i", [P, ROUNDS], I32)
        shift_all = sb("shift_all", [P, z.TILES, E])
        shift = sb("shift", [P, z.TILES])
        xg = sb("xg", [P, QUAD, 2, D])
        xgt = sb("xgt", [P, QUAD, KD, 2, P])
        gate = sb("gate", [P, 2, 2, DE])
        hid = sb("hid", [P, 2, 2, DE])
        hidt = sb("hidt", [DE, 2, 2, P])
        th = sb("th", [P, 2, 2, D])
        y = sb("y", [P, QUAD, 2, D])
        t_ps = ps("t_ps", [P, 2, KD, 2, P])
        gu_ps = ps("gu_ps", [P, 2, 512])
        ht_ps = ps("ht_ps", [P, 2, 512])
        y_ps = ps("y_ps", [P, 2, 2, D])
        g = sems("weights_loaded step tables_ready t_ready t_copied gu_ready gate_relu squared hid_ready ht_ready ht_copied y_ready y_tanh "
                 "silu_ready")
        loaded = [[ctx.enter_context(nc.semaphore(f"loaded{u}_{i}")) for i in range(QUAD)] for u in range(2)]
        stored = [ctx.enter_context(nc.semaphore(f"stored{i}")) for i in range(QUAD)]
        block = ctx.enter_context(nc.Block())
        y_rows = z.expert_dram.ap().rearrange("(n u p) d -> n p u d", u=2, p=P)

        def load(eng, n, i, u):
            first = eng.value_load(row_i[0:1, bass.ds(n * 2 + u, 1)], min_val=0, max_val=E * z.REGION - P)
            eng.dma_start(xg[:, i, u, :], z.sorted_dram.ap()[bass.ds(first, P), :]).then_inc(loaded[u][i], 16)

        def load_again(eng, n, i, u):
            eng.wait_ge(g["t_ready"], n + i - QUAD + 1)
            load(eng, n + i, i, u)

        def load_first(eng, u):
            for i in range(QUAD):
                load(eng, i, i, u)
            for i in range(QUAD):
                load_again(eng, QUAD, i, u)

        @block.sync
        def _(sp):
            for k in range(KD):
                for half, src in ((0, wg), (1, wu)):
                    sp.dma_start(wgu[:, k, :, half * DE:(half + 1) * DE],
                                 src[:, k * P:(k + 1) * P, :].rearrange("e p d -> p e d")).then_inc(g["weights_loaded"], 16)
            sp.dma_start(wdn[:], wd.rearrange("e d h -> d e h")).then_inc(g["weights_loaded"], 16)
            sp.wait_ge(g["tables_ready"], 1)

            def store(n, i):
                sp.wait_ge(g["silu_ready"], n + i + 1)
                sp.dma_start(y_rows[n + i], y[:, i]).then_inc(stored[i], 16)

            load_first(sp, 0)
            with sp.Fori(0, ROUNDS - 2) as r:
                for i in range(QUAD + 1):
                    if i < QUAD:
                        load_again(sp, r * QUAD + 2 * QUAD, i, 0)
                    if i == QUAD:
                        store(r * QUAD, i - 2)
                        store(r * QUAD, i - 1)
                    elif i >= 2:
                        store(r * QUAD, i - 2)
            for n in range(PAIRS - 2 * QUAD, PAIRS, QUAD):
                for i in range(QUAD):
                    store(n, i)
            for i in range(QUAD):
                sp.wait_ge(stored[i], 16 * ROUNDS)

        @block.gpsimd
        def _(pool):
            pool.wait_ge(g["tables_ready"], 1)
            load_first(pool, 1)
            with pool.Fori(0, ROUNDS - 2) as r:
                for i in range(QUAD):
                    load_again(pool, r * QUAD + 2 * QUAD, i, 1)

        @block.tensor
        def _(pe):
            pe.wait_ge(g["tables_ready"], 1)
            pe.wait_ge(g["weights_loaded"], 16 * (2 * KD + 1))

            def turn(n, i, reused):
                for u in range(2):
                    pe.wait_ge(loaded[u][i], (n - i) * (16 // QUAD) + 16)
                if reused:
                    pe.wait_ge(g["t_copied"], n - 1)
                for k in range(KD):
                    for u in range(2):
                        t = nc.tensor.transpose(t_ps[:, i % 2, k, u, :], xg[:, i, u, k * P:(k + 1) * P], z.ident[:])
                t.then_inc(g["t_ready"], 1)

            def gate_up(n, i, e, reused):
                pe.wait_ge(g["t_copied"], n + 1)
                if reused:
                    pe.wait_ge(g["hid_ready"], n - 1)
                for u in range(2):
                    for k in range(KD):
                        m = nc.tensor.matmul(gu_ps[:, i % 2, u * 2 * DE:(u + 1) * 2 * DE], xgt[:, i, k, u, :],
                                             wgu[:, k, bass.ds(e[i][u], 1), :].rearrange("p a f -> p (a f)"),
                                             start=(u == 0 and k == 0), stop=(k == KD - 1), skip_group_check=True)
                m.then_inc(g["gu_ready"], 1)

            def hidden_ready(n, reused):
                pe.wait_ge(g["hid_ready"], n + 1)
                if reused:
                    pe.wait_ge(g["ht_copied"], n - 1)

            def turn_hidden(n, i):
                for u in range(2):
                    t = nc.tensor.transpose(ht_ps[0:DE, i % 2, u * P:(u + 1) * P], hid[:, i % 2, u, :], z.ident[:])
                t.then_inc(g["ht_ready"], 1)

            def down(n, i, e, reused):
                pe.wait_ge(g["ht_copied"], n + 1)
                if reused:
                    pe.wait_ge(g["silu_ready"], n - 1)
                for u in range(2):
                    m = nc.tensor.matmul(y_ps[:, i % 2, u, :], hidt[:, i % 2, u, :],
                                         wdn[:, bass.ds(e[i][u], 1), :].rearrange("p a h -> p (a h)"),
                                         start=(u == 0), stop=True, skip_group_check=True)
                m.then_inc(g["y_ready"], 1)

            def four_pairs(r, first, last):
                n = r * QUAD
                owners = pe.value_load(owners_i[0:1, bass.ds(r, 1)], min_val=0, max_val=E ** (2 * QUAD) - 1)
                e = [[(owners >> (BITS * (2 * i + u))) & (E - 1) for u in range(2)] for i in range(QUAD)]
                up = lambda i: gate_up(n + i, i, e, not first or i >= 2)
                dn = lambda i: down(n + i, i, e, not first or i >= 2)

                def turns(i):
                    hidden_ready(n + i, not first or i >= 2)
                    if not last:
                        turn(n + QUAD + i, i, True)
                    turn_hidden(n + i, i)

                up(0)
                up(1)
                turns(0)
                up(2)
                turns(1)
                dn(0)
                up(3)
                turns(2)
                dn(1)
                turns(3)
                dn(2)
                dn(3)

            for i in range(QUAD):
                turn(i, i, i >= 2)
            four_pairs(0, True, False)
            with pe.Fori(1, ROUNDS - 1) as r:
                four_pairs(r, False, False)
            four_pairs(ROUNDS - 1, False, True)

        @block.scalar
        def _(act):
            def copy_turned(n, i, reused):
                act.wait_ge(g["t_ready"], n + 1)
                if reused:
                    act.wait_ge(g["gu_ready"], n - QUAD + 1)
                nc.scalar.activation(xgt[:, i], t_ps[:, i % 2], ACT.Copy).then_inc(g["t_copied"], 1)

            def relu(n, i):
                act.wait_ge(g["gu_ready"], n + 1)
                o = gu_ps[:, i % 2, 0:4 * DE].rearrange("p (u f) -> p u f", u=2)
                nc.scalar.activation(gate[:, i % 2], o[:, :, 0:DE], ACT.Relu).then_inc(g["gate_relu"], 1)

            def copy_hidden(n, i):
                act.wait_ge(g["ht_ready"], n + 1)
                nc.scalar.activation(hidt[:, i % 2], ht_ps[0:DE, i % 2, 0:2 * P].rearrange("p (u t) -> p u t", u=2), ACT.Copy).then_inc(g["ht_copied"], 1)

            def tanh(n, i):
                act.wait_ge(g["y_ready"], n + 1)
                nc.scalar.activation(th[:, i % 2], y_ps[:, i % 2], ACT.Tanh, scale=0.5).then_inc(g["y_tanh"], 1)

            def four_pairs(n, last):
                def turns(i):
                    if not last:
                        copy_turned(n + QUAD + i, i, True)
                    copy_hidden(n + i, i)

                relu(n, 0)
                relu(n + 1, 1)
                turns(0)
                relu(n + 2, 2)
                turns(1)
                tanh(n, 0)
                relu(n + 3, 3)
                turns(2)
                tanh(n + 1, 1)
                turns(3)
                tanh(n + 2, 2)
                tanh(n + 3, 3)

            for i in range(QUAD):
                copy_turned(i, i, False)
            with act.Fori(0, ROUNDS - 1) as r:
                four_pairs(r * QUAD, False)
            four_pairs(PAIRS - QUAD, True)

        @block.vector
        def _(dve):
            count = 0

            def link(ins):
                nonlocal count
                count += 1
                ins.then_inc(g["step"], 1)
                dve.wait_ge(g["step"], count)

            link(nc.vector.tensor_tensor(held[:], z.next_row[:], z.region0[:], ALU.subtract))
            link(nc.vector.tensor_scalar(held[:], held[:], float(P - 1), None, ALU.add))
            link(nc.vector.tensor_copy(held_i[:], held[:]))
            link(nc.vector.tensor_scalar(tiles_i[:], held_i[:], P.bit_length() - 1, None, ALU.arith_shift_right))
            link(nc.vector.tensor_copy(tiles[:], tiles_i[:]))
            link(nc.vector.memset(one_col[:], 1.0))
            link(nc.vector.tensor_tensor_scan(ends[:], one_col[:], tiles[:], 0.0, ALU.mult, ALU.add))
            link(nc.vector.tensor_tensor(starts[:], ends[:], tiles[:], ALU.subtract))
            shape = [P, SLOTS, E]
            link(nc.vector.tensor_tensor(past[:], ends[:].unsqueeze(1).to_broadcast(shape), z.slot_id[:].unsqueeze(2).to_broadcast(shape), ALU.is_le))
            link(nc.vector.tensor_reduce(owner[:], past[:], AX_X, ALU.add))
            link(nc.vector.tensor_tensor(past_end[:], past[:], ends[:].unsqueeze(1).to_broadcast(shape), ALU.mult))
            link(nc.vector.tensor_reduce(start[:], past_end[:], AX_X, ALU.max))
            link(nc.vector.tensor_tensor(within[:], z.slot_id[:], start[:], ALU.subtract))
            link(nc.vector.tensor_scalar(real[:], owner[:], float(E), None, ALU.is_lt))
            link(nc.vector.tensor_scalar(row_a[:], owner[:], float(z.REGION), float(-(E - 1) * z.REGION), ALU.mult, ALU.add))
            link(nc.vector.scalar_tensor_tensor(row_b[:], within[:], float(P), row_a[:], ALU.mult, ALU.add))
            link(nc.vector.tensor_tensor(row_b[:], row_b[:], real[:], ALU.mult))
            link(nc.vector.tensor_scalar(row_b[:], row_b[:], float((E - 1) * z.REGION), None, ALU.add))
            link(nc.vector.tensor_scalar(owner_c[:], owner[:], float(E - 1), None, ALU.min))
            link(nc.vector.tensor_copy(row_i[:], row_b[:]))
            for i in range(2 * QUAD):
                link(nc.vector.tensor_scalar(shifted[:, :, i], owner_c[:].rearrange("p (r i) -> p r i", i=2 * QUAD)[:, :, i], float(E ** i), None, ALU.mult))
            link(nc.vector.tensor_reduce(owners[:], shifted[:], AX_X, ALU.add))
            nc.vector.tensor_copy(owners_i[:], owners[:]).then_inc(g["tables_ready"], 1)
            link(nc.vector.scalar_tensor_tensor(moved[:], starts[:], float(P), z.region0[:], ALU.mult, ALU.subtract))
            link(nc.vector.tensor_tensor(shift_all[:], z.chosen[:], moved[:].unsqueeze(1).to_broadcast([P, z.TILES, E]), ALU.mult))
            link(nc.vector.tensor_reduce(shift[:], shift_all[:], AX_X, ALU.add))
            link(nc.vector.tensor_tensor(z.place[:, 0:z.TILES], z.place[:, 0:z.TILES], shift[:], ALU.add))

            def hidden(n, i):
                dve.wait_ge(g["gate_relu"], n + 1)
                o = gu_ps[:, i % 2, 0:4 * DE].rearrange("p (u f) -> p u f", u=2)
                nc.vector.scalar_tensor_tensor(hid[:, i % 2], o[:, :, 0:DE], 0.0, gate[:, i % 2], ALU.max, ALU.mult).then_inc(g["squared"], 1)
                dve.wait_ge(g["squared"], n + 1)
                nc.vector.tensor_tensor(hid[:, i % 2], o[:, :, DE:2 * DE], hid[:, i % 2], ALU.mult).then_inc(g["hid_ready"], 1)

            def silu(n, i, reused):
                dve.wait_ge(g["y_tanh"], n + 1)
                if reused:
                    dve.wait_ge(stored[i], (n - i) * (16 // QUAD))
                nc.vector.scalar_tensor_tensor(y[:, i], th[:, i % 2], 1.0, y_ps[:, i % 2], ALU.add, ALU.mult).then_inc(g["silu_ready"], 1)

            def four_pairs(n, reused):
                hidden(n, 0)
                hidden(n + 1, 1)
                hidden(n + 2, 2)
                silu(n, 0, reused)
                hidden(n + 3, 3)
                for i in range(1, QUAD):
                    silu(n + i, i, reused)

            four_pairs(0, False)
            with dve.Fori(1, ROUNDS) as r:
                four_pairs(r * QUAD, True)


def second_layer(nc, z):
    B, KD, D = z.B, z.KD, z.D
    SCALE = float(D) ** -0.5
    UT = 2
    UNITS = z.TILES // UT
    SLOTS = 4
    assert UNITS % SLOTS == 0 and UT * D <= 512
    with ExitStack() as ctx:
        sb, ps, sems = scope(nc, ctx)
        xin = sb("xin", [P, SLOTS, UT, D])
        moe = sb("moe", [P, SLOTS, UT, D])
        gather_u = sb("gather_u", [P, SLOTS, UT], U32)
        stats = sb("stats2", [P, SLOTS, UT, 6])
        pair = sb("pair2", [P, SLOTS, UT, 2])
        diff = sb("diff2", [P, SLOTS, UT])
        diff_sq = sb("diff_sq2", [P, SLOTS, UT])
        neg_mean = sb("neg_mean", [P, SLOTS, UT])
        var = sb("var2", [P, SLOTS, UT])
        var_eps = sb("var_eps2", [P, SLOTS, UT])
        rstd = sb("rstd2", [P, SLOTS, UT])
        shift = sb("shift2", [P, SLOTS, UT])
        var_n = sb("var_n", [P, SLOTS, UT])
        var_n2 = sb("var_n2", [P, SLOTS, UT])
        var_n_eps = sb("var_n_eps", [P, SLOTS, UT])
        rstd_n = sb("rstd_n", [P, SLOTS, UT])
        xn = sb("xn2nd", [P, SLOTS, UT, D])
        xt = sb("xt", [P, 2, KD, UT * P])
        qt = sb("qt", [P, 2, KD, UT * P])
        vo = sb("vo", [P, 2, UT, D])
        top = sb("top", [P, SLOTS, UT])
        ntop = sb("ntop", [P, SLOTS, UT])
        pr = sb("pr", [P, 2, UT, P])
        total = sb("total", [P, SLOTS, UT])
        total_eps = sb("total_eps", [P, SLOTS, UT])
        inv = sb("inv", [P, SLOTS, UT])
        prt = sb("prt", [P, 2, UT, P])
        zg = sb("zg", [P, SLOTS, UT, D])
        th = sb("th2", [P, SLOTS, UT, D])
        att = sb("att", [P, SLOTS, UT, D])
        t_ps = ps("t2_ps", [P, KD, UT * P])
        q_ps = ps("q_ps", [P, KD, UT * P])
        v_ps = ps("v_ps", [P, UT, D])
        s_ps = ps("s_ps", [P, 4, P])
        pt_ps = ps("pt_ps", [P, 4, P])
        a_ps = ps("a_ps", [P, UT, D])
        g = sems("index_ready moe_scaled x1_ready stats_done halves_met diff_squared var_ready eps_added rstd_ready "
                 "shift_ready var_scaled var_scaled2 neps_added nrstd_ready xn_ready t_ready t_copied q_ready q_copied "
                 "v_ready v_copied s_ready top_found top_ready p_ready pt_ready pt_copied att_ready z_scaled z_ready "
                 "z_tanh gate_ready total_based inv_ready att_scaled gated out_ready")
        per_slot = lambda name: [ctx.enter_context(nc.semaphore(f"{name}{i}")) for i in range(SLOTS)]
        x_loaded, moe_loaded, out_stored = per_slot("x_loaded"), per_slot("moe_loaded"), per_slot("out_stored")
        block = ctx.enter_context(nc.Block())
        x_units = z.x.rearrange("b (n u p) d -> (b n) p u d", u=UT, p=P)
        out_units = z.out.rearrange("b (n u p) d -> (b n) p u d", u=UT, p=P)
        tiles = lambda n: z.res[:, bass.ds(UT * n, UT), :]

        def there(n, least=0):
            return not isinstance(n, int) or least <= n < UNITS

        run = lambda eng, first, step, last: pipeline(eng, first, step, last, UNITS, SLOTS)
        at = lambda i, ahead: (i + ahead) % SLOTS
        turns = lambda n, i, k: (n - i) * (k // SLOTS)

        @block.sync
        def _(sp):
            def load(n, i):
                if there(n):
                    if there(n, SLOTS):
                        sp.wait_ge(g["x1_ready"], n - SLOTS + 1)
                    sp.dma_start(xin[:, i], x_units[n]).then_inc(x_loaded[i], 16)

            def store(n, i):
                if there(n):
                    sp.wait_ge(g["out_ready"], n + 1)
                    sp.dma_start(out_units[n], att[:, i]).then_inc(out_stored[i], 16)

            def step(n, i, _):
                load(n + 4, i)
                store(n - 2, at(i, -2))

            run(sp, -4, step, UNITS + 1)
            for i in range(SLOTS):
                sp.wait_ge(out_stored[i], 16 * UNITS // SLOTS)

        @block.tensor
        def _(pe):
            def q(n, i):
                if there(n):
                    pe.wait_ge(g["t_copied"], n + 1)
                    if there(n, 1):
                        pe.wait_ge(g["q_copied"], n)
                    for j in range(KD):
                        for k in range(KD):
                            m = nc.tensor.matmul(q_ps[:, j, :], z.wqk[:, k, j * P:(j + 1) * P], xt[:, i % 2, k, :],
                                                 start=(j == 0 and k == 0), stop=(k == KD - 1), skip_group_check=True)
                    m.then_inc(g["q_ready"], 1)

            def turn(n, i):
                if there(n):
                    pe.wait_ge(g["xn_ready"], n + 1)
                    if there(n, 1):
                        pe.wait_ge(g["t_copied"], n)
                    for k in range(KD):
                        for t in range(UT):
                            m = nc.tensor.transpose(t_ps[:, k, t * P:(t + 1) * P], xn[:, i, t, k * P:(k + 1) * P], z.ident[:])
                    m.then_inc(g["t_ready"], 1)

            def v(n, i):
                if there(n):
                    if there(n, 1):
                        pe.wait_ge(g["v_copied"], n)
                    for t in range(UT):
                        for k in range(KD):
                            m = nc.tensor.matmul(v_ps[:, t, :], xt[:, i % 2, k, t * P:(t + 1) * P], z.wvo[:, k, :],
                                                 start=(t == 0 and k == 0), stop=(k == KD - 1), skip_group_check=True)
                    m.then_inc(g["v_ready"], 1)

            def turn_probs(n, i):
                if there(n):
                    pe.wait_ge(g["p_ready"], UT * n + UT)
                    if there(n, 1):
                        pe.wait_ge(g["pt_copied"], n)
                    for t in range(UT):
                        m = nc.tensor.transpose(pt_ps[:, t, :], pr[:, i % 2, t, :], z.ident[:])
                    m.then_inc(g["pt_ready"], 1)

            def scores(n, i):
                if there(n):
                    pe.wait_ge(g["q_copied"], n + 1)
                    for t in range(UT):
                        for j in range(KD):
                            nc.tensor.matmul(s_ps[:, t, :], qt[:, i % 2, j, t * P:(t + 1) * P], xt[:, i % 2, j, t * P:(t + 1) * P],
                                             start=(t == 0 and j == 0), stop=False, skip_group_check=True)
                        m = nc.tensor.matmul(s_ps[:, t, :], z.ident_b[:], z.causal[:], start=False, stop=True, skip_group_check=True)
                    m.then_inc(g["s_ready"], 1)

            def attend(n, i):
                if there(n):
                    pe.wait_ge(g["pt_copied"], n + 1)
                    pe.wait_ge(g["v_copied"], n + 1)
                    if there(n, 1):
                        pe.wait_ge(g["att_scaled"], UT * n)
                    for t in range(UT):
                        m = nc.tensor.matmul(a_ps[:, t, :], prt[:, i % 2, t, :], vo[:, i % 2, t, :], start=(t == 0), stop=True,
                                             skip_group_check=True)
                    m.then_inc(g["att_ready"], 1)

            def step(n, i, _):
                q(n, i)
                turn(n + 1, at(i, 1))
                v(n, i)
                turn_probs(n - 1, at(i, -1))
                scores(n, i)
                attend(n - 1, at(i, -1))

            run(pe, -1, step, UNITS)

        @block.scalar
        def _(act):
            def copy_q(n, i):
                if there(n):
                    act.wait_ge(g["q_ready"], n + 1)
                    nc.scalar.activation(qt[:, i % 2], q_ps[:], ACT.Copy).then_inc(g["q_copied"], 1)

            def copy_turned(n, i):
                if there(n):
                    act.wait_ge(g["t_ready"], n + 1)
                    if there(n, 2):
                        act.wait_ge(g["s_ready"], n - 1)
                    nc.scalar.activation(xt[:, i % 2], t_ps[:], ACT.Copy).then_inc(g["t_copied"], 1)

            def copy_probs(n, i):
                if there(n):
                    act.wait_ge(g["pt_ready"], n + 1)
                    if there(n, 2):
                        act.wait_ge(g["att_ready"], n - 1)
                    nc.scalar.activation(prt[:, i % 2], pt_ps[:, 0:UT], ACT.Copy).then_inc(g["pt_copied"], 1)

            def copy_v(n, i):
                if there(n):
                    act.wait_ge(g["v_ready"], n + 1)
                    if there(n, 2):
                        act.wait_ge(g["att_ready"], n - 1)
                    nc.scalar.activation(vo[:, i % 2], v_ps[:], ACT.Copy).then_inc(g["v_copied"], 1)

            def norm_apply(n, i):
                if there(n):
                    act.wait_ge(g["shift_ready"], n + 1)
                    if there(n, SLOTS):
                        act.wait_ge(g["z_scaled"], n - SLOTS + 1)
                    for t in range(UT):
                        m = nc.scalar.activation(xn[:, i, t, :].unsqueeze(1), z.res[:, bass.ds(UT * n + t, 1), :], ACT.Identity,
                                                 bias=shift[:, i, t:t + 1], scale=rstd[:, i, t:t + 1])
                    m.then_inc(g["xn_ready"], 1)

            def tanh(n, i):
                if there(n):
                    act.wait_ge(g["z_ready"], n + 1)
                    nc.scalar.activation(th[:, i], zg[:, i], ACT.Tanh).then_inc(g["z_tanh"], 1)

            def exp(n, i):
                if there(n):
                    act.wait_ge(g["top_ready"], n + 1)
                    for t in range(UT):
                        nc.scalar.activation(pr[:, i % 2, t, :], s_ps[:, t, :], ACT.Exp, bias=ntop[:, i, t:t + 1], scale=SCALE,
                                             accum_out=total[:, i, t:t + 1]).then_inc(g["p_ready"], 1)

            def step(n, i, _):
                copy_q(n, i)
                copy_turned(n + 1, at(i, 1))
                copy_probs(n - 1, at(i, -1))
                copy_v(n, i)
                norm_apply(n + 2, at(i, 2))
                tanh(n, i)
                exp(n, i)

            run(act, -2, step, UNITS)

        @block.vector
        def _(dve):
            def index(n, i):
                nc.vector.tensor_copy(gather_u[:, i], z.place[:, bass.ds(UT * n, UT)]).then_inc(g["index_ready"], 1)

            def gate(n, i):
                if there(n):
                    dve.wait_ge(g["z_tanh"], n + 1)
                    nc.vector.scalar_tensor_tensor(zg[:, i], th[:, i], 1.0, zg[:, i], ALU.add, ALU.mult).then_inc(g["gate_ready"], 1)

            def first_result(n, i):
                if there(n):
                    dve.wait_ge(moe_loaded[i], turns(n, i, 16 * UT) + 16 * UT)
                    nc.vector.tensor_tensor(moe[:, i], moe[:, i], tiles(n), ALU.mult).then_inc(g["moe_scaled"], 1)
                    dve.wait_ge(x_loaded[i], turns(n, i, 16) + 16)
                    dve.wait_ge(g["moe_scaled"], n + 1)
                    nc.vector.tensor_tensor(tiles(n), moe[:, i], xin[:, i], ALU.add).then_inc(g["x1_ready"], 1)
                    dve.wait_ge(g["x1_ready"], n + 1)
                    if there(n + 2, SLOTS):
                        index(n + 2, at(i, 2))
                    for t in range(UT):
                        nc.vector.bn_stats(stats[:, i, t], z.res[:, bass.ds(UT * n + t, 1), :]).then_inc(g["stats_done"], 1)

            def spread(n, i):
                if there(n):
                    dve.wait_ge(g["stats_done"], UT * n + UT)
                    nc.vector.tensor_tensor(pair[:, i], stats[:, i, :, 1:3], stats[:, i, :, 4:6], ALU.add).then_inc(g["halves_met"], 1)
                    nc.vector.tensor_tensor(diff[:, i], stats[:, i, :, 1], stats[:, i, :, 4], ALU.subtract).then_inc(g["halves_met"], 1)
                    dve.wait_ge(g["halves_met"], 2 * n + 2)
                    nc.vector.tensor_scalar(neg_mean[:, i], pair[:, i, :, 0], -0.5, None, ALU.mult)
                    nc.vector.scalar_tensor_tensor(diff_sq[:, i], diff[:, i], 0.25, diff[:, i], ALU.mult, ALU.mult).then_inc(g["diff_squared"], 1)
                    dve.wait_ge(g["diff_squared"], n + 1)
                    nc.vector.scalar_tensor_tensor(var[:, i], pair[:, i, :, 1], 1.0 / D, diff_sq[:, i], ALU.mult, ALU.add).then_inc(g["var_ready"], 1)

            def scale_gate(n, i):
                if there(n):
                    dve.wait_ge(g["nrstd_ready"], n + 1)
                    dve.wait_ge(g["xn_ready"], n + 1)
                    if there(n, SLOTS):
                        dve.wait_ge(g["gated"], n - SLOTS + 1)
                    for t in range(UT):
                        m = nc.vector.scalar_tensor_tensor(zg[:, i, t, :], xn[:, i, t, :], rstd_n[:, i, t:t + 1], z.lng_half[:], ALU.mult, ALU.mult)
                    m.then_inc(g["z_scaled"], 1)

            def maximum(n, i):
                if there(n):
                    dve.wait_ge(g["s_ready"], n + 1)
                    nc.vector.tensor_reduce(top[:, i], s_ps[:, 0:UT], AX_X, ALU.max).then_inc(g["top_found"], 1)
                    dve.wait_ge(g["top_found"], n + 1)
                    nc.vector.tensor_scalar(ntop[:, i], top[:, i], -SCALE, None, ALU.mult).then_inc(g["top_ready"], 1)

            def divisor(n, i):
                if there(n):
                    dve.wait_ge(g["p_ready"], UT * n + UT)
                    nc.vector.tensor_scalar(total_eps[:, i], total[:, i], Z_EPS, None, ALU.add).then_inc(g["total_based"], 1)
                    dve.wait_ge(g["total_based"], n + 1)
                    nc.vector.reciprocal(inv[:, i], total_eps[:, i]).then_inc(g["inv_ready"], 1)

            def attend(n, i):
                if there(n):
                    dve.wait_ge(g["inv_ready"], n + 1)
                    dve.wait_ge(g["att_ready"], n + 1)
                    if there(n, SLOTS):
                        dve.wait_ge(out_stored[i], turns(n, i, 16))
                    for t in range(UT):
                        nc.vector.scalar_tensor_tensor(att[:, i, t, :], a_ps[:, t, :], inv[:, i, t:t + 1], z.bout[:], ALU.mult, ALU.add).then_inc(g["att_scaled"], 1)
                    dve.wait_ge(g["att_scaled"], UT * n + UT)
                    dve.wait_ge(g["gate_ready"], n + 1)
                    nc.vector.tensor_tensor(att[:, i], att[:, i], zg[:, i], ALU.mult).then_inc(g["gated"], 1)

            def step(n, i, _):
                gate(n - 1, at(i, -1))
                first_result(n + 3, at(i, 3))
                divisor(n - 1, at(i, -1))
                spread(n + 3, at(i, 3))
                scale_gate(n + 1, at(i, 1))
                maximum(n, i)
                attend(n - 1, at(i, -1))

            for n in range(SLOTS):
                index(n, n)
            run(dve, -3, step, UNITS)

        @block.gpsimd
        def _(pool):
            def indexed(n, i):
                if there(n):
                    pool.wait_ge(g["index_ready"], n + 1)

            def gather(n, i):
                if there(n):
                    for t in range(UT):
                        nc.gpsimd.indirect_dma_start(
                            out=moe[:, i, t, :], out_offset=None, in_=z.expert_dram.ap(),
                            in_offset=bass.IndirectOffsetOnAxis(ap=gather_u[:, i, t:t + 1], axis=0)).then_inc(moe_loaded[i], 16)

            def norm_scale(n, i):
                if there(n):
                    eps, power = z.eps[:, 0:UT], z.neg_half[:, 0:UT]
                    pool.wait_ge(g["var_ready"], n + 1)
                    nc.gpsimd.tensor_tensor(var_eps[:, i], var[:, i], eps, ALU.add).then_inc(g["eps_added"], 1)
                    pool.wait_ge(g["eps_added"], n + 1)
                    nc.gpsimd.tensor_tensor(rstd[:, i], var_eps[:, i], power, ALU.pow).then_inc(g["rstd_ready"], 1)
                    pool.wait_ge(g["rstd_ready"], n + 1)
                    nc.gpsimd.tensor_tensor(shift[:, i], neg_mean[:, i], rstd[:, i], ALU.mult).then_inc(g["shift_ready"], 1)
                    nc.gpsimd.tensor_tensor(var_n[:, i], var[:, i], rstd[:, i], ALU.mult).then_inc(g["var_scaled"], 1)
                    pool.wait_ge(g["var_scaled"], n + 1)
                    nc.gpsimd.tensor_tensor(var_n2[:, i], var_n[:, i], rstd[:, i], ALU.mult).then_inc(g["var_scaled2"], 1)
                    pool.wait_ge(g["var_scaled2"], n + 1)
                    nc.gpsimd.tensor_tensor(var_n_eps[:, i], var_n2[:, i], eps, ALU.add).then_inc(g["neps_added"], 1)
                    pool.wait_ge(g["neps_added"], n + 1)
                    nc.gpsimd.tensor_tensor(rstd_n[:, i], var_n_eps[:, i], power, ALU.pow).then_inc(g["nrstd_ready"], 1)

            def shift_gate(n, i):
                if there(n):
                    pool.wait_ge(g["z_scaled"], n + 1)
                    nc.gpsimd.tensor_tensor(zg[:, i], zg[:, i], z.lnb_half[:].unsqueeze(1).to_broadcast([P, UT, D]), ALU.add).then_inc(g["z_ready"], 1)

            def result(n, i):
                if there(n):
                    pool.wait_ge(g["gated"], n + 1)
                    nc.gpsimd.tensor_tensor(att[:, i], att[:, i], tiles(n), ALU.add).then_inc(g["out_ready"], 1)

            def step(n, i, _):
                indexed(n + 4, i)
                norm_scale(n + 2, at(i, 2))
                shift_gate(n, i)
                gather(n + 4, i)
                result(n - 2, at(i, -2))

            run(pool, -4, step, UNITS + 1)


_INS = ["L0_attn_x", "L0_attn_W", "L0_ffn_gate_w", "L0_ffn_wg", "L0_ffn_wu", "L0_ffn_wd", "L1_attn_W_qkv", "L1_attn_W_out",
        "L1_attn_b_out", "L1_ffn_ln_g", "L1_ffn_ln_b"]


def kernel(**inputs):
    import numpy as np
    import concourse.bacc as bacc
    from concourse.bass_utils import run_bass_kernel_spmd

    nc = bacc.Bacc("TRN2", target_bir_lowering=False, num_devices=1)
    arrays, args = {}, []
    for name in _INS:
        a = np.ascontiguousarray(inputs[name])
        arrays[f"in_{name}"] = a
        args.append(nc.dram_tensor(f"in_{name}", a.shape, mybir.dt.from_np(a.dtype), kind="ExternalInput").ap())
    x = arrays["in_L0_attn_x"]
    out = nc.dram_tensor("out_rows", x.shape, mybir.dt.from_np(x.dtype), kind="ExternalOutput").ap()
    program(nc, *args, out)
    result = run_bass_kernel_spmd(nc, [arrays], core_ids=[0])
    return result.results[0]["out_rows"]
```

```python
from contextlib import ExitStack

import concourse.bass as bass
from concourse import mybir

F32 = mybir.dt.float32
F32R = mybir.dt.float32r
BF16 = mybir.dt.bfloat16
I32 = mybir.dt.int32
U32 = mybir.dt.uint32
ALU = mybir.AluOpType
ACT = mybir.ActivationFunctionType
AX_X = mybir.AxisListType.X

P = 128
CT = 4
CHUNK = CT * P
CPB = 2
LN_EPS = 1e-5
Z_EPS = 1e-6
MASKED = 3.0e38


class Names:
    pass


def program(nc, x, W, gate_w, wg, wu, wd, W_qkv, W_out, b_out, ln_g, ln_b, out):
    z = Names()
    z.B, z.L, z.D = x.shape
    z.E, _, z.DE = wg.shape
    z.KD = z.D // P
    z.NK = z.D + z.E
    z.NV = z.D + 2
    z.TILES = z.B * z.L // P
    z.REGION = z.B * z.L + P
    z.SLOTS = z.TILES + z.E
    assert z.L == CPB * CHUNK and z.D == z.KD * P and z.SLOTS % 2 == 0 and z.KD == 2
    z.x, z.out = x, out
    z.sorted_dram = nc.dram_tensor("sorted_rows", (z.E * z.REGION, z.D), F32)
    z.expert_dram = nc.dram_tensor("expert_rows", (z.SLOTS * P, z.D), F32)

    with ExitStack() as whole:
        def sb(name, shape, dt=F32):
            return whole.enter_context(nc.sbuf_tensor(name, shape, dt))

        z.wq = sb("wq", [P, 2, z.KD, z.D], F32R)
        z.wkg = sb("wkg", [P, 2, z.KD, z.NK], F32R)
        z.wv = sb("wv", [P, 2, z.KD, z.D], F32R)
        z.ident = sb("ident", [P, P])
        z.ones = sb("ones", [P, 2])
        z.ones_b = sb("ones_b", [P, P], BF16)
        z.before = sb("before", [P, P], BF16)
        z.ident_b = sb("ident_b", [P, P], BF16)
        z.causal = sb("causal", [P, P], BF16)
        z.first_rank = sb("first_rank", [P, CT, z.E])
        z.region0 = sb("region0", [P, z.E])
        z.slot_id = sb("slot_id", [P, z.SLOTS])
        z.neg_half = sb("neg_half", [P, CPB * CT])
        z.res = sb("res", [P, z.TILES, z.D])
        z.chosen = sb("chosen", [P, z.TILES, z.E], BF16)
        z.place = sb("place", [P, z.TILES + CPB * CT])
        z.next_row = sb("next_row", [P, z.E])
        z.wgu = sb("wgu", [P, z.KD, z.E, 2 * z.DE])
        z.wdn = sb("wdn", [P, z.E, z.D])
        z.row_i = sb("row_i", [P, z.SLOTS], I32)
        z.owners_i = sb("owners_i", [P, z.SLOTS], I32)
        z.moved = sb("moved", [P, z.E])
        first_layer(nc, z, W, gate_w, wg, wu, wd)
        z.w2 = sb("w2", [P, z.KD, 3 * z.D])
        z.wo = sb("wo", [P, z.KD, z.D])
        z.bout = sb("bout", [P, z.D])
        z.lng = sb("lng", [P, z.D])
        z.lnb = sb("lnb", [P, z.D])
        experts(nc, z, W_qkv, W_out, b_out, ln_g, ln_b)
        second_layer(nc, z)


def scope(nc, ctx):
    def sb(name, shape, dt=F32):
        return ctx.enter_context(nc.sbuf_tensor(name, shape, dt))

    def ps(name, shape):
        return ctx.enter_context(nc.psum_tensor(name, shape, F32))

    def sems(names):
        return {n: ctx.enter_context(nc.semaphore(n)) for n in names.split()}

    return sb, ps, sems


def pipeline(eng, first, step, last, units, slots):
    for n in range(first, slots):
        step(n, n % slots, n // slots)
    with eng.Fori(1, units // slots - 1) as r:
        for i in range(slots):
            step(r * slots + i, i, r)
    for n in range(units - slots, last + 1):
        step(n, n % slots, n // slots)


def mm3(nc, out, lhs, rhs, first, last, **kw):
    nc.tensor.matmul(out, lhs[0], rhs[0], start=first, stop=False, **kw)
    nc.tensor.matmul(out, lhs[0], rhs[1], start=False, stop=False, **kw)
    return nc.tensor.matmul(out, lhs[1], rhs[0], start=False, stop=last, **kw)


def first_layer(nc, z, W, gate_w, wg, wu, wd):
    KD, D, E, NK, NV = z.KD, z.D, z.E, z.NK, z.NV
    UT = 2
    UNITS = z.TILES // UT
    ROW = z.L // (UT * P)
    SLOTS = 2 * ROW
    CU = CT // UT
    X_SLOTS, TWO = 4, 2
    V_LAG = ROW + 2
    COUNT_LAG = CU + 1
    SCATTER_LAG = COUNT_LAG + 1
    assert UNITS % SLOTS == 0 and CU == 2 and UT * D <= 512 and NK + (CT + 1) * E <= 512
    with ExitStack() as ctx:
        sb, ps, sems = scope(nc, ctx)
        w_s = sb("w_s", [P, KD, 3 * D])
        ids = sb("ids", [P, z.SLOTS], I32)
        held = sb("held", [P, E])
        held_i = sb("held_i", [P, E], I32)
        tiles_i = sb("tiles_i", [P, E], I32)
        tiles = sb("tiles", [P, E])
        ends = sb("ends", [P, E])
        change = sb("change", [P, E])
        one_col = sb("one_col", [P, E])
        owner = sb("owner", [P, z.SLOTS])
        offset = sb("offset", [P, z.SLOTS])
        real = sb("real", [P, z.SLOTS])
        first_row = sb("first_row", [P, z.SLOTS])
        xa = sb("xa", [P, X_SLOTS, UT, D])
        stats = sb("stats", [P, X_SLOTS, UT, 6])
        pair = sb("pair", [P, X_SLOTS, UT, 2])
        diff = sb("diff", [P, X_SLOTS, UT])
        diff_sq = sb("diff_sq", [P, X_SLOTS, UT])
        neg_mean = sb("neg_mean1", [P, X_SLOTS, UT])
        var = sb("var", [P, X_SLOTS, UT])
        var_eps = sb("var_eps", [P, X_SLOTS, UT])
        rstd = sb("rstd", [P, X_SLOTS, UT])
        shift = sb("shift1", [P, X_SLOTS, UT])
        xn = sb("xn", [P, SLOTS, UT, D])
        xn2 = sb("xn2", [P, TWO, 2, UT, D], F32R)
        xt2 = sb("xt2", [P, TWO, 2, KD, UT * P], F32R)
        qf = sb("qf", [P, TWO, KD, UT * P])
        qt2 = sb("qt2", [P, SLOTS, 2, KD, UT * P], F32R)
        kf = sb("kf", [P, TWO, UT, D])
        ones_s, tri_s, causal_s = (kf[:, 0].rearrange("p t d -> p (t d)")[:, k * P:(k + 1) * P] for k in range(3))
        k_sum = sb("k_sum", [P, TWO, D])
        gate_s = k_sum[0:E, 0]
        k2 = sb("k2", [P, TWO, 2, UT, D], F32R)
        logit = sb("logit", [P, TWO, CT, E])
        best = sb("best", [P, TWO, CT])
        tied = sb("tied", [P, TWO, CT, E])
        lead = sb("lead", [P, TWO, CT])
        pick = sb("pick", [P, TWO, CT, E], BF16)
        row = sb("row", [P, TWO, CT, E])
        row_f = sb("row_f", [P, TWO, CT])
        row_u = sb("row_u", [P, SLOTS // CU, CT], U32)
        m2 = sb("m2", [P, 2, KD, D], F32R)
        kv2 = sb("kv2", [P, TWO, 2, KD, NV], F32R)
        zsum = sb("zsum", [P, SLOTS, UT])
        zinv = sb("zinv", [P, SLOTS, UT])
        zeros = z.res[:, z.TILES - 1]
        t_ps = ps("t1_ps", [P, KD, UT * P])
        q_ps = ps("q1_ps", [P, KD, UT * P])
        k_ps = ps("k1_ps", [P, UT, 512])
        m_ps = ps("m1_ps", [P, KD, D])
        ks_ps = ps("ks1_ps", [P, 512])
        v_ps = ps("v1_ps", [P, UT, 512])
        count_ps = k_ps[:, 0, NK:NK + (CT + 1) * E]
        g = sems("w_loaded gate_loaded moe_w_loaded blank consts cast gate_turned rounded split step zeroed zeros_stored "
                 "stats_done halves_met diff_squared var_found var_ready rstd_ready shift_ready xn_ready xn_rounded "
                 "xn_split t_ready t_rounded t_split k_ready k_exp k_capped k_full k_read k_rounded k_split k_added q_ready q_below "
                 "q_capped q_full q_rounded q_split best_found ties_found ties_ranked lead_found picked counted "
                 "row_based row_masked row_found row_ready row_kept base_moved sums_done m_rounded m_split kv_ready "
                 "kv_rounded kv_split v_ready zsum_ready zinv_ready rows_ready")
        x_loaded = [ctx.enter_context(nc.semaphore(f"xa_loaded{i}")) for i in range(X_SLOTS)]
        scattered = [ctx.enter_context(nc.semaphore(f"scattered{i}")) for i in range(SLOTS)]
        block = ctx.enter_context(nc.Block())
        x_units = z.x.rearrange("b (n u p) d -> (b n) p u d", u=UT, p=P)

        def there(n, least=0):
            return not isinstance(n, int) or least <= n < UNITS

        at = lambda i, ahead: (i + ahead) % SLOTS

        def chunk_counted(n, i, r):
            if (i - COUNT_LAG) % CU == 0 and there(n - COUNT_LAG):
                c = r * (SLOTS // CU) + (i - COUNT_LAG) // CU
                return c, (i - COUNT_LAG) // CU % TWO
            return None

        def row_closed(n, i, r):
            if (i - 1) % ROW == 0 and there(n - ROW - 1):
                return r * TWO + (i - 1) // ROW - 1, ((i - 1) // ROW - 1) % TWO
            return None

        run = lambda eng, first, step, last: pipeline(eng, first, step, last, UNITS, SLOTS)

        FREE = UNITS + 2 - V_LAG
        assert FREE % 2 == 0 and FREE + V_LAG > UNITS - CU + COUNT_LAG
        by_turns = lambda n: isinstance(n, int) and n >= FREE
        v_bank = lambda n: k_ps if by_turns(n) and n % 2 == 0 else v_ps

        gate_ps = v_ps[:, 0, 0:KD * E].rearrange("p (k e) -> p k e", e=E)
        weights = ((z.wq[:], w_s[:, :, 0:D]), (z.wkg[:, :, :, 0:D], w_s[:, :, D:2 * D]), (z.wkg[:, :, :, D:NK], gate_ps),
                   (z.wv[:], w_s[:, :, 2 * D:3 * D]))
        SPLITS = len(weights)

        @block.sync
        def _(sp):
            def step(n, i, r):
                m = n + 5
                if there(m):
                    if there(m, X_SLOTS):
                        sp.wait_ge(g["xn_ready"], m - X_SLOTS + 1)
                    sp.dma_start(xa[:, at(i, 5) % X_SLOTS], x_units[m]).then_inc(x_loaded[at(i, 5) % X_SLOTS], 16)
                if isinstance(m, int) and m == 1:
                    sp.dma_start(w_s[:], W.rearrange("(k p) n -> p k n", p=P)).then_inc(g["w_loaded"], 16)
                    sp.dma_start(gate_s, gate_w).then_inc(g["gate_loaded"], 16)
                if isinstance(m, int) and m == 4:
                    for k in range(KD):
                        for half, src in ((0, wg), (1, wu)):
                            sp.dma_start(z.wgu[:, k, :, half * z.DE:(half + 1) * z.DE],
                                         src[:, k * P:(k + 1) * P, :].rearrange("e p d -> p e d")).then_inc(g["moe_w_loaded"], 16)
                    for half in range(2):
                        sp.dma_start(z.wdn[half * z.DE:(half + 1) * z.DE], wd.rearrange("e d h -> d e h")).then_inc(g["moe_w_loaded"], 16)
                    sp.wait_ge(g["zeroed"], 1)
                    for e in range(E):
                        sp.dma_start(z.sorted_dram.ap()[e * z.REGION:e * z.REGION + P, :], zeros).then_inc(g["zeros_stored"], 16)

            run(sp, -5, step, UNITS - 1)
            sp.wait_ge(g["moe_w_loaded"], 16 * (2 * KD + 2))
            sp.wait_ge(g["zeros_stored"], 16 * E)

        @block.tensor
        def _(pe):
            def turn(n, i):
                if there(n):
                    pe.wait_ge(g["xn_ready"], n + 1)
                    if there(n, 1):
                        pe.wait_ge(g["t_split"], n)
                    for k in range(KD):
                        for t in range(UT):
                            m = nc.tensor.transpose(t_ps[:, k, t * P:(t + 1) * P], xn[:, i, t, k * P:(k + 1) * P], z.ident[:])
                    m.then_inc(g["t_ready"], 1)

            def q(n, i, r):
                if there(n):
                    pe.wait_ge(g["t_split"], n + 1)
                    if there(n, 1):
                        pe.wait_ge(g["q_full"], n)
                    for j in range(KD):
                        for k in range(KD):
                            m = mm3(nc, q_ps[:, j, :], [z.wq[:, a, k, j * P:(j + 1) * P] for a in range(2)],
                                    [xt2[:, i % TWO, a, k, :] for a in range(2)], j == 0 and k == 0, k == KD - 1, skip_group_check=True)
                    m.then_inc(g["q_ready"], 1)

            def keys(n, i, r):
                if there(n):
                    if there(n, 1):
                        pe.wait_ge(g["k_read"], n)
                    before = chunk_counted(n - 1, (i - 1) % SLOTS, r if i else r - 1)
                    if before:
                        pe.wait_ge(g["base_moved"], before[0] + 1)
                    for t in range(UT):
                        for k in range(KD):
                            m = mm3(nc, k_ps[:, t, 0:NK], [xt2[:, i % TWO, a, k, t * P:(t + 1) * P] for a in range(2)],
                                    [z.wkg[:, a, k, :] for a in range(2)], k == 0, k == KD - 1, skip_group_check=True)
                        if t == 0:
                            count(n, i, r)
                    m.then_inc(g["k_ready"], 1)

            def count(n, i, r):
                counted = chunk_counted(n, i, r)
                if counted:
                    c, s = counted
                    pe.wait_ge(g["picked"], c + 1)
                    flat = pick[:, s].rearrange("p t e -> p (t e)")
                    m = nc.tensor.matmul(count_ps[:, 0:CT * E], z.before[:], flat, start=not there(n), stop=False, skip_group_check=True)
                    for d in range(1, CT):
                        nc.tensor.matmul(count_ps[:, d * E:CT * E], z.ones_b[:], flat[:, 0:(CT - d) * E], start=False, stop=False,
                                         skip_group_check=True)
                    for t in range(CT):
                        m = nc.tensor.matmul(count_ps[:, CT * E:], z.ones_b[:], pick[:, s, t, :], start=False,
                                             stop=(t == CT - 1), skip_group_check=True)
                    m.then_inc(g["counted"], 1)

            def sums(n, i, r):
                if there(n):
                    pe.wait_ge(g["xn_split"], n + 1)
                    pe.wait_ge(g["k_split"], n + 1)
                    first, last = i % ROW == 0, i % ROW == ROW - 1
                    if first and there(n, 1):
                        pe.wait_ge(g["kv_split"], r * TWO + i // ROW)
                    for t in range(UT):
                        st, en = first and t == 0, last and t == UT - 1
                        kk = [k2[:, i % TWO, a, t, :] for a in range(2)]
                        for j in range(KD):
                            m = mm3(nc, m_ps[:, j, :], [xn2[:, i % TWO, a, t, j * P:(j + 1) * P] for a in range(2)], kk,
                                    st and j == 0, en, skip_group_check=True)
                    if last:
                        pe.wait_ge(g["k_added"], 2 * n + 2)
                        for j in range(KD):
                            m = nc.tensor.matmul(ks_ps[:, 2 * j:2 * j + 2], k_sum[:, i // ROW, j * P:(j + 1) * P], z.ones[:],
                                                 start=j == 0, stop=True, skip_group_check=True)
                    m.then_inc(g["sums_done"], 1)

            def kv(n, i, r):
                closed = row_closed(n, i, r)
                if closed:
                    b, _ = closed
                    pe.wait_ge(g["m_split"], 2 * b + 2)
                    for j in range(KD):
                        for k in range(KD):
                            m = mm3(nc, m_ps[:, j, :], [m2[:, a, k, j * P:(j + 1) * P] for a in range(2)],
                                    [z.wv[:, a, k, :] for a in range(2)], j == 0 and k == 0, k == KD - 1, skip_group_check=True)
                    m.then_inc(g["kv_ready"], 1)

            def values(n, i, r):
                if there(n):
                    if i % ROW == 0:
                        pe.wait_ge(g["kv_split"], r * TWO + i // ROW + 1)
                    pe.wait_ge(g["q_split"], n + 1)
                    if by_turns(n):
                        if n == FREE:
                            pe.wait_ge(g["k_read"], UNITS)
                            pe.wait_ge(g["base_moved"], UNITS // CU)
                        else:
                            pe.wait_ge(g["rows_ready"], UT * (n - 1))
                    elif there(n, 1):
                        pe.wait_ge(g["rows_ready"], UT * n)
                    for t in range(UT):
                        for j in range(KD):
                            m = mm3(nc, v_bank(n)[:, t, 0:NV], [qt2[:, i, a, j, t * P:(t + 1) * P] for a in range(2)],
                                    [kv2[:, i // ROW, a, j, :] for a in range(2)], j == 0, j == KD - 1)
                    m.then_inc(g["v_ready"], 1)

            def step(n, i, r):
                turn(n + 1, at(i, 1))
                if isinstance(n, int) and n == 0:
                    pe.wait_ge(g["split"], SPLITS)
                    pe.wait_ge(g["cast"], 6)
                q(n, i, r)
                keys(n, i, r)
                if not there(n):
                    count(n, i, r)
                kv(n, i, r)
                before = lambda: sums(n - 1, at(i, -1), r if i else r - 1)
                if not row_closed(n, i, r):
                    before()
                values(n - V_LAG, at(i, -V_LAG), r if i >= V_LAG else r - 1)
                if row_closed(n, i, r):
                    before()

            pe.wait_ge(g["consts"], 6)
            pe.wait_ge(g["gate_loaded"], 16)
            for k in range(KD):
                t = nc.tensor.transpose(gate_ps[:, k], gate_s[:, k * P:(k + 1) * P], z.ident[0:E, 0:E])
            t.then_inc(g["gate_turned"], 1)
            run(pe, -1, step, UNITS - 1 + V_LAG)

        @block.scalar
        def _(act):
            def norm_apply(n, i):
                if there(n):
                    act.wait_ge(g["shift_ready"], n + 1)
                    if there(n, SLOTS):
                        act.wait_ge(scattered[i], (n - i) * (16 * UT // SLOTS))
                    for t in range(UT):
                        m = nc.scalar.activation(xn[:, i, t, :], xa[:, i % X_SLOTS, t, :], ACT.Identity,
                                                 bias=shift[:, i % X_SLOTS, t:t + 1], scale=rstd[:, i % X_SLOTS, t:t + 1])
                    m.then_inc(g["xn_ready"], 1)

            def round_xn(n, i):
                if there(n):
                    act.wait_ge(g["xn_ready"], n + 1)
                    if there(n, TWO):
                        act.wait_ge(g["sums_done"], n - TWO + 1)
                    nc.scalar.activation(xn2[:, i % TWO, 0], xn[:, i], ACT.Copy).then_inc(g["xn_rounded"], 1)

            def round_turned(n, i):
                if there(n):
                    act.wait_ge(g["t_ready"], n + 1)
                    nc.scalar.activation(xt2[:, i % TWO, 0], t_ps[:], ACT.Copy).then_inc(g["t_rounded"], 1)

            def below_q(n, i):
                if there(n):
                    act.wait_ge(g["q_ready"], n + 1)
                    if there(n, TWO):
                        act.wait_ge(g["q_split"], n - TWO + 1)
                    nc.scalar.activation(qf[:, i % TWO], q_ps[:], ACT.Relu, scale=-1.0).then_inc(g["q_below"], 1)

            def exp_q(n, i):
                if there(n):
                    act.wait_ge(g["q_below"], n + 1)
                    nc.scalar.activation(qf[:, i % TWO], qf[:, i % TWO], ACT.Exp, scale=-1.0).then_inc(g["q_capped"], 1)

            def exp_keys(n, i):
                if there(n):
                    act.wait_ge(g["k_ready"], n + 1)
                    if there(n, TWO):
                        act.wait_ge(g["k_split"], n - TWO + 1)
                    nc.scalar.activation(kf[:, i % TWO], k_ps[:, :, 0:D], ACT.Exp).then_inc(g["k_exp"], 1)

            def round_q(n, i):
                if there(n):
                    act.wait_ge(g["q_full"], n + 1)
                    nc.scalar.activation(qt2[:, i, 0], qf[:, i % TWO], ACT.Copy).then_inc(g["q_rounded"], 1)

            def round_keys(n, i):
                if there(n):
                    act.wait_ge(g["k_full"], n + 1)
                    if there(n, TWO):
                        act.wait_ge(g["sums_done"], n - TWO + 1)
                    nc.scalar.activation(k2[:, i % TWO, 0], kf[:, i % TWO], ACT.Copy).then_inc(g["k_rounded"], 1)

            def round_sums(n, i, r):
                closed = row_closed(n, i, r)
                if closed:
                    act.wait_ge(g["sums_done"], n - 1)
                    nc.scalar.activation(m2[:, 0], m_ps[:], ACT.Copy).then_inc(g["m_rounded"], 1)
                    nc.scalar.activation(kv2[:, closed[1], 0, :, D:NV], ks_ps[:, 0:2 * KD].rearrange("p (j c) -> p j c", c=2),
                                         ACT.Copy).then_inc(g["m_rounded"], 1)

            def round_kv(n, i, r):
                closed = row_closed(n, i, r)
                if closed:
                    act.wait_ge(g["kv_ready"], closed[0] + 1)
                    nc.scalar.activation(kv2[:, closed[1], 0, :, 0:D], m_ps[:], ACT.Copy).then_inc(g["kv_rounded"], 1)

            def scale_rows(n, i):
                if there(n):
                    act.wait_ge(g["zinv_ready"], n + 1)
                    if isinstance(n, int) and n == UNITS - 1:
                        act.wait_ge(g["zeros_stored"], 16 * E)
                    for t in range(UT):
                        nc.scalar.activation(z.res[:, bass.ds(UT * n + t, 1), :], v_bank(n)[:, t, 0:D].unsqueeze(1), ACT.Copy,
                                             scale=zinv[:, i, t:t + 1]).then_inc(g["rows_ready"], 1)

            def round_weights():
                act.wait_ge(g["w_loaded"], 16)
                for dst, src in weights:
                    if src is gate_ps:
                        act.wait_ge(g["gate_turned"], 1)
                    nc.scalar.activation(dst[:, 0], src, ACT.Copy).then_inc(g["rounded"], 1)

            def step(n, i, r):
                begin = isinstance(n, int) and n <= 0
                round_sums(n, i, r)
                if begin and n == -2:
                    norm_apply(0, 0)
                    round_weights()
                round_turned(n + 1, at(i, 1))
                if begin and n > -2:
                    norm_apply(n + 2, at(i, 2))
                below_q(n, i)
                scale_rows(n - V_LAG - 1, at(i, -V_LAG - 1))
                exp_q(n, i)
                round_kv(n, i, r)
                exp_keys(n, i)
                if not begin:
                    norm_apply(n + 2, at(i, 2))
                round_q(n, i)
                round_xn(n, i)
                round_keys(n, i)

            run(act, -2, step, UNITS + V_LAG)

        @block.vector
        def _(dve):
            def norm_stats(n, i):
                if there(n):
                    s = i % X_SLOTS
                    dve.wait_ge(x_loaded[s], (n - s) * (16 // X_SLOTS) + 16)
                    for t in range(UT):
                        nc.vector.bn_stats(stats[:, s, t], xa[:, s, t, :]).then_inc(g["stats_done"], 1)

            def meet_halves(n, i):
                if there(n):
                    s = i % X_SLOTS
                    dve.wait_ge(g["stats_done"], UT * n + UT)
                    nc.vector.tensor_tensor(pair[:, s], stats[:, s, :, 1:3], stats[:, s, :, 4:6], ALU.add).then_inc(g["halves_met"], 1)
                    nc.vector.tensor_tensor(diff[:, s], stats[:, s, :, 1], stats[:, s, :, 4], ALU.subtract).then_inc(g["halves_met"], 1)

            def square_difference(n, i):
                if there(n):
                    s = i % X_SLOTS
                    dve.wait_ge(g["halves_met"], 2 * n + 2)
                    nc.vector.scalar_tensor_tensor(diff_sq[:, s], diff[:, s], 0.25, diff[:, s], ALU.mult, ALU.mult).then_inc(g["diff_squared"], 1)
                    nc.vector.tensor_scalar(neg_mean[:, s], pair[:, s, :, 0], -0.5, None, ALU.mult)

            def variance(n, i):
                if there(n):
                    s = i % X_SLOTS
                    dve.wait_ge(g["diff_squared"], n + 1)
                    nc.vector.scalar_tensor_tensor(var[:, s], pair[:, s, :, 1], 1.0 / D, diff_sq[:, s], ALU.mult, ALU.add).then_inc(g["var_found"], 1)

            def variance_eps(n, i):
                if there(n):
                    s = i % X_SLOTS
                    dve.wait_ge(g["var_found"], n + 1)
                    nc.vector.tensor_scalar(var_eps[:, s], var[:, s], LN_EPS, None, ALU.add).then_inc(g["var_ready"], 1)

            def split_turned(n, i):
                if there(n):
                    dve.wait_ge(g["t_rounded"], n + 1)
                    nc.vector.tensor_tensor(xt2[:, i % TWO, 1], t_ps[:], xt2[:, i % TWO, 0].bitcast(F32), ALU.subtract).then_inc(g["t_split"], 1)

            def fill_q(n, i):
                if there(n):
                    f = qf[:, i % TWO]
                    dve.wait_ge(g["q_capped"], n + 1)
                    nc.vector.scalar_tensor_tensor(f, q_ps[:], 0.0, f, ALU.max, ALU.add).then_inc(g["q_full"], 1)

            def cap_keys(n, i):
                if there(n):
                    f = kf[:, i % TWO]
                    dve.wait_ge(g["k_exp"], n + 1)
                    nc.vector.tensor_scalar(f, f, 1.0, None, ALU.min).then_inc(g["k_capped"], 1)

            def fill_keys(n, i):
                if there(n):
                    f = kf[:, i % TWO]
                    dve.wait_ge(g["k_capped"], n + 1)
                    nc.vector.scalar_tensor_tensor(f, k_ps[:, :, 0:D], 0.0, f, ALU.max, ALU.add).then_inc(g["k_full"], 1)
                    nc.vector.tensor_copy(logit[:, i // CU % TWO, i % CU * UT:i % CU * UT + UT, :], k_ps[:, :, D:NK]).then_inc(g["k_read"], 1)

            def add_keys(n, i, t):
                if there(n):
                    rows = k_sum[:, i // ROW]
                    if t == 0:
                        dve.wait_ge(g["k_full"], n + 1)
                    if i % ROW == 0:
                        if t == 0:
                            if there(n, SLOTS):
                                dve.wait_ge(g["sums_done"], n - ROW)
                            nc.vector.tensor_tensor(rows, kf[:, i % TWO, 0], kf[:, i % TWO, 1], ALU.add).then_inc(g["k_added"], 2)
                    else:
                        dve.wait_ge(g["k_added"], 2 * n + t)
                        nc.vector.tensor_tensor(rows, rows, kf[:, i % TWO, t], ALU.add).then_inc(g["k_added"], 1)

            def split_keys(n, i):
                if there(n):
                    dve.wait_ge(g["k_rounded"], n + 1)
                    nc.vector.tensor_tensor(k2[:, i % TWO, 1], kf[:, i % TWO], k2[:, i % TWO, 0].bitcast(F32), ALU.subtract).then_inc(g["k_split"], 1)

            def route_and_place(n, i, r):
                routed = (r * (SLOTS // CU) + i // CU + 1, i // CU % TWO) if there(n) and i % CU == CU - 1 else None
                counted = chunk_counted(n, i, r)
                if counted:
                    c, s = counted
                    dve.wait_ge(g["counted"], c + 1)
                    if not (isinstance(c, int) and c == 0):
                        dve.wait_ge(g["base_moved"], c)
                    nc.vector.tensor_tensor(row[:, s], count_ps[:, 0:CT * E].rearrange("p (t e) -> p t e", e=E),
                                            z.next_row[:].unsqueeze(1).to_broadcast([P, CT, E]), ALU.add).then_inc(g["row_based"], 1)
                if routed:
                    rc, rs = routed
                    dve.wait_ge(g["k_read"], n + 1)
                    nc.vector.tensor_reduce(best[:, rs], logit[:, rs], AX_X, ALU.max).then_inc(g["best_found"], 1)
                if counted:
                    dve.wait_ge(g["row_based"], c + 1)
                    nc.vector.tensor_tensor(z.next_row[:], count_ps[:, CT * E:], z.next_row[:], ALU.add).then_inc(g["base_moved"], 1)
                    nc.vector.tensor_tensor(row[:, s], row[:, s], pick[:, s], ALU.mult).then_inc(g["row_masked"], 1)
                if routed:
                    dve.wait_ge(g["best_found"], rc)
                    nc.vector.tensor_tensor(tied[:, rs], logit[:, rs], best[:, rs].unsqueeze(2).to_broadcast([P, CT, E]), ALU.is_equal).then_inc(g["ties_found"], 1)
                if counted:
                    dve.wait_ge(g["row_masked"], c + 1)
                    nc.vector.tensor_reduce(row_f[:, s], row[:, s], AX_X, ALU.add).then_inc(g["row_found"], 1)
                if routed:
                    dve.wait_ge(g["ties_found"], rc)
                    nc.vector.tensor_tensor(tied[:, rs], tied[:, rs], z.first_rank[:], ALU.mult).then_inc(g["ties_ranked"], 1)
                if counted:
                    dve.wait_ge(g["row_found"], c + 1)
                    nc.vector.tensor_copy(row_u[:, (i - COUNT_LAG) // CU % (SLOTS // CU)], row_f[:, s]).then_inc(g["row_ready"], 1)
                if routed:
                    dve.wait_ge(g["ties_ranked"], rc)
                    nc.vector.tensor_reduce(lead[:, rs], tied[:, rs], AX_X, ALU.max).then_inc(g["lead_found"], 1)
                if counted:
                    nc.vector.tensor_copy(z.place[:, bass.ds(CT * c, CT)], row_f[:, s]).then_inc(g["row_kept"], 1)
                if routed:
                    dve.wait_ge(g["lead_found"], rc)
                    nc.vector.tensor_tensor(pick[:, rs], tied[:, rs], lead[:, rs].unsqueeze(2).to_broadcast([P, CT, E]), ALU.is_equal).then_inc(g["picked"], 1)

            def keep_pick(n, i, r):
                if there(n) and i % CU == CU - 1:
                    rc = r * (SLOTS // CU) + i // CU + 1
                    dve.wait_ge(g["picked"], rc)
                    nc.vector.tensor_copy(z.chosen[:, bass.ds(CT * rc - CT, CT), :], pick[:, i // CU % TWO])

            def split_sums(n, i, r):
                closed = row_closed(n, i, r)
                if closed:
                    b, s = closed
                    dve.wait_ge(g["m_rounded"], 2 * b + 2)
                    nc.vector.tensor_tensor(m2[:, 1], m_ps[:], m2[:, 0].bitcast(F32), ALU.subtract).then_inc(g["m_split"], 1)
                    nc.vector.tensor_tensor(kv2[:, s, 1, :, D:NV], ks_ps[:, 0:2 * KD].rearrange("p (j c) -> p j c", c=2),
                                            kv2[:, s, 0, :, D:NV].bitcast(F32), ALU.subtract).then_inc(g["m_split"], 1)

            def split_kv(n, i, r):
                closed = row_closed(n, i, r)
                if closed:
                    b, s = closed
                    dve.wait_ge(g["kv_rounded"], b + 1)
                    nc.vector.tensor_tensor(kv2[:, s, 1, :, 0:D], m_ps[:], kv2[:, s, 0, :, 0:D].bitcast(F32), ALU.subtract).then_inc(g["kv_split"], 1)

            def base_divisors(n, i):
                if there(n):
                    dve.wait_ge(g["v_ready"], n + 1)
                    nc.vector.tensor_scalar(zsum[:, i], v_bank(n)[:, :, D], Z_EPS, 2.0, ALU.add, ALU.mult).then_inc(g["zsum_ready"], 1)

            def invert_divisors(n, i):
                if there(n):
                    dve.wait_ge(g["zsum_ready"], n + 1)
                    nc.vector.reciprocal(zinv[:, i], zsum[:, i]).then_inc(g["zinv_ready"], 1)

            def split_weights():
                for k, (dst, src) in enumerate(weights):
                    dve.wait_ge(g["rounded"], k + 1)
                    nc.vector.tensor_tensor(dst[:, 1], src, dst[:, 0].bitcast(F32), ALU.subtract).then_inc(g["split"], 1)

            links = 0

            def link(ins):
                nonlocal links
                links += 1
                ins.then_inc(g["step"], 1)
                dve.wait_ge(g["step"], links)

            shape = [P, z.SLOTS, E]
            of_slots = lambda v: v[:].unsqueeze(2).to_broadcast(shape)
            of_experts = lambda v: v[:].unsqueeze(1).to_broadcast(shape)
            spare = w_s[:].rearrange("p k n -> p (k n)")
            past = spare[:, 0:z.SLOTS * E].rearrange("p (s e) -> p s e", e=E)

            def table_experts():
                dve.wait_ge(g["base_moved"], UNITS // CU)
                link(nc.vector.tensor_tensor(held[:], z.next_row[:], z.region0[:], ALU.subtract))
                link(nc.vector.tensor_scalar(held[:], held[:], float(P - 1), None, ALU.add))
                link(nc.vector.tensor_copy(held_i[:], held[:]))
                link(nc.vector.tensor_scalar(tiles_i[:], held_i[:], P.bit_length() - 1, None, ALU.arith_shift_right))
                link(nc.vector.tensor_copy(tiles[:], tiles_i[:]))
                link(nc.vector.memset(one_col[:], 1.0))
                link(nc.vector.tensor_tensor_scan(ends[:], one_col[:], tiles[:], 0.0, ALU.mult, ALU.add))
                link(nc.vector.scalar_tensor_tensor(z.moved[:], ends[:], float(-P), z.next_row[:], ALU.mult, ALU.add))

            def table_owners():
                link(nc.vector.memset(change[:, E - 1:E], 0.0))
                link(nc.vector.tensor_tensor(change[:, 0:E - 1], z.moved[:, 1:E], z.moved[:, 0:E - 1], ALU.subtract))
                link(nc.vector.tensor_tensor(past, of_experts(ends), of_slots(z.slot_id), ALU.is_le))
                link(nc.vector.tensor_reduce(owner[:], past, AX_X, ALU.add))

            def table_offsets():
                link(nc.vector.tensor_tensor(past, past, of_experts(change), ALU.mult))
                link(nc.vector.tensor_reduce(offset[:], past, AX_X, ALU.add))

            def table_rows():
                link(nc.vector.tensor_scalar(real[:], owner[:], float(E), None, ALU.is_lt))
                link(nc.vector.tensor_scalar(offset[:], offset[:], z.moved[:, 0:1], None, ALU.add))
                link(nc.vector.scalar_tensor_tensor(first_row[:], z.slot_id[:], float(P), offset[:], ALU.mult, ALU.add))
                link(nc.vector.tensor_tensor(first_row[:], first_row[:], real[:], ALU.mult))
                link(nc.vector.tensor_copy(z.row_i[:], first_row[:]))
                link(nc.vector.tensor_scalar(owner[:], owner[:], float(E - 1), None, ALU.min))
                link(nc.vector.tensor_copy(z.owners_i[:], owner[:]))

            tables = {UNITS + 2: table_owners, UNITS + 3: table_offsets, UNITS + 4: table_rows}

            def step(n, i, r):
                late, ahead = (n - V_LAG - 1, at(i, -V_LAG - 1)), (n + 3, at(i, 3))
                if isinstance(n, int) and n == -1:
                    split_weights()
                if not there(n):
                    split_sums(n, i, r)
                base_divisors(*late)
                add_keys(n - 1, at(i, -1), 0)
                split_keys(n - 1, at(i, -1))
                add_keys(n - 1, at(i, -1), 1)
                invert_divisors(*late)
                if there(n):
                    split_sums(n, i, r)
                split_turned(n + 1, at(i, 1))
                norm_stats(*ahead)
                meet_halves(*ahead)
                fill_q(n, i)
                if there(n):
                    split_kv(n, i, r)
                square_difference(*ahead)
                cap_keys(n, i)
                variance(*ahead)
                fill_keys(n, i)
                variance_eps(*ahead)
                route_and_place(n, i, r)
                if isinstance(n, int) and n == UNITS + 1:
                    table_experts()
                if not there(n):
                    split_kv(n, i, r)
                keep_pick(n, i, r)
                if isinstance(n, int) and n in tables:
                    tables[n]()

            run(dve, -3, step, UNITS + V_LAG)
            dve.wait_ge(g["row_kept"], UNITS // CU)

        @block.gpsimd
        def _(pool):
            def norm_scale(n, i):
                if there(n):
                    s = i % X_SLOTS
                    pool.wait_ge(g["var_ready"], n + 1)
                    nc.gpsimd.tensor_tensor(rstd[:, s], var_eps[:, s], z.neg_half[:, 0:UT], ALU.pow).then_inc(g["rstd_ready"], 1)
                    pool.wait_ge(g["rstd_ready"], n + 1)
                    nc.gpsimd.tensor_tensor(shift[:, s], neg_mean[:, s], rstd[:, s], ALU.mult).then_inc(g["shift_ready"], 1)

            def split_xn(n, i):
                if there(n):
                    pool.wait_ge(g["xn_rounded"], n + 1)
                    s = i % TWO
                    nc.gpsimd.tensor_tensor(xn2[:, s, 1], xn[:, i], xn2[:, s, 0].bitcast(F32), ALU.subtract).then_inc(g["xn_split"], 1)

            def split_q(n, i):
                if there(n):
                    pool.wait_ge(g["q_rounded"], n + 1)
                    nc.gpsimd.tensor_tensor(qt2[:, i, 1], qf[:, i % TWO], qt2[:, i, 0].bitcast(F32), ALU.subtract).then_inc(g["q_split"], 1)

            def placed(n, i, r):
                if there(n):
                    pool.wait_ge(g["row_ready"], r * (SLOTS // CU) + i // CU + 1)

            def scatter(n, i):
                if there(n):
                    for t in range(UT):
                        k = i % CU * UT + t
                        nc.gpsimd.indirect_dma_start(
                            out=z.sorted_dram.ap(), out_offset=bass.IndirectOffsetOnAxis(ap=row_u[:, i // CU, k:k + 1], axis=0),
                            in_=xn[:, i, t, :], in_offset=None).then_inc(scattered[i], 16)

            def step(n, i, r):
                norm_scale(n + 2, at(i, 2))
                if isinstance(n, int) and n == -1:
                    for dst, src in ((z.ones, ones_s[:, 0:2]), (z.ones_b, ones_s), (z.before, tri_s), (z.causal, causal_s),
                                     (z.ident_b, z.ident[:]), (z.slot_id, ids[:])):
                        nc.gpsimd.tensor_copy(dst[:], src).then_inc(g["cast"], 1)
                placed(n - SCATTER_LAG, at(i, -SCATTER_LAG), r if i >= SCATTER_LAG else r - 1)
                split_q(n - 1, at(i, -1))
                scatter(n - SCATTER_LAG, at(i, -SCATTER_LAG))
                split_xn(n, i)

            nc.gpsimd.memset(z.ident[:], 0.0).then_inc(g["blank"], 1)
            nc.gpsimd.memset(tri_s, 1.0).then_inc(g["blank"], 1)
            nc.gpsimd.memset(causal_s, 0.0).then_inc(g["blank"], 1)
            pool.wait_ge(g["blank"], 3)
            nc.gpsimd.affine_select(out=z.ident[:], in_=z.ident[:], compare_op=ALU.not_equal, fill=1.0, base=0,
                                    pattern=[[-1, P]], channel_multiplier=1).then_inc(g["consts"], 1)
            nc.gpsimd.affine_select(out=tri_s, in_=tri_s, compare_op=ALU.is_gt, fill=0.0, base=0,
                                    pattern=[[1, P]], channel_multiplier=-1).then_inc(g["consts"], 1)
            nc.gpsimd.affine_select(out=causal_s, in_=causal_s, compare_op=ALU.is_ge, fill=MASKED, base=0,
                                    pattern=[[-1, P]], channel_multiplier=1).then_inc(g["consts"], 1)
            nc.gpsimd.memset(ones_s, 1.0).then_inc(g["consts"], 1)
            nc.gpsimd.iota(ids[:], pattern=[[1, z.SLOTS]], base=0, channel_multiplier=0).then_inc(g["consts"], 1)
            nc.gpsimd.memset(z.neg_half[:], -0.5)
            for e in range(E):
                nc.gpsimd.memset(z.first_rank[:, :, e:e + 1], float(E - e))
                nc.gpsimd.memset(z.region0[:, e:e + 1], float(e * z.REGION + P))
                nc.gpsimd.memset(z.next_row[:, e:e + 1], float(e * z.REGION + P))
            nc.gpsimd.memset(z.place[:, z.TILES:], 0.0).then_inc(g["consts"], 1)
            nc.gpsimd.memset(zeros, 0.0).then_inc(g["zeroed"], 1)
            pool.wait_ge(g["consts"], 6)
            run(pool, -2, step, UNITS - 1 + SCATTER_LAG)
            for i in range(SLOTS):
                pool.wait_ge(scattered[i], 16 * UT * UNITS // SLOTS)


def experts(nc, z, W_qkv, W_out, b_out, ln_g, ln_b):
    KD, D, E, DE, SLOTS = z.KD, z.D, z.E, z.DE, z.SLOTS
    QUAD = 4
    PAIRS = SLOTS // 2
    ROUNDS = PAIRS // QUAD
    assert PAIRS == ROUNDS * QUAD
    with ExitStack() as ctx:
        sb, ps, sems = scope(nc, ctx)
        shift_all = sb("shift_all", [P, z.TILES, E])
        shift = sb("shift", [P, z.TILES])
        xg = sb("xg", [P, QUAD, 2, D])
        xgt = sb("xgt", [P, QUAD, KD, 2, P])
        gate = sb("gate", [P, 2, 2, DE])
        hid = sb("hid", [P, 2, 2, 2, DE])
        hidt = sb("hidt", [P, 2, 2, P], F32R)
        wdn2 = sb("wdn2", [P, 2, E, D], F32R)
        th = sb("th", [P, 2, 2, D])
        y = sb("y", [P, QUAD, 2, D])
        t_ps = ps("t_ps", [P, 2, KD, 2, P])
        gu_ps = ps("gu_ps", [P, 2, 512])
        ht_ps = ps("ht_ps", [P, 2, 512])
        y_ps = ps("y_ps", [P, 2, 2, D])
        g = sems("weights_loaded shifts_ready shift_found t_ready t_copied gu_ready gate_relu squared hid_ready ht_ready ht_rounded ht_copied y_ready "
                 "y_tanh silu_ready wdn_rounded wdn_split")
        loaded = [[ctx.enter_context(nc.semaphore(f"loaded{u}_{i}")) for i in range(QUAD)] for u in range(2)]
        stored = [ctx.enter_context(nc.semaphore(f"stored{i}")) for i in range(QUAD)]
        block = ctx.enter_context(nc.Block())
        y_rows = z.expert_dram.ap().rearrange("(n u p) d -> n p u d", u=2, p=P)

        def load(eng, n, i, u):
            first = eng.value_load(z.row_i[0:1, bass.ds(n * 2 + u, 1)], min_val=0, max_val=E * z.REGION - P)
            eng.dma_start(xg[:, i, u, :], z.sorted_dram.ap()[bass.ds(first, P), :]).then_inc(loaded[u][i], 16)

        def load_again(eng, n, i, u):
            eng.wait_ge(g["t_ready"], n + i - QUAD + 1)
            load(eng, n + i, i, u)

        def load_first(eng, u):
            for i in range(QUAD):
                load(eng, i, i, u)
            for i in range(QUAD):
                load_again(eng, QUAD, i, u)

        @block.sync
        def _(sp):
            def store(n, i):
                sp.wait_ge(g["silu_ready"], n + i + 1)
                sp.dma_start(y_rows[n + i], y[:, i]).then_inc(stored[i], 16)

            load_first(sp, 0)
            with sp.Fori(0, ROUNDS - 2) as r:
                for i in range(QUAD + 1):
                    if i < QUAD:
                        load_again(sp, r * QUAD + 2 * QUAD, i, 0)
                    if i == QUAD:
                        store(r * QUAD, i - 2)
                        store(r * QUAD, i - 1)
                    elif i >= 2:
                        store(r * QUAD, i - 2)
            for dst, src in ((z.w2, W_qkv), (z.wo, W_out)):
                sp.dma_start(dst[:], src.rearrange("(k p) n -> p k n", p=P)).then_inc(g["weights_loaded"], 16)
            for dst, src in ((z.bout, b_out), (z.lng, ln_g), (z.lnb, ln_b)):
                sp.dma_start(dst[:], src.partition_broadcast(P)).then_inc(g["weights_loaded"], 16)
            for n in range(PAIRS - 2 * QUAD, PAIRS, QUAD):
                for i in range(QUAD):
                    store(n, i)
            for i in range(QUAD):
                sp.wait_ge(stored[i], 16 * ROUNDS)
            sp.wait_ge(g["weights_loaded"], 16 * 5)

        @block.gpsimd
        def _(pool):
            load_first(pool, 1)
            with pool.Fori(0, ROUNDS - 2) as r:
                for i in range(QUAD):
                    load_again(pool, r * QUAD + 2 * QUAD, i, 1)

        @block.tensor
        def _(pe):
            def turn(n, i, reused):
                for u in range(2):
                    pe.wait_ge(loaded[u][i], (n - i) * (16 // QUAD) + 16)
                if reused:
                    pe.wait_ge(g["t_copied"], n - 1)
                for k in range(KD):
                    for u in range(2):
                        t = nc.tensor.transpose(t_ps[:, i % 2, k, u, :], xg[:, i, u, k * P:(k + 1) * P], z.ident[:])
                t.then_inc(g["t_ready"], 1)

            def gate_up(n, i, e, reused):
                pe.wait_ge(g["t_copied"], n + 1)
                if reused:
                    pe.wait_ge(g["hid_ready"], n - 1)
                for u in range(2):
                    for k in range(KD):
                        m = nc.tensor.matmul(gu_ps[:, i % 2, u * 2 * DE:(u + 1) * 2 * DE], xgt[:, i, k, u, :],
                                             z.wgu[:, k, bass.ds(e[u], 1), :].rearrange("p a f -> p (a f)"),
                                             start=(u == 0 and k == 0), stop=(k == KD - 1), skip_group_check=True)
                m.then_inc(g["gu_ready"], 1)

            def turn_hidden(n, i, reused):
                pe.wait_ge(g["hid_ready"], n + 1)
                if reused:
                    pe.wait_ge(g["ht_copied"], n - 1)
                for u in range(2):
                    t = nc.tensor.transpose(ht_ps[:, i % 2, u * P:(u + 1) * P], hid[:, i % 2, u].rearrange("p c f -> p (c f)"), z.ident[:])
                t.then_inc(g["ht_ready"], 1)

            def down(n, i, e, reused):
                pe.wait_ge(g["ht_copied"], n + 1)
                if reused:
                    pe.wait_ge(g["silu_ready"], n - 1)
                for u in range(2):
                    for part in range(2):
                        m = nc.tensor.matmul(y_ps[:, i % 2, u, :], hidt[:, i % 2, u, :],
                                             wdn2[:, part, bass.ds(e[u], 1), :].rearrange("p a h -> p (a h)"),
                                             start=(u == 0 and part == 0), stop=(part == 1), skip_group_check=True)
                m.then_inc(g["y_ready"], 1)

            owners = [pe.alloc_register(f"owner{j}") for j in range(2 * QUAD)]

            earlier = {i: [pe.alloc_register(f"earlier{i}_{u}") for u in range(2)] for i in (2, 3)}

            def load_owners(r):
                pe.load(owners, z.owners_i[0:1, bass.ds(r * 2 * QUAD, 2 * QUAD)])

            def four_pairs(r, first, last):
                n = r * QUAD
                e = [None] * QUAD

                def expert(register):
                    return pe.snap(register, min_val=0, max_val=E - 1)

                def know(i):
                    e[i] = [expert(o) for o in owners[2 * i:2 * i + 2]]

                def up(i):
                    gate_up(n + i, i, e[i], not first or i >= 2)

                def dn(i):
                    down(n + i, i, e[i], not first or i >= 2)

                def turns(i):
                    if not last:
                        turn(n + QUAD + i, i, True)
                    turn_hidden(n + i, i, not first or i >= 2)

                def earlier_down(i):
                    if first:
                        turn(i, i, True)
                    else:
                        down(n - QUAD + i, i, [expert(o) for o in earlier[i]], True)

                know(0)
                up(0)
                earlier_down(2)
                know(1)
                up(1)
                earlier_down(3)
                turns(0)
                know(2)
                up(2)
                know(3)
                if not last:
                    for i in earlier:
                        for u in range(2):
                            pe.reg_mov(earlier[i][u], e[i][u])
                turns(1)
                dn(0)
                up(3)
                if not last:
                    load_owners(r + 1)
                turns(2)
                dn(1)
                turns(3)
                if last:
                    dn(2)
                    dn(3)

            load_owners(0)
            for i in range(2):
                turn(i, i, False)
            pe.wait_ge(g["wdn_split"], 1)
            four_pairs(0, True, False)
            with pe.Fori(1, ROUNDS - 1) as r:
                four_pairs(r, False, False)
            four_pairs(ROUNDS - 1, False, True)

        @block.scalar
        def _(act):
            def copy_turned(n, i, reused):
                act.wait_ge(g["t_ready"], n + 1)
                if reused:
                    act.wait_ge(g["gu_ready"], n - QUAD + 1)
                nc.scalar.activation(xgt[:, i], t_ps[:, i % 2], ACT.Copy).then_inc(g["t_copied"], 1)

            def relu(n, i):
                act.wait_ge(g["gu_ready"], n + 1)
                o = gu_ps[:, i % 2, 0:4 * DE].rearrange("p (u f) -> p u f", u=2)
                nc.scalar.activation(gate[:, i % 2], o[:, :, 0:DE], ACT.Relu).then_inc(g["gate_relu"], 1)

            def copy_hidden(n, i):
                act.wait_ge(g["ht_ready"], n + 1)
                nc.scalar.activation(hidt[:, i % 2], ht_ps[:, i % 2, 0:2 * P].rearrange("p (u t) -> p u t", u=2), ACT.Copy).then_inc(g["ht_rounded"], 1)

            def tanh(n, i):
                act.wait_ge(g["y_ready"], n + 1)
                nc.scalar.activation(th[:, i % 2], y_ps[:, i % 2], ACT.Tanh, scale=0.5).then_inc(g["y_tanh"], 1)

            def four_pairs(n, first, last):
                def turns(i):
                    if not last:
                        copy_turned(n + QUAD + i, i, True)
                    copy_hidden(n + i, i)

                for i in range(2):
                    relu(n + i, i)
                    if first:
                        copy_turned(i + 2, i + 2, False)
                    else:
                        tanh(n + i - 2, i + 2)
                turns(0)
                relu(n + 2, 2)
                turns(1)
                tanh(n, 0)
                relu(n + 3, 3)
                turns(2)
                tanh(n + 1, 1)
                turns(3)
                if last:
                    tanh(n + 2, 2)
                    tanh(n + 3, 3)

            for i in range(2):
                copy_turned(i, i, False)
            four_pairs(0, True, False)
            with act.Fori(1, ROUNDS - 1) as r:
                four_pairs(r * QUAD, False, False)
            four_pairs(PAIRS - QUAD, False, True)

        @block.vector
        def _(dve):
            def hidden(n, i):
                dve.wait_ge(g["gate_relu"], n + 1)
                o = gu_ps[:, i % 2, 0:4 * DE].rearrange("p (u f) -> p u f", u=2)
                nc.vector.scalar_tensor_tensor(gate[:, i % 2], o[:, :, 0:DE], 0.0, gate[:, i % 2], ALU.max, ALU.mult).then_inc(g["squared"], 1)
                dve.wait_ge(g["squared"], n + 1)
                twice = [P, 2, 2, DE]
                nc.vector.tensor_tensor(hid[:, i % 2], o[:, :, DE:2 * DE].unsqueeze(2).to_broadcast(twice),
                                        gate[:, i % 2].unsqueeze(2).to_broadcast(twice), ALU.mult).then_inc(g["hid_ready"], 1)

            def hidden_rest(n, i):
                dve.wait_ge(g["ht_rounded"], n + 1)
                nc.vector.tensor_tensor(hidt[DE:P, i % 2], ht_ps[DE:P, i % 2, 0:2 * P].rearrange("p (u t) -> p u t", u=2),
                                        hidt[DE:P, i % 2], ALU.subtract).then_inc(g["ht_copied"], 1)

            def silu(n, i, reused):
                dve.wait_ge(g["y_tanh"], n + 1)
                if reused:
                    dve.wait_ge(stored[i], (n - i) * (16 // QUAD))
                nc.vector.scalar_tensor_tensor(y[:, i], th[:, i % 2], 1.0, y_ps[:, i % 2], ALU.add, ALU.mult).then_inc(g["silu_ready"], 1)

            def four_pairs(n, first=False, second=False, last=False):
                hidden(n, 0)
                if not first:
                    silu(n - 2, 2, not second)
                hidden(n + 1, 1)
                if not first:
                    silu(n - 1, 3, not second)
                hidden_rest(n, 0)
                hidden(n + 2, 2)
                hidden_rest(n + 1, 1)
                silu(n, 0, not first)
                hidden(n + 3, 3)
                hidden_rest(n + 2, 2)
                silu(n + 1, 1, not first)
                hidden_rest(n + 3, 3)
                if last:
                    silu(n + 2, 2, True)
                    silu(n + 3, 3, True)

            nc.vector.tensor_copy(wdn2[:, 0], z.wdn[:]).then_inc(g["wdn_rounded"], 1)
            dve.wait_ge(g["wdn_rounded"], 1)
            nc.vector.tensor_tensor(wdn2[:, 1], z.wdn[:], wdn2[:, 0], ALU.subtract).then_inc(g["wdn_split"], 1)
            nc.vector.tensor_tensor(shift_all[:], z.chosen[:], z.moved[:].unsqueeze(1).to_broadcast([P, z.TILES, E]), ALU.mult).then_inc(g["shifts_ready"], 1)
            dve.wait_ge(g["shifts_ready"], 1)
            nc.vector.tensor_reduce(shift[:], shift_all[:], AX_X, ALU.add).then_inc(g["shift_found"], 1)
            dve.wait_ge(g["shift_found"], 1)
            nc.vector.tensor_tensor(z.place[:, 0:z.TILES], z.place[:, 0:z.TILES], shift[:], ALU.subtract).then_inc(g["shift_found"], 1)
            dve.wait_ge(g["shift_found"], 2)
            four_pairs(0, first=True)
            four_pairs(QUAD, second=True)
            with dve.Fori(2, ROUNDS - 1) as r:
                four_pairs(r * QUAD)
            four_pairs(PAIRS - QUAD, last=True)


def second_layer(nc, z):
    B, KD, D = z.B, z.KD, z.D
    SCALE = float(D) ** -0.5
    assert D == 4 ** (D.bit_length() // 2)
    UT = 2
    UNITS = z.TILES // UT
    SLOTS = 4
    assert UNITS % SLOTS == 0 and UT * D <= 512
    with ExitStack() as ctx:
        sb, ps, sems = scope(nc, ctx)
        turned = sb("turned", [P, 4, KD, D])
        wqk = sb("wqk", [P, KD, D])
        wvo = sb("wvo", [P, KD, D])
        lng_half = sb("lng_half", [P, D])
        lnb_half = sb("lnb_half", [P, D])
        xin = sb("xin", [P, SLOTS, UT, D])
        moe = sb("moe", [P, SLOTS, UT, D])
        gather_u = sb("gather_u", [P, SLOTS, UT], U32)
        stats = sb("stats2", [P, SLOTS, UT, 6])
        pair = sb("pair2", [P, SLOTS, UT, 2])
        diff = sb("diff2", [P, SLOTS, UT])
        diff_sq = sb("diff_sq2", [P, SLOTS, UT])
        neg_mean = sb("neg_mean", [P, SLOTS, UT])
        var = sb("var2", [P, SLOTS, UT])
        var_eps = sb("var_eps2", [P, SLOTS, 2, UT])
        inv_var = sb("inv_var", [P, SLOTS, UT])
        var_n = sb("var_n", [P, SLOTS, UT])
        rstd = sb("rstd2", [P, SLOTS, 2, UT])
        shift = sb("shift2", [P, SLOTS, UT])
        xn = sb("xn2nd", [P, SLOTS, UT, D])
        xt = sb("xt", [P, 2, KD, UT * P])
        qt = sb("qt", [P, 2, KD, UT * P])
        vo = sb("vo", [P, 2, UT, D])
        ntop = sb("ntop", [P, SLOTS, UT])
        pr = sb("pr", [P, 2, UT, P])
        total = sb("total", [P, SLOTS, UT])
        total_eps = sb("total_eps", [P, SLOTS, UT])
        inv = sb("inv", [P, SLOTS, UT])
        prt = sb("prt", [P, 2, UT, P])
        zg = sb("zg", [P, SLOTS, UT, D])
        th = sb("th2", [P, SLOTS, UT, D])
        att = sb("att", [P, SLOTS, UT, D])
        t_ps = ps("t2_ps", [P, KD, UT * P])
        q_ps = ps("q_ps", [P, KD, UT * P])
        v_ps = ps("v_ps", [P, UT, D])
        s_ps = ps("s_ps", [P, 4, P])
        pt_ps = ps("pt_ps", [P, 4, P])
        a_ps = ps("a_ps", [P, UT, D])
        g = sems("index_ready moe_scaled x1_ready stats_done halves_met diff_squared var_found eps_added inv_var_ready "
                 "var_scaled var_ready mean_ready rstd_ready shift_ready xn_ready t_ready t_copied q_ready q_copied "
                 "v_ready v_copied s_ready top_ready p_ready pt_ready pt_copied att_ready z_scaled z_ready "
                 "z_tanh gate_ready total_based inv_ready att_scaled gated out_ready "
                 "halved turned_ready turned_copied folded_ready folded_copied")
        per_slot = lambda name: [ctx.enter_context(nc.semaphore(f"{name}{i}")) for i in range(SLOTS)]
        x_loaded, moe_loaded, out_stored = per_slot("x_loaded"), per_slot("moe_loaded"), per_slot("out_stored")
        block = ctx.enter_context(nc.Block())
        x_units = z.x.rearrange("b (n u p) d -> (b n) p u d", u=UT, p=P)
        out_units = z.out.rearrange("b (n u p) d -> (b n) p u d", u=UT, p=P)
        tiles = lambda n: z.res[:, bass.ds(UT * n, UT), :]

        def there(n, least=0):
            return not isinstance(n, int) or least <= n < UNITS

        run = lambda eng, first, step, last: pipeline(eng, first, step, last, UNITS, SLOTS)
        at = lambda i, ahead: (i + ahead) % SLOTS
        turns = lambda n, i, k: (n - i) * (k // SLOTS)

        @block.sync
        def _(sp):
            def load(n, i):
                if there(n):
                    if there(n, SLOTS):
                        sp.wait_ge(g["x1_ready"], n - SLOTS + 1)
                    sp.dma_start(xin[:, i], x_units[n]).then_inc(x_loaded[i], 16)

            def store(n, i):
                if there(n):
                    sp.wait_ge(g["out_ready"], n + 1)
                    sp.dma_start(out_units[n], att[:, i]).then_inc(out_stored[i], 16)

            def step(n, i, _):
                load(n + 4, i)
                store(n - 2, at(i, -2))

            run(sp, -4, step, UNITS + 1)
            for i in range(SLOTS):
                sp.wait_ge(out_stored[i], 16 * UNITS // SLOTS)

        @block.tensor
        def _(pe):
            def q(n, i):
                if there(n):
                    pe.wait_ge(g["t_copied"], n + 1)
                    if there(n, 1):
                        pe.wait_ge(g["q_copied"], n)
                    for j in range(KD):
                        for k in range(KD):
                            m = nc.tensor.matmul(q_ps[:, j, :], wqk[:, k, j * P:(j + 1) * P], xt[:, i % 2, k, :],
                                                 start=(j == 0 and k == 0), stop=(k == KD - 1), skip_group_check=True)
                    m.then_inc(g["q_ready"], 1)

            def turn(n, i):
                if there(n):
                    pe.wait_ge(g["xn_ready"], n + 1)
                    if there(n, 1):
                        pe.wait_ge(g["t_copied"], n)
                    for k in range(KD):
                        for t in range(UT):
                            m = nc.tensor.transpose(t_ps[:, k, t * P:(t + 1) * P], xn[:, i, t, k * P:(k + 1) * P], z.ident[:])
                    m.then_inc(g["t_ready"], 1)

            def v(n, i):
                if there(n):
                    if there(n, 1):
                        pe.wait_ge(g["v_copied"], n)
                    for t in range(UT):
                        for k in range(KD):
                            m = nc.tensor.matmul(v_ps[:, t, :], xt[:, i % 2, k, t * P:(t + 1) * P], wvo[:, k, :],
                                                 start=(t == 0 and k == 0), stop=(k == KD - 1), skip_group_check=True)
                    m.then_inc(g["v_ready"], 1)

            def turn_probs(n, i):
                if there(n):
                    pe.wait_ge(g["p_ready"], UT * n + UT)
                    if there(n, 1):
                        pe.wait_ge(g["pt_copied"], n)
                    for t in range(UT):
                        m = nc.tensor.transpose(pt_ps[:, t, :], pr[:, i % 2, t, :], z.ident[:])
                    m.then_inc(g["pt_ready"], 1)

            def scores(n, i):
                if there(n):
                    pe.wait_ge(g["q_copied"], n + 1)
                    for t in range(UT):
                        for j in range(KD):
                            nc.tensor.matmul(s_ps[:, t, :], qt[:, i % 2, j, t * P:(t + 1) * P], xt[:, i % 2, j, t * P:(t + 1) * P],
                                             start=(t == 0 and j == 0), stop=False, skip_group_check=True)
                        m = nc.tensor.matmul(s_ps[:, t, :], z.ident_b[:], z.causal[:], start=False, stop=True, skip_group_check=True)
                    m.then_inc(g["s_ready"], 1)

            def attend(n, i):
                if there(n):
                    pe.wait_ge(g["pt_copied"], n + 1)
                    pe.wait_ge(g["v_copied"], n + 1)
                    if there(n, 1):
                        pe.wait_ge(g["att_scaled"], UT * n)
                    for t in range(UT):
                        m = nc.tensor.matmul(a_ps[:, t, :], prt[:, i % 2, t, :], vo[:, i % 2, t, :], start=(t == 0), stop=True,
                                             skip_group_check=True)
                    m.then_inc(g["att_ready"], 1)

            def step(n, i, _):
                q(n, i)
                turn(n + 1, at(i, 1))
                v(n, i)
                turn_probs(n - 1, at(i, -1))
                scores(n, i)
                attend(n - 1, at(i, -1))

            for o, src in ((t_ps, z.w2[:, :, 0:D]), (q_ps, z.w2[:, :, D:2 * D]), (v_ps, z.w2[:, :, 2 * D:3 * D]), (a_ps, z.wo[:, :, :])):
                for k in range(KD):
                    for j in range(KD):
                        m = nc.tensor.transpose(o[:, k, j * P:(j + 1) * P], src[:, j, k * P:(k + 1) * P], z.ident[:])
                m.then_inc(g["turned_ready"], 1)
            for f, o in enumerate((t_ps, v_ps)):
                pe.wait_ge(g["turned_copied"], 2 * f + 2)
                for j in range(KD):
                    for k in range(KD):
                        m = nc.tensor.matmul(o[:, j, :], turned[:, 2 * f, k, j * P:(j + 1) * P], turned[:, 2 * f + 1, k, :],
                                             start=(j == 0 and k == 0), stop=(k == KD - 1), skip_group_check=True)
                m.then_inc(g["folded_ready"], 1)
            pe.wait_ge(g["folded_copied"], 2)
            run(pe, -1, step, UNITS)

        @block.scalar
        def _(act):
            def copy_q(n, i):
                if there(n):
                    act.wait_ge(g["q_ready"], n + 1)
                    nc.scalar.activation(qt[:, i % 2], q_ps[:], ACT.Copy).then_inc(g["q_copied"], 1)

            def copy_turned(n, i):
                if there(n):
                    act.wait_ge(g["t_ready"], n + 1)
                    if there(n, 2):
                        act.wait_ge(g["s_ready"], n - 1)
                    nc.scalar.activation(xt[:, i % 2], t_ps[:], ACT.Copy).then_inc(g["t_copied"], 1)

            def copy_probs(n, i):
                if there(n):
                    act.wait_ge(g["pt_ready"], n + 1)
                    if there(n, 2):
                        act.wait_ge(g["att_ready"], n - 1)
                    nc.scalar.activation(prt[:, i % 2], pt_ps[:, 0:UT], ACT.Copy).then_inc(g["pt_copied"], 1)

            def copy_v(n, i):
                if there(n):
                    act.wait_ge(g["v_ready"], n + 1)
                    if there(n, 2):
                        act.wait_ge(g["att_ready"], n - 1)
                    nc.scalar.activation(vo[:, i % 2], v_ps[:], ACT.Copy).then_inc(g["v_copied"], 1)

            def norm_apply(n, i):
                if there(n):
                    act.wait_ge(g["shift_ready"], n + 1)
                    if there(n, SLOTS):
                        act.wait_ge(g["z_scaled"], n - SLOTS + 1)
                    for t in range(UT):
                        m = nc.scalar.activation(xn[:, i, t, :].unsqueeze(1), z.res[:, bass.ds(UT * n + t, 1), :], ACT.Identity,
                                                 bias=shift[:, i, t:t + 1], scale=rstd[:, i, 0, t:t + 1])
                    m.then_inc(g["xn_ready"], 1)

            def tanh(n, i):
                if there(n):
                    act.wait_ge(g["z_ready"], n + 1)
                    nc.scalar.activation(th[:, i], zg[:, i], ACT.Tanh).then_inc(g["z_tanh"], 1)

            def exp(n, i):
                if there(n):
                    act.wait_ge(g["top_ready"], n + 1)
                    for t in range(UT):
                        nc.scalar.activation(pr[:, i % 2, t, :], s_ps[:, t, :], ACT.Exp, bias=ntop[:, i, t:t + 1], scale=-1.0,
                                             accum_out=total[:, i, t:t + 1]).then_inc(g["p_ready"], 1)

            def step(n, i, _):
                copy_q(n, i)
                exp(n - 1, at(i, -1))
                copy_turned(n + 1, at(i, 1))
                copy_probs(n - 1, at(i, -1))
                copy_v(n, i)
                norm_apply(n + 2, at(i, 2))
                tanh(n, i)

            for f, o in enumerate((t_ps, q_ps, v_ps, a_ps)):
                act.wait_ge(g["turned_ready"], f + 1)
                nc.scalar.activation(turned[:, f], o[:], ACT.Copy).then_inc(g["turned_copied"], 1)
            for f, (dst, o) in enumerate(((wqk, t_ps), (wvo, v_ps))):
                act.wait_ge(g["folded_ready"], f + 1)
                nc.scalar.activation(dst[:], o[:], ACT.Copy, scale=-SCALE if dst is wqk else 1.0).then_inc(g["folded_copied"], 1)
            run(act, -2, step, UNITS)

        @block.vector
        def _(dve):
            def index(n, i):
                nc.vector.tensor_copy(gather_u[:, i], z.place[:, bass.ds(UT * n, UT)]).then_inc(g["index_ready"], 1)

            def gate(n, i):
                if there(n):
                    dve.wait_ge(g["z_tanh"], n + 1)
                    nc.vector.scalar_tensor_tensor(zg[:, i], th[:, i], 1.0, zg[:, i], ALU.add, ALU.mult).then_inc(g["gate_ready"], 1)

            def scale_rows(n, i):
                if there(n):
                    dve.wait_ge(moe_loaded[i], turns(n, i, 16 * UT) + 16 * UT)
                    nc.vector.tensor_tensor(moe[:, i], moe[:, i], tiles(n), ALU.mult).then_inc(g["moe_scaled"], 1)

            def add_rows(n, i):
                if there(n):
                    dve.wait_ge(x_loaded[i], turns(n, i, 16) + 16)
                    dve.wait_ge(g["moe_scaled"], n + 1)
                    nc.vector.tensor_tensor(tiles(n), moe[:, i], xin[:, i], ALU.add).then_inc(g["x1_ready"], 1)

            def norm_stats(n, i):
                if there(n):
                    dve.wait_ge(g["x1_ready"], n + 1)
                    if there(n + 2, SLOTS):
                        index(n + 2, at(i, 2))
                    for t in range(UT):
                        nc.vector.bn_stats(stats[:, i, t], z.res[:, bass.ds(UT * n + t, 1), :]).then_inc(g["stats_done"], 1)

            def meet_halves(n, i):
                if there(n):
                    dve.wait_ge(g["stats_done"], UT * n + UT)
                    nc.vector.tensor_tensor(pair[:, i], stats[:, i, :, 1:3], stats[:, i, :, 4:6], ALU.add).then_inc(g["halves_met"], 1)
                    nc.vector.tensor_tensor(diff[:, i], stats[:, i, :, 1], stats[:, i, :, 4], ALU.subtract).then_inc(g["halves_met"], 1)

            def square_difference(n, i):
                if there(n):
                    dve.wait_ge(g["halves_met"], 2 * n + 2)
                    nc.vector.scalar_tensor_tensor(diff_sq[:, i], diff[:, i], 0.25, diff[:, i], ALU.mult, ALU.mult).then_inc(g["diff_squared"], 1)

            def variance(n, i):
                if there(n):
                    dve.wait_ge(g["diff_squared"], n + 1)
                    nc.vector.scalar_tensor_tensor(var[:, i], pair[:, i, :, 1], 1.0 / D, diff_sq[:, i], ALU.mult, ALU.add).then_inc(g["var_found"], 1)

            def variance_eps(n, i):
                if there(n):
                    dve.wait_ge(g["var_found"], n + 1)
                    nc.vector.tensor_scalar(var_eps[:, i, 0], var[:, i], LN_EPS, None, ALU.add).then_inc(g["eps_added"], 1)

            def inverse_variance(n, i):
                if there(n):
                    dve.wait_ge(g["eps_added"], n + 1)
                    nc.vector.reciprocal(inv_var[:, i], var_eps[:, i, 0]).then_inc(g["inv_var_ready"], 1)

            def normal_variance(n, i):
                if there(n):
                    dve.wait_ge(g["inv_var_ready"], n + 1)
                    nc.vector.tensor_tensor(var_n[:, i], var[:, i], inv_var[:, i], ALU.mult).then_inc(g["var_scaled"], 1)

            def normal_variance_eps(n, i):
                if there(n):
                    dve.wait_ge(g["var_scaled"], n + 1)
                    nc.vector.tensor_scalar(var_eps[:, i, 1], var_n[:, i], LN_EPS, None, ALU.add).then_inc(g["var_ready"], 1)

            def scale_gate(n, i):
                if there(n):
                    dve.wait_ge(g["xn_ready"], n + 1)
                    if there(n, SLOTS):
                        dve.wait_ge(g["gated"], n - SLOTS + 1)
                    for t in range(UT):
                        m = nc.vector.scalar_tensor_tensor(zg[:, i, t, :], xn[:, i, t, :], rstd[:, i, 1, t:t + 1], lng_half[:], ALU.mult, ALU.mult)
                    m.then_inc(g["z_scaled"], 1)

            def maximum(n, i):
                if there(n):
                    dve.wait_ge(g["s_ready"], n + 1)
                    nc.vector.tensor_reduce(ntop[:, i], s_ps[:, 0:UT], AX_X, ALU.min).then_inc(g["top_ready"], 1)

            def base_divisor(n, i):
                if there(n):
                    dve.wait_ge(g["p_ready"], UT * n + UT)
                    nc.vector.tensor_scalar(total_eps[:, i], total[:, i], Z_EPS, None, ALU.add).then_inc(g["total_based"], 1)

            def invert_divisor(n, i):
                if there(n):
                    dve.wait_ge(g["total_based"], n + 1)
                    nc.vector.reciprocal(inv[:, i], total_eps[:, i]).then_inc(g["inv_ready"], 1)

            def attend(n, i, t):
                if there(n):
                    if t == 0:
                        dve.wait_ge(g["inv_ready"], n + 1)
                        dve.wait_ge(g["att_ready"], n + 1)
                        if there(n, SLOTS):
                            dve.wait_ge(out_stored[i], turns(n, i, 16))
                    nc.vector.scalar_tensor_tensor(att[:, i, t, :], a_ps[:, t, :], inv[:, i, t:t + 1], z.bout[:], ALU.mult, ALU.add).then_inc(g["att_scaled"], 1)

            def gate_rows(n, i):
                if there(n):
                    dve.wait_ge(g["att_scaled"], UT * n + UT)
                    dve.wait_ge(g["gate_ready"], n + 1)
                    nc.vector.tensor_tensor(att[:, i], att[:, i], zg[:, i], ALU.mult).then_inc(g["gated"], 1)

            def step(n, i, _):
                back, next_one, ahead = (n - 1, at(i, -1)), (n + 2, at(i, 2)), (n + 3, at(i, 3))
                begin = isinstance(n, int) and n == -2
                if not begin:
                    scale_rows(*ahead)
                inverse_variance(*next_one)
                base_divisor(*back)
                normal_variance(*next_one)
                gate(*back)
                normal_variance_eps(*next_one)
                if begin:
                    scale_rows(*ahead)
                add_rows(*ahead)
                invert_divisor(*back)
                scale_gate(n + 1, at(i, 1))
                norm_stats(*ahead)
                maximum(n, i)
                meet_halves(*ahead)
                attend(*back, 0)
                square_difference(*ahead)
                attend(*back, 1)
                variance(*ahead)
                gate_rows(*back)
                variance_eps(*ahead)

            for n in range(SLOTS):
                index(n, n)
            nc.vector.tensor_scalar(lng_half[:], z.lng[:], 0.5, None, ALU.mult).then_inc(g["halved"], 1)
            nc.vector.tensor_scalar(lnb_half[:], z.lnb[:], 0.5, None, ALU.mult).then_inc(g["halved"], 1)
            dve.wait_ge(g["halved"], 2)
            run(dve, -3, step, UNITS)

        @block.gpsimd
        def _(pool):
            def indexed(n, i):
                if there(n):
                    pool.wait_ge(g["index_ready"], n + 1)

            def gather(n, i):
                if there(n):
                    for t in range(UT):
                        nc.gpsimd.indirect_dma_start(
                            out=moe[:, i, t, :], out_offset=None, in_=z.expert_dram.ap(),
                            in_offset=bass.IndirectOffsetOnAxis(ap=gather_u[:, i, t:t + 1], axis=0)).then_inc(moe_loaded[i], 16)

            def norm_scale(n, i):
                if there(n):
                    pool.wait_ge(g["var_ready"], n + 1)
                    nc.gpsimd.tensor_tensor(neg_mean[:, i], pair[:, i, :, 0], z.neg_half[:, 0:UT], ALU.mult).then_inc(g["mean_ready"], 1)
                    nc.gpsimd.tensor_tensor(rstd[:, i], var_eps[:, i], z.neg_half[:, 0:2 * UT].rearrange("p (a t) -> p a t", a=2), ALU.pow).then_inc(g["rstd_ready"], 1)
                    pool.wait_ge(g["mean_ready"], n + 1)
                    pool.wait_ge(g["rstd_ready"], n + 1)
                    nc.gpsimd.tensor_tensor(shift[:, i], neg_mean[:, i], rstd[:, i, 0], ALU.mult).then_inc(g["shift_ready"], 1)

            def shift_gate(n, i):
                if there(n):
                    pool.wait_ge(g["z_scaled"], n + 1)
                    nc.gpsimd.tensor_tensor(zg[:, i], zg[:, i], lnb_half[:].unsqueeze(1).to_broadcast([P, UT, D]), ALU.add).then_inc(g["z_ready"], 1)

            def result(n, i):
                if there(n):
                    pool.wait_ge(g["gated"], n + 1)
                    nc.gpsimd.tensor_tensor(att[:, i], att[:, i], tiles(n), ALU.add).then_inc(g["out_ready"], 1)

            def step(n, i, _):
                gather(n + 4, i)
                norm_scale(n + 2, at(i, 2))
                shift_gate(n, i)
                indexed(n + 5, at(i, 5))
                result(n - 2, at(i, -2))

            indexed(0, 0)
            run(pool, -4, step, UNITS + 1)


_INS = ["L0_attn_x", "L0_attn_W", "L0_ffn_gate_w", "L0_ffn_wg", "L0_ffn_wu", "L0_ffn_wd", "L1_attn_W_qkv", "L1_attn_W_out",
        "L1_attn_b_out", "L1_ffn_ln_g", "L1_ffn_ln_b"]


def kernel(**inputs):
    import numpy as np
    import concourse.bacc as bacc
    from concourse.bass_utils import run_bass_kernel_spmd

    nc = bacc.Bacc("TRN2", target_bir_lowering=False, num_devices=1)
    arrays, args = {}, []
    for name in _INS:
        a = np.ascontiguousarray(inputs[name])
        arrays[f"in_{name}"] = a
        args.append(nc.dram_tensor(f"in_{name}", a.shape, mybir.dt.from_np(a.dtype), kind="ExternalInput").ap())
    x = arrays["in_L0_attn_x"]
    out = nc.dram_tensor("out_rows", x.shape, mybir.dt.from_np(x.dtype), kind="ExternalOutput").ap()
    program(nc, *args, out)
    result = run_bass_kernel_spmd(nc, [arrays], core_ids=[0])
    return result.results[0]["out_rows"]
```
